# Optimizing a Trainium2 kernel written in Bass

```python
import numpy as np
import jax
import jax.numpy as jnp

def _softmax(x, axis=-1):
    return jax.nn.softmax(x, axis=axis)

def _gelu(x):
    return jax.nn.gelu(x, approximate=True)

def _silu(x):
    return jax.nn.silu(x)

def _sigmoid(x):
    return jax.nn.sigmoid(x)

def _layernorm(x, axis=-1, eps=1e-05):
    m = jnp.mean(x, axis=axis, keepdims=True)
    v = jnp.var(x, axis=axis, keepdims=True)
    return (x - m) / jnp.sqrt(v + eps)

def _scatter_add(tgt, idx, src, axis=0):
    return tgt.at[idx].add(src)

def _segment_sum(src, seg, n):
    return jax.ops.segment_sum(src, seg, n)
kernel_name = 'mk_sandwich_d1_jaxref_r8_e9c993'

def setup_inputs(seed: int=0):
    np.random.seed(seed)
    _w = jnp.asarray

    def _L0_attn_setup():
        import jax, jax.numpy as jnp
        import numpy as np
        B, T, C = (2, 256, 128)
        LAT = 32
        N_HEAD = 16
        HEAD_DIM = C // N_HEAD
        SCALE = 1.0 / np.sqrt(HEAD_DIM).astype(np.float32)
        key = jax.random.key(seed)
        ks = jax.random.split(key, 9)
        s_in = 0.02
        return {'x': jax.random.normal(ks[0], (B, T, C), dtype=jnp.float32), 'wq_lat': jax.random.normal(ks[1], (C, LAT), dtype=jnp.float32) * s_in, 'wk_lat': jax.random.normal(ks[2], (C, LAT), dtype=jnp.float32) * s_in, 'wv_lat': jax.random.normal(ks[3], (C, LAT), dtype=jnp.float32) * s_in, 'wq_heads': jax.random.normal(ks[4], (LAT, C), dtype=jnp.float32) * s_in, 'wk_heads': jax.random.normal(ks[5], (LAT, C), dtype=jnp.float32) * s_in, 'wv_heads': jax.random.normal(ks[6], (LAT, C), dtype=jnp.float32) * s_in, 'w_proj': jax.random.normal(ks[7], (C, C), dtype=jnp.float32) * s_in, 'b_proj': jnp.zeros((C,), dtype=jnp.float32)}
    _L0_attn_in = _L0_attn_setup()

    def _L0_ffn_setup():
        import jax, jax.numpy as jnp
        import numpy as np
        D = 128
        E = 12
        HS = 2 * D
        HR = 3 * D
        TAU = 1.5

        def _geglu(h):
            a, g = jnp.split(h, 2, axis=-1)
            return a * jax.nn.gelu(g, approximate=False)
        key = jax.random.key(seed)
        ks = jax.random.split(key, 12)

        def xavier(k, shape):
            fan_in, fan_out = (shape[-2], shape[-1])
            lim = jnp.sqrt(6.0 / (fan_in + fan_out))
            return jax.random.uniform(k, shape, jnp.float32, -lim, lim)
        x = jax.random.normal(ks[0], (2, 128, D), jnp.float32)
        Ws1 = xavier(ks[1], (D, 2 * HS))
        bs1 = jnp.zeros((2 * HS,), jnp.float32)
        Ws2 = xavier(ks[2], (HS, D))
        bs2 = jnp.zeros((D,), jnp.float32)
        We1 = xavier(ks[3], (E, D, 2 * HR))
        be1 = jnp.zeros((E, 2 * HR), jnp.float32)
        We2 = xavier(ks[4], (E, HR, D))
        be2 = jnp.zeros((E, D), jnp.float32)
        Wr = xavier(ks[5], (D, E))
        br = jnp.zeros((E,), jnp.float32)
        return {'x': x, 'Ws1': Ws1, 'bs1': bs1, 'Ws2': Ws2, 'bs2': bs2, 'We1': We1, 'be1': be1, 'We2': We2, 'be2': be2, 'Wr': Wr, 'br': br}
    _L0_ffn_in = _L0_ffn_setup()
    _d = {'L0_attn_x': _L0_attn_in['x'], 'L0_attn_wq_lat': _L0_attn_in['wq_lat'], 'L0_attn_wk_lat': _L0_attn_in['wk_lat'], 'L0_attn_wv_lat': _L0_attn_in['wv_lat'], 'L0_attn_wq_heads': _L0_attn_in['wq_heads'], 'L0_attn_wk_heads': _L0_attn_in['wk_heads'], 'L0_attn_wv_heads': _L0_attn_in['wv_heads'], 'L0_attn_w_proj': _L0_attn_in['w_proj'], 'L0_attn_b_proj': _L0_attn_in['b_proj'], 'L0_ffn_Ws1': _L0_ffn_in['Ws1'], 'L0_ffn_bs1': _L0_ffn_in['bs1'], 'L0_ffn_Ws2': _L0_ffn_in['Ws2'], 'L0_ffn_bs2': _L0_ffn_in['bs2'], 'L0_ffn_We1': _L0_ffn_in['We1'], 'L0_ffn_be1': _L0_ffn_in['be1'], 'L0_ffn_We2': _L0_ffn_in['We2'], 'L0_ffn_be2': _L0_ffn_in['be2'], 'L0_ffn_Wr': _L0_ffn_in['Wr'], 'L0_ffn_br': _L0_ffn_in['br']}
    _x0 = _d['L0_attn_x']
    _d['L0_attn_x'] = jax.random.normal(jax.random.fold_in(jax.random.key(seed), 1), (16, 512, 128), dtype=_x0.dtype)
    del _x0
    return _d

def reference(L0_attn_x, L0_attn_wq_lat, L0_attn_wk_lat, L0_attn_wv_lat, L0_attn_wq_heads, L0_attn_wk_heads, L0_attn_wv_heads, L0_attn_w_proj, L0_attn_b_proj, L0_ffn_Ws1, L0_ffn_bs1, L0_ffn_Ws2, L0_ffn_bs2, L0_ffn_We1, L0_ffn_be1, L0_ffn_We2, L0_ffn_be2, L0_ffn_Wr, L0_ffn_br):

    def _L0_attn_ref(x, wq_lat, wk_lat, wv_lat, wq_heads, wk_heads, wv_heads, w_proj, b_proj):
        import jax, jax.numpy as jnp
        import numpy as np
        B, T, C = (2, 256, 128)
        LAT = 32
        N_HEAD = 16
        HEAD_DIM = C // N_HEAD
        SCALE = 1.0 / np.sqrt(HEAD_DIM).astype(np.float32)
        Bx, Tx, Cx = x.shape
        q = x @ wq_lat @ wq_heads
        k = x @ wk_lat @ wk_heads
        v = x @ wv_lat @ wv_heads
        q = q.reshape(Bx, Tx, N_HEAD, HEAD_DIM).transpose(0, 2, 1, 3)
        k = k.reshape(Bx, Tx, N_HEAD, HEAD_DIM).transpose(0, 2, 1, 3)
        v = v.reshape(Bx, Tx, N_HEAD, HEAD_DIM).transpose(0, 2, 1, 3)
        att = jnp.einsum('bhqd,bhkd->bhqk', q, k) * SCALE
        causal = jnp.tril(jnp.ones((Tx, Tx), dtype=bool))
        att = jnp.where(causal[None, None], att, -jnp.inf)
        att = jax.nn.softmax(att, axis=-1)
        y = jnp.einsum('bhqk,bhkd->bhqd', att, v)
        y = y.transpose(0, 2, 1, 3).reshape(Bx, Tx, Cx)
        return y @ w_proj + b_proj

    def _L0_ffn_ref(x, Ws1, bs1, Ws2, bs2, We1, be1, We2, be2, Wr, br):
        import jax, jax.numpy as jnp
        import numpy as np
        D = 128
        E = 12
        HS = 2 * D
        HR = 3 * D
        TAU = 1.5

        def _geglu(h):
            a, g = jnp.split(h, 2, axis=-1)
            return a * jax.nn.gelu(g, approximate=False)
        B, T, Dm = x.shape
        xf = x.reshape(-1, Dm)
        ys = _geglu(xf @ Ws1 + bs1) @ Ws2 + bs2
        logits = (xf @ Wr + br) / TAU
        top_val, top_idx = jax.lax.top_k(logits, 2)
        top_w = jax.nn.softmax(top_val, axis=-1)
        onehot = jax.nn.one_hot(top_idx, E, dtype=x.dtype)
        w = jnp.einsum('nke,nk->ne', onehot, top_w)
        h = jnp.einsum('nd,edh->enh', xf, We1) + be1[:, None, :]
        act = _geglu(h)
        yE = jnp.einsum('enh,ehd->end', act, We2) + be2[:, None, :]
        yr = jnp.einsum('end,ne->nd', yE, w)
        return (ys + yr).reshape(B, T, Dm)
    x = L0_attn_x
    x = x + _layernorm(_L0_attn_ref(_layernorm(x, axis=-1), L0_attn_wq_lat, L0_attn_wk_lat, L0_attn_wv_lat, L0_attn_wq_heads, L0_attn_wk_heads, L0_attn_wv_heads, L0_attn_w_proj, L0_attn_b_proj), axis=-1)
    x = x + _layernorm(_L0_ffn_ref(_layernorm(x, axis=-1), L0_ffn_Ws1, L0_ffn_bs1, L0_ffn_Ws2, L0_ffn_bs2, L0_ffn_We1, L0_ffn_be1, L0_ffn_We2, L0_ffn_be2, L0_ffn_Wr, L0_ffn_br), axis=-1)
    return x

_drawn_inputs = setup_inputs


def setup_inputs(seed=0):
    import zlib

    import numpy as np

    out = dict(_drawn_inputs(seed))
    spreads = {'L0_attn_b_proj': (0.0, 0.1),
     'L0_ffn_bs1': (0.0, 0.1),
     'L0_ffn_bs2': (0.0, 0.1),
     'L0_ffn_be1': (0.0, 0.1),
     'L0_ffn_be2': (0.0, 0.1),
     'L0_ffn_br': (0.0, 0.1)}
    factors = {'L0_attn_wq_lat': 8.0,
     'L0_attn_wk_lat': 8.0,
     'L0_attn_wv_lat': 4.041,
     'L0_attn_wq_heads': 8.0,
     'L0_attn_wk_heads': 8.0,
     'L0_attn_wv_heads': 3.88,
     'L0_attn_w_proj': 3.796}
    for name, (base, spread) in spreads.items():
        noise = np.random.default_rng([zlib.crc32(name.encode()), seed]).standard_normal(out[name].shape)
        drawn = base * np.exp(spread * noise) if base else spread * noise
        out[name] = jnp.asarray(drawn.astype(out[name].dtype))
    for name, factor in factors.items():
        out[name] = (out[name] * factor).astype(out[name].dtype)
    return out
```

```python
from contextlib import ExitStack

import concourse.bass as bass
from concourse import mybir

ALU = mybir.AluOpType
ACT = mybir.ActivationFunctionType
AX = mybir.AxisListType.X
F32 = mybir.dt.float32
BF16 = mybir.dt.bfloat16
I32 = mybir.dt.int32

P = 128
B, T, C = 16, 512, 128
NT = T // P
TILES = B * NT
LAT, HEADS, HD = 32, 16, 8
QUADS = B * HEADS // 4
E, HS, HR = 12, 256, 384
TAU = 1.5
EPS = 1e-5
MASKED = -1e30
ROUTED = -(-(2 * B * T // P + E - 1) // 4) * 4
FAR = 16.0
HUGE = 3e38
Q_SLOTS = (0, 0, 1, 1, 0, 2)
K_SLOTS = (0, 1, 0, 1, 2, 0)
QK_ROWS = HD * len(Q_SLOTS)
ROWS = QK_ROWS + 3


BOTH_STEP = 12
DIFFERENCE_STEP = 13
ROUTING_STEPS = 67


def wait_apart(engine, sem, value, passed):
    engine.wait_ge(sem, value)
    engine.sem_inc(passed, 1)


def ge(engine, sem, value):
    if not (isinstance(value, int) and value <= 0):
        engine.wait_ge(sem, value)


def rot_items(g):
    items = []
    for n in range(12):
        if n == 3:
            if 0 <= g + 1 < QUADS:
                items.append(("max_rows", 0))
        elif n == 7:
            if 0 <= g - 2 < QUADS:
                items.append(("turn_back", 0))
        elif g + 2 < QUADS:
            items.append(("scores", n - (n > 3) - (n > 7)))
    return items


FIRST, LAST = -2, QUADS + 1
ROT_BASE = {}
_n = 0
for _g in range(FIRST, LAST + 1):
    ROT_BASE[_g] = _n
    _n += len(rot_items(_g))
ROT_PER = 12


def rot_base(gs, g):
    if isinstance(g, int):
        return ROT_BASE[g]
    return ROT_PER * g + (ROT_BASE[gs] - ROT_PER * gs)


NEWTON = 3
NEWTON_OPS = 4 * NEWTON
SEED_OPS = 4


def seed(dve, sem, done, y, v, half, var):
    dve.wait_ge(sem, done)
    dve.tensor_scalar(v, var, EPS, None, ALU.add).then_inc(sem, 1)
    dve.wait_ge(sem, done + 1)
    dve.tensor_scalar(half.bitcast(I32), v.bitcast(I32), 1, None, ALU.arith_shift_right).then_inc(sem, 1)
    dve.wait_ge(sem, done + 2)
    dve.tensor_scalar(y.bitcast(I32), half.bitcast(I32), -1.0, float(0x5F3759DF), ALU.mult, ALU.add).then_inc(sem, 1)


def newton(pool, passed, sem, done, y, v, t):
    for _ in range(NEWTON):
        pool.tensor_tensor(t, y, y, ALU.mult).then_inc(sem, 1)
        pool.wait_ge(sem, done + 1)
        pool.tensor_tensor(t, t, v, ALU.mult).then_inc(sem, 1)
        wait_apart(pool, sem, done + 2, passed)
        pool.tensor_scalar(t, t, -0.5, 1.5, ALU.mult, ALU.add).then_inc(sem, 1)
        pool.wait_ge(sem, done + 3)
        pool.tensor_tensor(y, y, t, ALU.mult).then_inc(sem, 1)
        done = done + 4
        pool.wait_ge(sem, done)


def rows_of(vector, n):
    return vector.rearrange("(o n) -> o n", o=1).broadcast_to([P, n])


def build(nc, a, out):
    with ExitStack() as ctx:
        def sb(name, shape, dt=F32):
            return ctx.enter_context(nc.sbuf_tensor(name, shape, dt))

        def sem(name):
            return ctx.enter_context(nc.semaphore(name))

        x_sb = sb("x_sb", [P, TILES, C])
        v_all = sb("v_all", [P, TILES, C])
        y_sb = sb("y_sb", [P, TILES, C])
        ident = sb("ident", [P, P])
        ident_bf = sb("ident_bf", [P, P], BF16)
        mask_q = sb("mask_q", [P, P], BF16)
        mask_k = sb("mask_k", [P, P], BF16)
        ysum = y_sb
        late = v_all[:, TILES - 8:TILES, :].rearrange("p t c -> p (t c)")
        lat_in = late[:, 0:3 * LAT].rearrange("p (n c) -> p n c", n=3)
        heads_in = late[0:LAT, P:4 * P].rearrange("p (n c) -> p n c", n=3)
        latT = late[0:LAT, 4 * P:7 * P].rearrange("p (n c) -> p n c", n=3)
        iota_i = v_all[:, TILES - 10:TILES - 8, :].rearrange("p t c -> p (t c)")[:, 0:ROUTED + E].bitcast(I32)
        w_qkv = sb("w_qkv", [P, 3, C])
        st = sb("st", [P, 2, NT, 6])
        mv = sb("mv", [P, 2, NT, 2])
        rstd = sb("rstd", [P, 2, NT])
        root = sb("root", [P, 2, 3, NT])
        xn = sb("xn", [P, 2, NT, C])
        xnT = sb("xnT", [P, 2, T])
        split_area = sb("split_area", [P, 5 * 1024])
        part = split_area[:, 0:3 * 1024].bitcast(BF16).rearrange("p (a b c t) -> p a b c t", a=2, b=2, c=3)
        rest = split_area[:, 3 * 1024:5 * 1024].rearrange("p (a b t) -> p a b t", a=2, b=2)
        we2 = split_area[:, 0:E * HR]
        quad_area = sb("quad_area", [P, 6 * 1024])
        qk = quad_area[:, 0:4 * 1024].bitcast(BF16).rearrange("p (q s r t) -> p q s r t", q=4, s=2, r=2)
        v_cur = quad_area[:, 4 * 1024:6 * 1024].rearrange("p (q t h r) -> p q t h r", q=4, t=NT, h=4)
        be1r = quad_area[0:3, 0:E * HR].bitcast(BF16)
        be2r = quad_area[0:3, 5 * 1024:5 * 1024 + E * C // 2].bitcast(BF16)
        pT_area = sb("pT_area", [P, 10 * 1024])

        def area(n, count=1):
            return pT_area[:, 1024 * n:1024 * (n + count)]

        pT = pT_area[:, :].rearrange("p (a n t) -> p a n t", a=2, n=5)
        ycur = area(0).rearrange("p (a t c) -> p a t c", a=2, c=C)
        yT = area(1).rearrange("p (a t) -> p a t", a=2)
        xn2 = area(2).rearrange("p (a t c) -> p a t c", a=2, c=C)
        gel = area(3).rearrange("p (a t) -> p a t", a=2)
        hid = area(4).rearrange("p (a t) -> p a t", a=2)
        lowest = area(5)[:, 0:TILES * E].rearrange("p (t e) -> p t e", e=E)
        onehot = [area(6 + k)[:, 0:TILES * E].rearrange("p (t e) -> p t e", e=E) for k in range(2)]
        both = area(8)[:, 0:TILES * E].rearrange("p (t e) -> p t e", e=E)
        counts = [area(9 * k)[:, 0:TILES * E].rearrange("p (t e) -> p t e", e=E) for k in range(2)]
        top = area(1)[:, 0:6 * TILES].rearrange("p (k t) -> p k t", k=6)
        small = area(1)[:, 6 * TILES:6 * TILES + 6 * E].rearrange("p (k e) -> p k e", e=E)
        small_i = area(1)[:, 512:512 + 2 * E].bitcast(I32).rearrange("p (k e) -> p k e", e=E)
        etile_f = area(1)[0:1, 640:640 + 2 * ROUTED].rearrange("p (k j) -> p k j", k=2)
        we1 = pT_area[:, 0:E * 2 * HR]
        picked = area(0, 2).rearrange("p (a t k c) -> p a t k c", a=2, t=NT, k=2)
        summed = area(2).rearrange("p (a t c) -> p a t c", a=2, t=NT)
        final = area(3).rearrange("p (a t c) -> p a t c", a=2, t=NT)
        m_q = sb("m_q", [P, 2, 16])
        m_rest = sb("m_rest", [P, 2, 16])
        m_part = sb("m_part", [P, 2, 3, 16], BF16)
        mT_sb = sb("mT_sb", [48, 2, P], BF16)
        outT = sb("outT", [P, 2, T])
        logits = sb("logits", [P, TILES, E])
        a_sb = xn
        xT2 = xnT
        flat_xn = xn[:].rearrange("p a t c -> p (a t c)")
        xs = flat_xn[:, 0:4 * C].rearrange("p (a c) -> p a c", a=4)
        xsT = flat_xn[:, 4 * C:6 * C].rearrange("p (a c) -> p a c", a=2)
        ys = flat_xn[:, 6 * C:8 * C].rearrange("p (a c) -> p a c", a=2)
        gelE = xnT[:].rearrange("p a t -> p (a t)")[:, 0:2 * HR].rearrange("p (a h) -> p a h", a=2)
        hidE = outT[:].rearrange("p a t -> p (a t)")[:, 0:2 * HR].rearrange("p (a h) -> p a h", a=2)
        hidT = logits[:].rearrange("p t e -> p (t e)").rearrange("p (a h) -> p a h", a=2)
        w_proj = sb("w_proj", [P, C])
        w_r = sb("w_r", [P, E])
        ws1 = sb("ws1", [P, 2 * HS])
        ws2 = sb("ws2", [P, 2, C])
        b_proj = sb("b_proj", [P, C])
        b_s1 = sb("b_s1", [P, 4])
        b_s2 = sb("b_s2", [P, C])
        b_r = sb("b_r", [P, E])
        be_in = sb("be_in", [P, 84])
        be_rest = sb("be_rest", [P, 84])
        be_part = sb("be_part", [P, 3, 84], BF16)
        ones_bf = sb("ones_bf", [3, P], BF16)
        before = sb("before", [P, P])
        ones = sb("ones", [P, P])
        st2 = sb("st2", [P, 2, NT, 6])
        mv2 = sb("mv2", [P, 2, NT, 2])
        rstd2 = sb("rstd2", [P, 2, NT])
        root2 = sb("root2", [P, 2, 3, NT])
        iota_f = sb("iota_f", [P, ROUTED + E])
        kept = split_area[:, E * HR:5 * 1024]
        weight = kept[:, 0:2 * TILES].rearrange("p (k t) -> p k t", k=2)
        slot_i = kept[:, 2 * TILES:4 * TILES].bitcast(I32).rearrange("p (t k) -> p t k", k=2)
        etile = kept[0:1, 4 * TILES:4 * TILES + ROUTED].bitcast(I32)
        idx_cur = sb("idx_cur", [P, 2, 2 * NT], I32)
        rden = sb("rden", [P, 2, NT, 4])
        ps = ctx.enter_context(nc.psum_tensor("ps", [P, 8, 512], F32))

        qk_dram = nc.dram_tensor("qk_dram", [2, B * HEADS, QK_ROWS, T], BF16).ap()
        be1_dram = nc.dram_tensor("be1_dram", [3, E * 2 * HR], BF16).ap()
        be2_dram = nc.dram_tensor("be2_dram", [3, E * C], BF16).ap()
        xs_dram = nc.dram_tensor("xs_dram", [ROUTED * P, C], F32).ap()
        ys_dram = nc.dram_tensor("ys_dram", [ROUTED * P, C], F32).ap()
        m_dram = nc.dram_tensor("m_dram", [4, 3, 2, 2 * T], BF16).ap()

        s_x = sem("x_loaded"); s_w = sem("w_loaded")
        s_const = sem("const_ready"); s_pstep = sem("pool_step")
        s_latT = sem("latT_done"); s_latT_sb = sem("latT_copied"); s_wmul = sem("w_multiplied"); s_wsb = sem("w_ready")
        s_stats = sem("ln_stats"); s_seed = sem("ln_seed"); s_newton = sem("ln_newton"); s_xn = sem("xn_ready")
        s_xT = sem("xT_done"); s_xT_sb = sem("xnT_ready")
        s_qkp = sem("qk_projected"); s_vp = sem("v_projected"); s_vsb = sem("v_ready")
        s_p1 = sem("part1_ready"); s_r = sem("rest_ready"); s_p2 = sem("part2_ready"); s_p3 = sem("part3_ready")
        s_parts = [sem("parts_stored0"), sem("parts_stored1")]
        s_qk = [sem(f"qk_loaded{n}") for n in range(4)]
        s_m = [sem(f"m_loaded{n}") for n in range(4)]
        s_mw = sem("m_stored")
        s_rot = sem("rot_filled"); s_rotf = sem("rot_freed")
        s_msplit = sem("m_split")
        s_st = sem("scoresT_filled"); s_exp = sem("exp_done"); s_pv = sem("pv_done"); s_outT = sem("outT_ready")
        s_rden = sem("rden_ready"); s_y = sem("y_ready"); s_vcur = sem("v_cur_ready")
        s_done = sem("out_stored")
        s_passed = sem("waits_passed")
        s_zset = sem("zeros_set"); s_zero = sem("rows_zeroed")
        s_w2 = sem("small_weights_loaded"); s_be = sem("be_split"); s_bew = sem("be_stored"); s_ber = sem("be_rows_loaded")
        s_we = sem("expert_weights_loaded")
        s_ycur = sem("ycur_ready"); s_yT = sem("yT_done"); s_yTsb = sem("yT_ready"); s_proj = sem("projected")
        s_a = sem("a_ready"); s_stA = sem("statsA"); s_seedA = sem("seedA"); s_newtA = sem("newtonA"); s_x1 = sem("x1_ready")
        s_res = sem("residual_steps"); s_st2 = sem("stats2")
        s_seedB = sem("seedB"); s_newtB = sem("newtonB"); s_xn2 = sem("xn2_ready")
        s_xT2 = sem("xT2_done"); s_xT2sb = sem("xT2_ready"); s_lg = sem("logits_done"); s_lgsb = sem("logits_ready")
        s_hg = sem("shared_g_done"); s_gel = sem("shared_gelu_ready"); s_ha = sem("shared_a_done"); s_hid = sem("shared_hidden_ready")
        s_y2 = sem("shared_y_done"); s_ysum = sem("shared_y_ready")
        s_rt = sem("routing_step"); s_pref = sem("prefixes_done"); s_exw = sem("exp_of_difference")
        s_rows = sem("rows_staged"); s_idx = sem("slots_staged"); s_scat = [sem(f"rows_scattered{n}") for n in range(2)]
        s_xs = [sem(f"xs_loaded{n}") for n in range(4)]
        s_xsT = sem("xsT_done"); s_xsTsb = sem("xsT_ready"); s_he = sem("expert_h_done"); s_ge = sem("expert_gelu_ready")
        s_hide = sem("expert_hidden_ready"); s_hT = sem("expert_hiddenT_done"); s_hTsb = sem("expert_hiddenT_ready")
        s_ye = sem("expert_y_done"); s_yesb = sem("expert_y_ready"); s_yst = [sem(f"ys_stored{n}") for n in range(2)]
        s_idx2 = sem("slots_staged_again"); s_pick = [sem(f"rows_picked{n}") for n in range(2)]
        s_comb = sem("combine_steps"); s_st3 = sem("stats3"); s_seedC = sem("seedC"); s_newtC = sem("newtonC"); s_fin = sem("final_steps")
        s_out = [sem(f"out_stored{n}") for n in range(2)]

        ROT_ALL = ROT_BASE[LAST] + len(rot_items(LAST))
        SKEW = 3

        def skewed(engine, step):
            for n in range(SKEW + 3):
                step(n, n)
            with engine.Fori(0, (B - SKEW - 3) // 2) as it:
                for k in range(2):
                    step(SKEW + 3 + k, 2 * it + (SKEW + 3 + k))
            for n in range(B, B + SKEW):
                step(n, n)

        def col(t, k, b):
            return t[:, k, b:b + 1] if isinstance(b, int) else t[:, k, bass.ds(b, 1)]

        def quad_steps(engine, step):
            for g in range(FIRST, 4):
                step(g, g)
            with engine.Fori(1, B - 1) as it:
                for q in range(4):
                    step(4 + q, 4 * it + q)
            for g in range(4 * (B - 1), LAST + 1):
                step(g, g)

        def batches(engine, first, step):
            first()
            with engine.Fori(0, B // 2 - 1) as it:
                for par in range(2):
                    step(par, 2 * it + par, True)
            for b in (B - 2, B - 1):
                step(b % 2, b, b + 1 < B)

        def tiles_by_four(engine, step):
            for j in range(4):
                step(j, j, True)
            with engine.Fori(1, ROUTED // 4 - 1) as it:
                for k in range(4):
                    step(k, 4 * it + k, True)
            for j in range(ROUTED - 4, ROUTED):
                step(j % 4, j, j + 3 < ROUTED)

        def combine_steps(engine, step):
            for n in range(4):
                step(n, n)
            with engine.Fori(0, B // 2 - 3) as it:
                for k in range(2):
                    step(4 + k, 2 * it + 4 + k)
            for n in range(B - 2, B + 1):
                step(n, n)

        def tiles4(t, b):
            return t[:, 4 * b:4 * b + 4, :] if isinstance(b, int) else t[:, bass.ds(4 * b, 4), :]

        block = ctx.enter_context(nc.Block())

        @block.sync
        def _(sp):
            for n, name in enumerate(("L0_attn_wq_lat", "L0_attn_wk_lat", "L0_attn_wv_lat")):
                sp.dma_start(lat_in[:, n, :], a[name]).then_inc(s_w, 16)
            for n, name in enumerate(("L0_attn_wq_heads", "L0_attn_wk_heads", "L0_attn_wv_heads")):
                sp.dma_start(heads_in[:, n, :], a[name]).then_inc(s_w, 16)
            small_loads = [
                (w_proj[:], a["L0_attn_w_proj"]), (w_r[:], a["L0_ffn_Wr"]), (ws1[:], a["L0_ffn_Ws1"]),
                (ws2[:], a["L0_ffn_Ws2"].rearrange("(k p) d -> p k d", p=P)),
                (b_proj[:], rows_of(a["L0_attn_b_proj"], C)), (b_s2[:], rows_of(a["L0_ffn_bs2"], C)),
                (b_r[:], rows_of(a["L0_ffn_br"], E)), (b_s1[:], a["L0_ffn_bs1"].rearrange("(k p) -> p k", p=P)),
                (be_in[:, 0:72], a["L0_ffn_be1"].rearrange("e h -> (e h)").rearrange("(p x) -> p x", p=P)),
                (be_in[:, 72:84], a["L0_ffn_be2"].rearrange("e h -> (e h)").rearrange("(p x) -> p x", p=P))]
            for n in range(4):
                sp.dma_start(x_sb[:, 16 * n:16 * n + 16, :],
                             a["L0_attn_x"][4 * n:4 * n + 4].rearrange("b (t p) c -> p (b t) c", p=P)).then_inc(s_x, 16)

            for to, what in small_loads:
                sp.dma_start(to, what, allow_slow_non_contiguous=True).then_inc(s_w2, 16)
            sp.wait_ge(s_zset, 1)
            zeros = y_sb[:].rearrange("p t c -> p (t c)")
            blank = xs_dram.rearrange("(p r) c -> p (r c)", p=P)
            for at in range(0, ROUTED * C, TILES * C):
                n = min(TILES * C, ROUTED * C - at)
                sp.dma_start(blank[:, at:at + n], zeros[:, 0:n]).then_inc(s_zero, 16)
            sp.wait_ge(s_be, 4)
            sp.dma_start(be1_dram.rearrange("n (p x) -> p n x", p=P), be_part[:, :, 0:72]).then_inc(s_bew, 16)
            sp.dma_start(be2_dram.rearrange("n (p x) -> p n x", p=P), be_part[:, :, 72:84]).then_inc(s_bew, 16)
            sp.wait_ge(s_bew, 32)

            def store_parts(par, b, more):
                rows = [qk_dram[s, bass.ds(HEADS * b, HEADS)].rearrange("h (j d) t -> j h d t", j=6) for s in range(2)]
                for part_n, sem_ready in ((0, s_p1), (1, s_p2), (2, s_p3)):
                    sp.wait_ge(sem_ready, 2 * b + 2)
                    for s, slots in ((0, Q_SLOTS), (1, K_SLOTS)):
                        for j in range(6):
                            if slots[j] == part_n:
                                sp.dma_start(rows[s][j], part[:, par, s, part_n, :]).then_inc(s_parts[par], 16)

            batches(sp, lambda: None, store_parts)
            for par in range(2):
                sp.wait_ge(s_parts[par], 12 * 16 * B // 2)

            def load_quad(slot, h):
                for s in range(2):
                    for hp in range(2):
                        sp.dma_start(qk[64 * hp:64 * hp + QK_ROWS, slot, s],
                                     qk_dram[s, bass.ds(4 * h + 2 * hp, 2)].rearrange("r p t -> p r t")
                                     ).then_inc(s_qk[slot], 16)

            def step(gs, g):
                if gs + 3 < QUADS:
                    ge(sp, s_st, 5 * g)
                    slot = (gs + 3) % 4
                    load_quad(slot, g + 3)
                if 0 <= gs + 1 < QUADS:
                    slot = (gs + 1) % 4
                    sp.wait_ge(s_rotf, rot_base(gs, g) + rot_items(gs).index(("max_rows", 0)) + 1)
                    sp.dma_start(m_dram[slot].rearrange("n h (x q) -> (n h x) q", q=P),
                                 mT_sb[:, (gs + 1) % 2, :]).then_inc(s_mw, 16)
                    sp.wait_ge(s_mw, 16 * (g + 2))
                    for hp in range(2):
                        sp.dma_start(qk[64 * hp + QK_ROWS:64 * hp + ROWS, slot, 0].rearrange("p r t -> p (r t)"),
                                     m_dram[slot, :, hp]).then_inc(s_m[slot], 16)

            sp.wait_ge(s_const, 1)
            load_quad(0, 0)
            quad_steps(sp, step)

            sp.wait_ge(s_st, 5 * QUADS)
            sp.wait_ge(s_pv, QUADS)
            sp.dma_start(be1r, be1_dram).then_inc(s_ber, 16)
            sp.dma_start(be2r, be2_dram).then_inc(s_ber, 16)
            for e in range(E):
                sp.dma_start(we2[:, e * HR:(e + 1) * HR].rearrange("p (k d) -> p k d", k=3),
                             a["L0_ffn_We2"][e].rearrange("(k p) d -> p k d", p=P)).then_inc(s_we, 16)
            sp.wait_ge(s_rt, ROUTING_STEPS)
            for e in range(E):
                sp.dma_start(we1[:, e * 2 * HR:(e + 1) * 2 * HR], a["L0_ffn_We1"][e]).then_inc(s_we, 16)
            for par in range(2):
                sp.wait_ge(s_scat[par], 16 * 2 * NT * B // 2)

            def load_rows(ring, j):
                sp.dma_start(xs[:, ring, :], xs_dram[bass.ds(j * P, P), :]).then_inc(s_xs[ring], 16)

            for j in range(3):
                load_rows(j, j)

            def expert_tile(js, j, more):
                if more:
                    ge(sp, s_xsT, j)
                    load_rows((js + 3) % 4, j + 3)
                sp.wait_ge(s_yesb, j + 1)
                sp.dma_start(ys_dram[bass.ds(j * P, P), :], ys[:, js % 2, :]).then_inc(s_yst[js % 2], 16)

            tiles_by_four(sp, expert_tile)

            def store(ns, n):
                if 0 <= ns - 1 < B:
                    par = (ns - 1) % 2
                    sp.wait_ge(s_fin, 2 * n)
                    sp.dma_start(out[bass.ds(n - 1, 1)].rearrange("b (t p) c -> p (b t) c", p=P), final[:, par]).then_inc(s_out[par], 16)

            combine_steps(sp, store)
            for par in range(2):
                sp.wait_ge(s_out[par], 16 * B // 2)

        @block.gpsimd
        def _(pool):
            n = 0

            def chain(ins):
                nonlocal n
                n += 1
                ins.then_inc(s_pstep, 1)
                pool.wait_ge(s_pstep, n)

            pool.memset(y_sb[:], 0.0).then_inc(s_zset, 1)
            pool.memset(ident[:], 0.0)
            pool.memset(before[:], 1.0)
            pool.memset(ones[:], 1.0)
            pool.memset(ones_bf[:], 1.0)
            pool.iota(iota_i[:, 0:ROUTED], pattern=[[1, ROUTED]], base=0, channel_multiplier=0)
            pool.iota(iota_i[:, ROUTED:], pattern=[[1, E]], base=-int(FAR), channel_multiplier=0)
            pool.memset(mask_q[:], 0.0)
            pool.memset(mask_k[:], 0.0)
            pool.memset(qk[:], 1.0)
            chain(pool.memset(v_cur[:], 0.0))
            pool.memset(v_cur[:, :, :, :, HD:HD + 1], 1.0)
            chain(pool.affine_select(out=ident[:], in_=ident[:], compare_op=ALU.not_equal, fill=1.0, base=0,
                                     pattern=[[-1, P]], channel_multiplier=1))
            pool.affine_select(out=before[:], in_=before[:], compare_op=ALU.is_gt, fill=0.0, base=0,
                               pattern=[[1, P]], channel_multiplier=-1)
            pool.tensor_copy(iota_f[:], iota_i[:])
            pool.affine_select(out=mask_q[:], in_=mask_q[:], compare_op=ALU.is_ge, fill=MASKED, base=0,
                               pattern=[[-1, P]], channel_multiplier=1)
            pool.affine_select(out=mask_k[:], in_=mask_k[:], compare_op=ALU.is_ge, fill=MASKED, base=0,
                               pattern=[[1, P]], channel_multiplier=-1)
            pool.tensor_copy(ident_bf[:], ident[:]).then_inc(s_const, 1)

            def ln_rstd(par, b):
                pool.wait_ge(s_seed, SEED_OPS * (b + 1))
                newton(pool, s_passed, s_newton, NEWTON_OPS * b, rstd[:, par, :], root[:, par, 0, :], root[:, par, 2, :])

            def third_parts(par, b, more):
                if more:
                    ln_rstd(1 - par, b + 1)
                for s in range(2):
                    pool.wait_ge(s_p2, 2 * b + s + 1)
                    pool.tensor_tensor(part[:, par, s, 2, :], rest[:, par, s, :], part[:, par, s, 1, :],
                                       ALU.subtract).then_inc(s_p3, 1)

            batches(pool, lambda: ln_rstd(0, 0), third_parts)

            def step(gs, g):
                if not 0 <= gs + 1 < QUADS:
                    return
                ge(pool, s_pv, g - 2)
                q = (gs + 1) % 4
                if isinstance(g, int):
                    first = 4 * ((g + 1) // 4)
                    src = v_all[:, first:first + 4, 32 * q:32 * q + 32]
                else:
                    src = v_all[:, bass.ds(g + 1 - q, 4), 32 * q:32 * q + 32]
                pool.tensor_copy(v_cur[:, q, :, :, 0:HD], src.rearrange("p t (h d) -> p t h d", d=HD)).then_inc(s_vcur, 1)

            pool.wait_ge(s_vsb, B)
            quad_steps(pool, step)

            def roots(ns, n):
                if 0 <= ns < B:
                    par = ns % 2
                    pool.wait_ge(s_seedA, SEED_OPS * (n + 1))
                    newton(pool, s_passed, s_newtA, NEWTON_OPS * n, rstd[:, par, :], root[:, par, 0, :], root[:, par, 2, :])
                if 0 <= ns - 1 < B:
                    par = (ns - 1) % 2
                    pool.wait_ge(s_seedB, SEED_OPS * n)
                    newton(pool, s_passed, s_newtB, NEWTON_OPS * (n - 1), rstd2[:, par, :], root2[:, par, 0, :], root2[:, par, 2, :])

            skewed(pool, roots)
            pool.wait_ge(s_zero, 48)

            def scatter(par, b):
                pool.wait_ge(s_rows, b + 1)
                wait_apart(pool, s_idx, b + 1, s_passed)
                for t in range(NT):
                    for k in range(2):
                        at = bass.IndirectOffsetOnAxis(ap=idx_cur[:, par, 2 * t + k:2 * t + k + 1], axis=0)
                        pool.indirect_dma_start(xs_dram, at, a_sb[:, par, t, :], None).then_inc(s_scat[par], 16)

            with pool.Fori(0, B // 2) as it:
                for par in range(2):
                    scatter(par, 2 * it + par)

            for par in range(2):
                pool.wait_ge(s_yst[par], 16 * ROUTED // 2)

            def pick(ns, n):
                if 0 <= ns < B:
                    par = ns % 2
                    ge(pool, s_comb, 2 * NT * (n - 1))
                    wait_apart(pool, s_idx2, n + 1, s_passed)
                    for t in range(NT):
                        for k in range(2):
                            at = bass.IndirectOffsetOnAxis(ap=idx_cur[:, par, 2 * t + k:2 * t + k + 1], axis=0)
                            pool.indirect_dma_start(picked[:, par, t, k, :], None, ys_dram, at).then_inc(s_pick[par], 16)
                if 0 <= ns - 1 < B:
                    par = (ns - 1) % 2
                    pool.wait_ge(s_seedC, SEED_OPS * n)
                    newton(pool, s_passed, s_newtC, NEWTON_OPS * (n - 1), rstd[:, par, :], root[:, par, 0, :], root[:, par, 2, :])

            combine_steps(pool, pick)

        @block.scalar
        def _(act):
            act.wait_ge(s_latT, 1)
            act.activation(latT[:], ps[0:LAT, 0, 0:3 * P].rearrange("p (n c) -> p n c", n=3), ACT.Copy).then_inc(s_latT_sb, 1)
            act.wait_ge(s_wmul, 1)
            act.activation(w_qkv[:, 0, :], ps[:, 1, 0:C], ACT.Copy, scale=float(HD) ** -0.5)
            act.activation(w_qkv[:, 1:3, :], ps[:, 1, C:3 * C].rearrange("p (n c) -> p n c", n=2), ACT.Copy).then_inc(s_wsb, 1)

            def copy_xT(par, b):
                act.wait_ge(s_xT, b + 1)
                ge(act, s_vp, b - 1)
                act.activation(xnT[:, par, :], ps[:, par, :], ACT.Copy).then_inc(s_xT_sb, 1)

            def first_parts(par, b, more):
                if more:
                    copy_xT(1 - par, b + 1)
                if isinstance(b, int):
                    if b >= 2:
                        act.wait_ge(s_parts[par], 12 * 16 * (b // 2))
                for s in range(2):
                    act.wait_ge(s_qkp, 2 * b + s + 1)
                    act.activation(part[:, par, s, 0, :], ps[:, 2 + 2 * s + par, :], ACT.Copy).then_inc(s_p1, 1)
                for s in range(2):
                    act.wait_ge(s_r, 2 * b + s + 1)
                    act.activation(part[:, par, s, 1, :], rest[:, par, s, :], ACT.Copy).then_inc(s_p2, 1)

            copy_xT(0, 0)
            for b in (0, 1):
                first_parts(b, b, True)
            with act.Fori(1, B // 2 - 1) as it:
                for par in range(2):
                    act.wait_ge(s_parts[par], 12 * 16 * it)
                    first_parts(par, 2 * it + par, True)
            for b in (B - 2, B - 1):
                first_parts(b % 2, b, b + 1 < B)

            def step(gs, g):
                for n in range(5):
                    if n == 4 and 0 <= gs - 1 < QUADS:
                        act.wait_ge(s_pv, g)
                        if gs - 3 >= 0:
                            pos = rot_items(gs - 1).index(("turn_back", 0))
                            act.wait_ge(s_rot, rot_base(gs - 1, g - 1) + pos + 1)
                        act.activation(outT[:, (gs - 1) % 2, :], ps[:, 6 + (gs - 1) % 2, :], ACT.Copy).then_inc(s_outT, 1)
                    if 0 <= gs < QUADS:
                        act.wait_ge(s_st, 5 * g + n + 1)
                        if n == 0:
                            ge(act, s_pv, g - 1)
                        u = 2 + 2 * ((5 * gs + n) % 2)
                        act.activation(pT[:, gs % 2, n, :], ps[:, u:u + 2, :].rearrange("p a b -> p (a b)"),
                                       ACT.Exp).then_inc(s_exp, 1)

            quad_steps(act, step)

            act.wait_ge(s_w2, 160)
            act.wait_ge(s_rotf, ROT_ALL)

            def shared(ns, n):
                if 0 <= ns < B:
                    par = ns % 2
                    ge(act, s_yT, n - 1)
                    act.activation(ycur[:, par], tiles4(y_sb, n), ACT.Copy).then_inc(s_ycur, 1)
                if 0 <= ns - SKEW < B:
                    par, b = (ns - SKEW) % 2, n - SKEW
                    act.wait_ge(s_xT2, b + 1)
                    ge(act, s_ha, 2 * b - 2)
                    act.activation(xT2[:, par, :], ps[:, 0, :], ACT.Copy).then_inc(s_xT2sb, 1)
                    act.activation(tiles4(v_all, b), xn2[:, par], ACT.Copy).then_inc(s_y, 1)
                    for j in range(2):
                        act.wait_ge(s_hg, 2 * b + j + 1)
                        ge(act, s_hid, 2 * b + j - 1)
                        act.activation(gel[:, j, :], ps[:, 4 + 2 * j, :], ACT.Gelu, bias=b_s1[:, 2 + j:3 + j]).then_inc(s_gel, 1)
                if 0 <= ns < B:
                    par = ns % 2
                    act.wait_ge(s_yT, n + 1)
                    ge(act, s_proj, n - 1)
                    act.activation(yT[:, par, :], ps[:, 0, :], ACT.Copy).then_inc(s_yTsb, 1)

            skewed(act, shared)
            act.wait_ge(s_rt, DIFFERENCE_STEP)
            act.activation(top[:, 4, :], top[:, 3, :], ACT.Exp, scale=1.0 / TAU).then_inc(s_exw, 1)
            act.wait_ge(s_y, B)
            for b in range(2):
                act.activation(a_sb[:, b], tiles4(v_all, b), ACT.Copy).then_inc(s_rows, 1)
            with act.Fori(1, B // 2) as it:
                for par in range(2):
                    act.wait_ge(s_scat[par], 16 * 2 * NT * it)
                    act.activation(a_sb[:, par], tiles4(v_all, 2 * it + par), ACT.Copy).then_inc(s_rows, 1)

            def expert_tile(js, j, more):
                par = js % 2
                act.wait_ge(s_xsT, j + 1)
                act.activation(xsT[:, par, :], ps[:, par, 0:C], ACT.Copy).then_inc(s_xsTsb, 1)
                act.wait_ge(s_he, j + 1)
                act.activation(gelE[:, par, :], ps[:, 2 + par, 0:HR], ACT.Gelu).then_inc(s_ge, 1)
                act.wait_ge(s_hT, j + 1)
                act.activation(hidT[:, par, :], ps[:, 6 + par, 0:HR], ACT.Copy).then_inc(s_hTsb, 1)

            tiles_by_four(act, expert_tile)

        @block.tensor
        def _(pe):
            pe.wait_ge(s_const, 1)
            pe.wait_ge(s_w, 6 * 16)
            for n in range(3):
                last = pe.transpose(ps[0:LAT, 0, n * P:(n + 1) * P], lat_in[:, n, :], ident[:])
            last.then_inc(s_latT, 1)
            pe.wait_ge(s_latT_sb, 1)
            for n in range(3):
                last = pe.matmul(ps[:, 1, n * C:(n + 1) * C], latT[:, n, :], heads_in[:, n, :], start=True, stop=True)
            last.then_inc(s_wmul, 1)
            pe.wait_ge(s_wsb, 1)

            def turn_x(par, b):
                pe.wait_ge(s_xn, b + 1)
                ge(pe, s_xT_sb, b - 1)
                for t in range(NT):
                    last = pe.transpose(ps[:, par, t * P:(t + 1) * P], xn[:, par, t, :], ident[:])
                last.then_inc(s_xT, 1)

            def project(par, b, more):
                if more:
                    turn_x(1 - par, b + 1)
                pe.wait_ge(s_xT_sb, b + 1)
                ge(pe, s_r, 2 * b - 2)
                for s in range(2):
                    pe.matmul(ps[:, 2 + 2 * s + par, :], w_qkv[:, s, :], xnT[:, par, :], start=True, stop=True).then_inc(s_qkp, 1)
                ge(pe, s_vsb, b - 1)
                for t in range(NT):
                    last = pe.matmul(ps[:, 6 + par, t * C:(t + 1) * C], xnT[:, par, t * P:(t + 1) * P], w_qkv[:, 2, :],
                                     start=True, stop=True)
                last.then_inc(s_vp, 1)

            turn_x(0, 0)
            project(0, 0, True)
            project(1, 1, True)
            with pe.Fori(1, B // 2 - 1) as it:
                for par in range(2):
                    project(par, 2 * it + par, True)
            for b in (B - 2, B - 1):
                project(b % 2, b, b + 1 < B)
            pe.wait_ge(s_r, 2 * B)
            pe.wait_ge(s_vsb, B)

            def rows(i, part_of_q, lo, hi, slot, k):
                base = 64 * (i // 2)
                return qk[base:base + k, slot, part_of_q, i % 2, lo:hi]

            def rot(gs, g, pos, kind, n):
                index = rot_base(gs, g) + pos
                bank = (rot_base(gs, gs) + pos) % 2
                ge(pe, s_rotf, index - 1)
                if kind == "scores":
                    slot = (gs + 2) % 4
                    if n == 0:
                        pe.wait_ge(s_qk[slot], 16 * (g + 2 - slot) + 64)
                    pr, j = divmod(n, 5)
                    if j < 4:
                        i = 2 * pr + j // 2
                        places = [(i, 3, 0)] if j % 2 == 0 else [(i, 2, 0), (i, 0, 384)]
                    else:
                        places = [(2 * pr, 1, 0), (2 * pr + 1, 1, 256)]
                    for i, qt, at in places:
                        w = (qt + 1) * P
                        pe.matmul(ps[:, bank, at:at + w], rows(i, 0, qt * P, qt * P + P, slot, QK_ROWS),
                                  rows(i, 1, 0, w, slot, QK_ROWS), start=True, stop=False)
                        last = pe.matmul(ps[:, bank, at + w - P:at + w], ident_bf[:], mask_q[:], start=False, stop=True)
                elif kind == "max_rows":
                    wait_apart(pe, s_msplit, 4 * (g + 2), s_passed)
                    last = pe.transpose(ps[0:48, bank, 0:64].bitcast(BF16), m_part[:, (gs + 1) % 2].rearrange("p n x -> p (n x)"),
                                        ident_bf[:])
                else:
                    pe.wait_ge(s_outT, g - 1)
                    for qt in range(NT):
                        last = pe.transpose(ps[:, bank, qt * P:(qt + 1) * P], outT[:, gs % 2, qt * P:(qt + 1) * P], ident[:])
                last.then_inc(s_rot, 1)

            def scores_by_key(gs, g, n, half):
                u = 2 + 2 * ((5 * gs + n) % 2) + half
                slot = gs % 4
                if half == 0:
                    ge(pe, s_exp, 5 * g + n - 1)
                    if n == 0:
                        pe.wait_ge(s_m[slot], 8 * (g - slot) + 32)
                if n < 4:
                    places = [(n, 0, 0)] if half == 0 else [(n, 1, 0), (n, 3, 384)]
                else:
                    places = [(2 * half, 2, 0), (2 * half + 1, 2, 256)]
                for i, kb, at in places:
                    w = T - kb * P
                    pe.matmul(ps[:, u, at:at + w], rows(i, 1, kb * P, kb * P + P, slot, ROWS),
                              rows(i, 0, kb * P, T, slot, ROWS), start=True, stop=False)
                    last = pe.matmul(ps[:, u, at:at + P], ident_bf[:], mask_k[:], start=False, stop=True)
                if half == 1:
                    last.then_inc(s_st, 1)

            def products(gs, g, kb):
                buf, slot = (gs - 1) % 2, (gs - 1) % 4
                if kb == 0:
                    pe.wait_ge(s_exp, 5 * g)
                    pe.wait_ge(s_vcur, g)
                    ge(pe, s_outT, g - 2)
                w = T - kb * P
                for i in range(4):
                    at = i * 1024 + (0, 512, 0, 896)[kb] if kb != 2 else 4 * 1024 + i * 256
                    flat = pT[:, buf].rearrange("p n t -> p (n t)")
                    last = pe.matmul(ps[32 * i:32 * i + 32, 6 + buf, kb * P:T], v_cur[:, slot, kb, i, :], flat[:, at:at + w],
                                     start=(kb == 0), stop=(kb == 3))
                if kb == 3:
                    last.then_inc(s_pv, 1)

            def step(gs, g):
                items = rot_items(gs)
                todo = list(enumerate(items))

                def some(k):
                    for _ in range(k):
                        if todo:
                            pos, (kind, n) = todo.pop(0)
                            rot(gs, g, pos, kind, n)

                for n in range(5):
                    if 0 <= gs < QUADS:
                        scores_by_key(gs, g, n, 0)
                    some(1)
                    if 0 <= gs < QUADS:
                        scores_by_key(gs, g, n, 1)
                    some(1)
                    if n < 4 and 0 <= gs - 1 < QUADS:
                        products(gs, g, n)
                    if n in (1, 3):
                        some(1)
                some(12)

            quad_steps(pe, step)

            pe.wait_ge(s_w2, 160)
            pe.wait_ge(s_rotf, ROT_ALL)
            pe.wait_ge(s_outT, QUADS)

            def shared(ns, n):
                if 0 <= ns - SKEW < B:
                    par, b = (ns - SKEW) % 2, n - SKEW
                    pe.wait_ge(s_xn2, b + 1)
                    if ns - 1 < B:
                        pe.wait_ge(s_yTsb, n)
                    else:
                        pe.wait_ge(s_yTsb, B)
                        pe.wait_ge(s_xT2sb, b)
                    for t in range(NT):
                        last = pe.transpose(ps[:, 0, t * P:(t + 1) * P], xn2[:, par, t, :], ident[:])
                    last.then_inc(s_xT2, 1)
                    pe.wait_ge(s_xT2sb, b + 1)
                    ge(pe, s_lgsb, b)
                    for t in range(NT):
                        last = pe.matmul(ps[:, 3, t * E:(t + 1) * E], xT2[:, par, t * P:(t + 1) * P], w_r[:],
                                         start=True, stop=True)
                    last.then_inc(s_lg, 1)
                    for j in range(2):
                        ge(pe, s_gel, 2 * b + j - 1)
                        pe.matmul(ps[:, 4 + 2 * j, :], ws1[:, HS + j * P:HS + (j + 1) * P], xT2[:, par, :],
                                  start=True, stop=True).then_inc(s_hg, 1)
                        ge(pe, s_hid, 2 * b + j - 1)
                        pe.matmul(ps[:, 5 + 2 * j, :], ws1[:, j * P:(j + 1) * P], xT2[:, par, :],
                                  start=True, stop=True).then_inc(s_ha, 1)
                if 0 <= ns < B:
                    par = ns % 2
                    pe.wait_ge(s_ycur, n + 1)
                    if ns - SKEW >= 0:
                        pe.wait_ge(s_xT2sb, n - SKEW + 1)
                    else:
                        ge(pe, s_yTsb, n)
                    for t in range(NT):
                        last = pe.transpose(ps[:, 0, t * P:(t + 1) * P], ycur[:, par, t, :], ident[:])
                    last.then_inc(s_yT, 1)
                    pe.wait_ge(s_yTsb, n + 1)
                    ge(pe, s_a, n)
                    for t in range(NT):
                        last = pe.matmul(ps[:, 1, t * C:(t + 1) * C], yT[:, par, t * P:(t + 1) * P], w_proj[:],
                                         start=True, stop=True)
                    last.then_inc(s_proj, 1)
                if 0 <= ns - SKEW < B:
                    b = n - SKEW
                    pe.wait_ge(s_hid, 2 * b + 2)
                    ge(pe, s_ysum, b)
                    for t in range(NT):
                        for j in range(2):
                            last = pe.matmul(ps[:, 2, t * C:(t + 1) * C], hid[:, j, t * P:(t + 1) * P], ws2[:, j, :],
                                             start=(j == 0), stop=(j == 1))
                    last.then_inc(s_y2, 1)

            skewed(pe, shared)

            pe.wait_ge(s_rt, BOTH_STEP)
            pe.wait_ge(s_ysum, B)
            flat = both.rearrange("p t e -> p (t e)")
            half = TILES * E // 2
            for k in range(2):
                pe.matmul(ps[:, k, 0:half], before[:], flat[:, k * half:(k + 1) * half], start=True, stop=True)
                last = pe.matmul(ps[:, 2 + k, 0:half], ones[:], flat[:, k * half:(k + 1) * half], start=True, stop=True)
            last.then_inc(s_pref, 1)

            pe.wait_ge(s_rt, ROUTING_STEPS)
            pe.wait_ge(s_we, 16 * 2 * E)
            pe.wait_ge(s_ber, 32)

            def turn_rows(js, j):
                pe.wait_ge(s_xs[js % 4], 16 * (j // 4 + 1) if isinstance(j, int) else 4 * (j - js % 4) + 16)
                ge(pe, s_yesb, j - 1)
                pe.transpose(ps[:, js % 2, 0:C], xs[:, js % 4, :], ident[:]).then_inc(s_xsT, 1)

            def expert_tile(js, j, more):
                par = js % 2
                e = pe.value_load(etile[0:1, bass.ds(j, 1)], min_val=0, max_val=E - 1)
                pe.wait_ge(s_xsTsb, j + 1)
                for k, bank in ((1, 2 + par), (0, 4 + par)):
                    ge(pe, s_ge if k else s_hide, j - 1)
                    pe.matmul(ps[:, bank, 0:HR], ones_bf[:], be1r[:, bass.ds(e * (2 * HR) + k * HR, HR)], start=True, stop=False)
                    last = pe.matmul(ps[:, bank, 0:HR], xsT[:, par, :], we1[:, bass.ds(e * (2 * HR) + k * HR, HR)],
                                     start=False, stop=True)
                last.then_inc(s_he, 1)
                if more or js < 3:
                    turn_rows(js + 1, j + 1)
                pe.wait_ge(s_hide, j + 1)
                ge(pe, s_hTsb, j - 1)
                for k in range(3):
                    last = pe.transpose(ps[:, 6 + par, k * P:(k + 1) * P], hidE[:, par, k * P:(k + 1) * P], ident[:])
                last.then_inc(s_hT, 1)
                pe.wait_ge(s_hTsb, j + 1)
                pe.matmul(ps[:, par, 0:C], ones_bf[:], be2r[:, bass.ds(e * C, C)], start=True, stop=False)
                for k in range(3):
                    last = pe.matmul(ps[:, par, 0:C], hidT[:, par, k * P:(k + 1) * P], we2[:, bass.ds(e * HR + k * P, P)],
                                     start=False, stop=(k == 2))
                last.then_inc(s_ye, 1)

            turn_rows(0, 0)
            tiles_by_four(pe, expert_tile)

        @block.vector
        def _(dve):
            def norm_x(par, b):
                x4 = tiles4(x_sb, b)
                for t in range(NT):
                    last = dve.bn_stats(st[:, par, t, :], x4[:, t, :])
                last.then_inc(s_stats, 1)
                wait_apart(dve, s_stats, b + 1, s_passed)
                for t in range(NT):
                    last = dve.bn_aggr(mv[:, par, t, :], st[:, par, t, :])
                last.then_inc(s_seed, 1)
                seed(dve, s_seed, SEED_OPS * b + 1, rstd[:, par, :], root[:, par, 0, :], root[:, par, 1, :], mv[:, par, :, 1])
                dve.wait_ge(s_newton, NEWTON_OPS * (b + 1))
                ge(dve, s_xT, b - 1)
                for t in range(NT):
                    last = dve.tensor_scalar(xn[:, par, t, :], x4[:, t, :], mv[:, par, t, 0:1], rstd[:, par, t:t + 1],
                                             ALU.subtract, ALU.mult)
                last.then_inc(s_xn, 1)

            def rests(par, b, more):
                if more:
                    norm_x(1 - par, b + 1)
                for s in range(2):
                    dve.wait_ge(s_p1, 2 * b + s + 1)
                    ge(dve, s_p3, 2 * b + s - 3)
                    dve.tensor_tensor(rest[:, par, s, :], ps[:, 2 + 2 * s + par, :], part[:, par, s, 0, :],
                                      ALU.subtract).then_inc(s_r, 1)
                dve.wait_ge(s_vp, b + 1)
                dve.tensor_copy(tiles4(v_all, b), ps[:, 6 + par, :].rearrange("p (t c) -> p t c", c=C)).then_inc(s_vsb, 1)

            dve.wait_ge(s_w2, 160)
            dve.tensor_copy(be_part[:, 0, :], be_in[:]).then_inc(s_be, 1)
            dve.wait_ge(s_be, 1)
            dve.tensor_tensor(be_rest[:], be_in[:], be_part[:, 0, :], ALU.subtract).then_inc(s_be, 1)
            dve.wait_ge(s_be, 2)
            dve.tensor_copy(be_part[:, 1, :], be_rest[:]).then_inc(s_be, 1)
            dve.wait_ge(s_be, 3)
            dve.tensor_tensor(be_part[:, 2, :], be_rest[:], be_part[:, 1, :], ALU.subtract).then_inc(s_be, 1)
            dve.wait_ge(s_x, 64)
            norm_x(0, 0)
            rests(0, 0, True)
            rests(1, 1, True)
            with dve.Fori(1, B // 2 - 1) as it:
                for par in range(2):
                    rests(par, 2 * it + par, True)
            for b in (B - 2, B - 1):
                rests(b % 2, b, b + 1 < B)

            def take(gs, g, pos, kind, n):
                index = rot_base(gs, g) + pos
                bank = (rot_base(gs, gs) + pos) % 2
                dve.wait_ge(s_rot, index + 1)
                if kind == "scores":
                    buf = (gs + 2) % 2
                    pr, j = divmod(n, 5)
                    if n == 0:
                        ge(dve, s_msplit, 4 * (g + 1))
                    if j < 4:
                        i = 2 * pr + j // 2
                        places = [(i, 3, 0)] if j % 2 == 0 else [(i, 2, 0), (i, 0, 384)]
                        for i, qt, at in places:
                            last = dve.tensor_reduce(m_q[:, buf, 4 * i + qt:4 * i + qt + 1],
                                                     ps[:, bank, at:at + (qt + 1) * P], AX, ALU.max)
                    else:
                        cols = m_q[:, buf, 8 * pr:8 * pr + 8].rearrange("p (i q) -> p i q", q=4)[:, :, 1]
                        last = dve.tensor_reduce(cols, ps[:, bank, :].rearrange("p (i k) -> p i k", i=2), AX, ALU.max)
                    last.then_inc(s_rotf, 1)
                    if n == 9:
                        done = 4 * (g + 2)
                        dve.wait_ge(s_rotf, index + 1)
                        dve.tensor_scalar(m_part[:, buf, 0, :], m_q[:, buf, :], -1.0, None, ALU.mult).then_inc(s_msplit, 1)
                        dve.wait_ge(s_msplit, done + 1)
                        dve.scalar_tensor_tensor(out=m_rest[:, buf, :], in0=m_q[:, buf, :], scalar=-1.0,
                                                 in1=m_part[:, buf, 0, :], op0=ALU.mult, op1=ALU.subtract).then_inc(s_msplit, 1)
                        dve.wait_ge(s_msplit, done + 2)
                        dve.tensor_copy(m_part[:, buf, 1, :], m_rest[:, buf, :]).then_inc(s_msplit, 1)
                        dve.wait_ge(s_msplit, done + 3)
                        dve.tensor_tensor(m_part[:, buf, 2, :], m_rest[:, buf, :], m_part[:, buf, 1, :],
                                          ALU.subtract).then_inc(s_msplit, 1)
                elif kind == "max_rows":
                    ge(dve, s_mw, 16 * g)
                    dve.tensor_copy(mT_sb[:, (gs + 1) % 2, :], ps[0:48, bank, 0:64].bitcast(BF16)).then_inc(s_rotf, 1)
                else:
                    o = ps[:, bank, :].rearrange("p (t i r) -> p t i r", t=NT, i=4)
                    dve.reciprocal(rden[:, gs % 2], o[:, :, :, HD]).then_inc(s_rden, 1)
                    dve.wait_ge(s_rden, g - 1)
                    q = (gs - 2) % 4
                    y4 = (y_sb[:, g - 2 - q:g + 2 - q] if isinstance(g, int) else y_sb[:, bass.ds(g - 2 - q, 4)])
                    dve.tensor_tensor(y4[:, :, 32 * q:32 * q + 32].rearrange("p t (i d) -> p t i d", d=HD),
                                      o[:, :, :, 0:HD], rden[:, gs % 2].rearrange("p t (i o) -> p t i o", o=1).broadcast_to([P, NT, 4, HD]),
                                      ALU.mult).then_inc(s_rotf, 1)

            def step(gs, g):
                for pos, (kind, n) in enumerate(rot_items(gs)):
                    take(gs, g, pos, kind, n)

            quad_steps(dve, step)

            def stats(x4, st_, mv_, s_stat, s_seed_, par, b, y, r):
                for t in range(NT):
                    last = dve.bn_stats(st_[:, par, t, :], x4[:, t, :])
                last.then_inc(s_stat, 1)
                wait_apart(dve, s_stat, b + 1, s_passed)
                for t in range(NT):
                    last = dve.bn_aggr(mv_[:, par, t, :], st_[:, par, t, :])
                last.then_inc(s_seed_, 1)
                seed(dve, s_seed_, SEED_OPS * b + 1, y[:, par, :], r[:, par, 0, :], r[:, par, 1, :], mv_[:, par, :, 1])

            def spread(row, n):
                return row[:].rearrange("p (o n) -> p o n", o=1).broadcast_to([P, NT, n])

            def shared(ns, n):
                if 0 <= ns < B:
                    par = ns % 2
                    dve.wait_ge(s_proj, n + 1)
                    dve.tensor_tensor(a_sb[:, par], ps[:, 1, :].rearrange("p (t c) -> p t c", c=C), spread(b_proj, C),
                                      ALU.add).then_inc(s_a, 1)
                    dve.wait_ge(s_a, n + 1)
                    stats(a_sb[:, par], st, mv, s_stA, s_seedA, par, n, rstd, root)
                if 0 <= ns - 1 < B:
                    par, b = (ns - 1) % 2, n - 1
                    x4 = tiles4(x_sb, b)
                    dve.wait_ge(s_newtA, NEWTON_OPS * (b + 1))
                    for t in range(NT):
                        last = dve.tensor_scalar(a_sb[:, par, t, :], a_sb[:, par, t, :], mv[:, par, t, 0:1],
                                                 rstd[:, par, t:t + 1], ALU.subtract, ALU.mult)
                    last.then_inc(s_res, 1)
                    dve.wait_ge(s_res, 2 * b + 1)
                    dve.tensor_tensor(x4, x4, a_sb[:, par], ALU.add).then_inc(s_res, 1)
                    wait_apart(dve, s_res, 2 * b + 2, s_passed)
                    stats(x4, st2, mv2, s_st2, s_seedB, par, b, rstd2, root2)
                if 0 <= ns - 2 < B:
                    par, b = (ns - 2) % 2, n - 2
                    x4 = tiles4(x_sb, b)
                    dve.wait_ge(s_newtB, NEWTON_OPS * (b + 1))
                    ge(dve, s_xT2, b - 1)
                    ge(dve, s_y, b - 1)
                    for t in range(NT):
                        last = dve.tensor_scalar(xn2[:, par, t, :], x4[:, t, :], mv2[:, par, t, 0:1],
                                                 rstd2[:, par, t:t + 1], ALU.subtract, ALU.mult)
                    last.then_inc(s_xn2, 1)
                if 0 <= ns - SKEW < B:
                    b = n - SKEW
                    dve.wait_ge(s_lg, b + 1)
                    dve.tensor_tensor(tiles4(logits, b), ps[:, 3, 0:NT * E].rearrange("p (t e) -> p t e", e=E), spread(b_r, E),
                                      ALU.add).then_inc(s_lgsb, 1)
                    for j in range(2):
                        dve.wait_ge(s_gel, 2 * b + j + 1)
                        dve.wait_ge(s_ha, 2 * b + j + 1)
                        ge(dve, s_y2, b)
                        dve.scalar_tensor_tensor(out=hid[:, j, :], in0=ps[:, 5 + 2 * j, :], scalar=b_s1[:, j:j + 1],
                                                 in1=gel[:, j, :], op0=ALU.add, op1=ALU.mult).then_inc(s_hid, 1)
                    dve.wait_ge(s_y2, b + 1)
                    dve.tensor_tensor(tiles4(ysum, b), ps[:, 2, :].rearrange("p (t c) -> p t c", c=C), spread(b_s2, C),
                                      ALU.add).then_inc(s_ysum, 1)

            skewed(dve, shared)

            def wide(t):
                return t.rearrange("p (t o) -> p t o", o=1).broadcast_to([P, TILES, E])

            def per_expert(t):
                return t.rearrange("p (o e) -> p o e", o=1).broadcast_to([P, TILES, E])

            done = 0

            def then(ins):
                nonlocal done
                done += 1
                ins.then_inc(s_rt, 1)
                dve.wait_ge(s_rt, done)

            numbers = per_expert(iota_f[:, ROUTED:])
            dve.wait_ge(s_lgsb, B)
            source = logits[:]
            for k in range(2):
                then(dve.tensor_reduce(top[:, k, :], source, AX, ALU.max))
                then(dve.tensor_tensor(lowest, source, wide(top[:, k, :]), ALU.is_equal))
                then(dve.tensor_tensor(lowest, lowest, numbers, ALU.mult))
                then(dve.tensor_reduce(top[:, 2, :], lowest, AX, ALU.min))
                then(dve.tensor_tensor(onehot[k], numbers, wide(top[:, 2, :]), ALU.is_equal))
                if k == 0:
                    then(dve.scalar_tensor_tensor(out=both, in0=onehot[0], scalar=-HUGE, in1=logits[:], op0=ALU.mult, op1=ALU.add))
                    source = both
            then(dve.tensor_tensor(both, onehot[0], onehot[1], ALU.add))
            assert done == BOTH_STEP
            then(dve.tensor_tensor(top[:, 3, :], top[:, 1, :], top[:, 0, :], ALU.subtract))
            assert done == DIFFERENCE_STEP
            dve.wait_ge(s_exw, 1)
            then(dve.tensor_scalar(top[:, 5, :], top[:, 4, :], 1.0, None, ALU.add))
            then(dve.reciprocal(weight[:, 0, :], top[:, 5, :]))
            then(dve.tensor_tensor(weight[:, 1, :], top[:, 4, :], weight[:, 0, :], ALU.mult))
            dve.wait_ge(s_pref, 1)

            def halves(bank):
                return ps[:, bank:bank + 2, 0:TILES * E // 2]

            def split2(t):
                return t.rearrange("p (k t) e -> p k (t e)", k=2)

            then(dve.tensor_copy(split2(counts[0]), halves(2)))
            at, s_ = 0, 1
            while s_ < TILES:
                then(dve.tensor_tensor(counts[1 - at][:, s_:, :], counts[at][:, s_:, :], counts[at][:, :TILES - s_, :], ALU.add))
                then(dve.tensor_copy(counts[1 - at][:, :s_, :], counts[at][:, :s_, :]))
                at, s_ = 1 - at, 2 * s_
            then(dve.tensor_scalar(small[:, 0, :], counts[at][:, TILES - 1, :], float(P - 1), None, ALU.add))
            then(dve.tensor_copy(small_i[:, 0, :], small[:, 0, :]))
            then(dve.tensor_scalar(small_i[:, 1, :], small_i[:, 0, :], 7, None, ALU.arith_shift_right))
            then(dve.tensor_copy(small[:, 1, :], small_i[:, 1, :]))
            then(dve.tensor_copy(small[:, 2, :], small[:, 1, :]))
            end, s_ = 2, 1
            while s_ < E:
                then(dve.tensor_tensor(small[:, 5 - end, s_:], small[:, end, s_:], small[:, end, :E - s_], ALU.add))
                then(dve.tensor_copy(small[:, 5 - end, :s_], small[:, end, :s_]))
                end, s_ = 5 - end, 2 * s_
            then(dve.tensor_tensor(small[:, 4, :], small[:, end, :], small[:, 1, :], ALU.subtract))
            then(dve.tensor_scalar(small[:, 5, :], small[:, 4, :], float(P), None, ALU.mult))
            then(dve.tensor_scalar(etile_f[:, 0, :], iota_f[0:1, 0:ROUTED], small[0:1, end, 0:1], None, ALU.is_ge))
            for e in range(1, E):
                then(dve.scalar_tensor_tensor(out=etile_f[:, e % 2, :], in0=iota_f[0:1, 0:ROUTED], scalar=small[0:1, end, e:e + 1],
                                              in1=etile_f[:, 1 - e % 2, :], op0=ALU.is_ge, op1=ALU.add))
            then(dve.tensor_scalar(etile_f[:, E % 2, :], etile_f[:, 1 - E % 2, :], float(E - 1), None, ALU.min))
            then(dve.tensor_copy(etile[:], etile_f[:, E % 2, :]))
            then(dve.tensor_tensor(split2(counts[at]), split2(counts[at]), halves(2), ALU.subtract))
            then(dve.tensor_tensor(split2(counts[at]), split2(counts[at]), halves(0), ALU.add))
            then(dve.tensor_tensor(counts[at], counts[at], per_expert(small[:, 5, :]), ALU.add))
            for k in range(2):
                then(dve.tensor_tensor(onehot[k], onehot[k], counts[at], ALU.mult))
                then(dve.tensor_reduce(top[:, k, :], onehot[k], AX, ALU.add))
                then(dve.tensor_copy(slot_i[:, :, k], top[:, k, :]))
            assert done == ROUTING_STEPS, done

            def stage_slots(par, b, sem_):
                b4 = slot_i[:, 4 * b:4 * b + 4, :] if isinstance(b, int) else slot_i[:, bass.ds(4 * b, 4), :]
                dve.tensor_copy(idx_cur[:, par, :], b4.rearrange("p t k -> p (t k)")).then_inc(sem_, 1)

            for b in range(2):
                stage_slots(b, b, s_idx)
            with dve.Fori(1, B // 2) as it:
                for par in range(2):
                    dve.wait_ge(s_scat[par], 16 * 2 * NT * it)
                    stage_slots(par, 2 * it + par, s_idx)

            def expert_tile(js, j, more):
                par = js % 2
                dve.wait_ge(s_ge, j + 1)
                ge(dve, s_hT, j - 1)
                dve.tensor_tensor(hidE[:, par, :], ps[:, 4 + par, 0:HR], gelE[:, par, :], ALU.mult).then_inc(s_hide, 1)
                dve.wait_ge(s_ye, j + 1)
                if isinstance(j, int):
                    if j >= 2:
                        dve.wait_ge(s_yst[par], 16 * (j // 2))
                else:
                    dve.wait_ge(s_yst[par], 8 * (j - par))
                dve.tensor_copy(ys[:, par, :], ps[:, par, 0:C]).then_inc(s_yesb, 1)

            tiles_by_four(dve, expert_tile)

            for b in range(2):
                dve.wait_ge(s_scat[b], 16 * NT * B)
                stage_slots(b, b, s_idx2)

            def combine(ns, n):
                if 0 <= ns < B:
                    par = ns % 2
                    dve.wait_ge(s_pick[par], 16 * 2 * NT * (n // 2 + 1) if isinstance(n, int) else 16 * NT * (n - par) + 16 * 2 * NT)
                    if ns + 2 < B or not isinstance(n, int):
                        stage_slots(par, n + 2, s_idx2)
                    y4 = tiles4(ysum, n)
                    for k in range(2):
                        for t in range(NT):
                            dve.scalar_tensor_tensor(out=summed[:, par, t, :], in0=picked[:, par, t, k, :],
                                                     scalar=col(weight, k, 4 * n + t), in1=(y4[:, t, :] if k == 0 else summed[:, par, t, :]),
                                                     op0=ALU.mult, op1=ALU.add).then_inc(s_comb, 1)
                        dve.wait_ge(s_comb, 2 * NT * n + NT * (k + 1))
                    stats(summed[:, par], st, mv, s_st3, s_seedC, par, n, rstd, root)
                if 0 <= ns - 1 < B:
                    par, b = (ns - 1) % 2, n - 1
                    dve.wait_ge(s_newtC, NEWTON_OPS * (b + 1))
                    ge(dve, s_out[par], 8 * (b - par))
                    for t in range(NT):
                        last = dve.tensor_scalar(final[:, par, t, :], summed[:, par, t, :], mv[:, par, t, 0:1],
                                                 rstd[:, par, t:t + 1], ALU.subtract, ALU.mult)
                    last.then_inc(s_fin, 1)
                    dve.wait_ge(s_fin, 2 * b + 1)
                    dve.tensor_tensor(final[:, par], final[:, par], tiles4(x_sb, b), ALU.add).then_inc(s_fin, 1)

            combine_steps(dve, combine)


_OUTS = [((16, 512, 128), "float32")]


def kernel(**inputs):
    import numpy as _np
    import concourse.bacc as _bacc
    from concourse import mybir as _mybir
    from concourse.bass_utils import run_bass_kernel_spmd as _run

    nc = _bacc.Bacc("TRN2", target_bir_lowering=False, num_devices=1)
    arrays, aps = {}, {}
    for name, value in inputs.items():
        v = _np.ascontiguousarray(value)
        arrays[f"in_{name}"] = v
        aps[name] = nc.dram_tensor(f"in_{name}", v.shape, _mybir.dt.from_np(v.dtype), kind="ExternalInput").ap()
    shape, dtype = _OUTS[0]
    out = nc.dram_tensor("out_0_dram", shape, _mybir.dt.from_np(_np.dtype(dtype)), kind="ExternalOutput").ap()
    build(nc, aps, out)
    r = _run(nc, [arrays], core_ids=[0])
    return r.results[0]["out_0_dram"]
```

```python
from contextlib import ExitStack

import concourse.bass as bass
from concourse import mybir

ALU = mybir.AluOpType
ACT = mybir.ActivationFunctionType
AX = mybir.AxisListType.X
F32 = mybir.dt.float32
BF16 = mybir.dt.bfloat16
I32 = mybir.dt.int32

P = 128
B, T, C = 16, 512, 128
NT = T // P
TILES = B * NT
LAT, HEADS, HD = 32, 16, 8
QUADS = B * HEADS // 4
E, HS, HR = 12, 256, 384
TAU = 1.5
EPS = 1e-5
MASKED = -1e30
ROUTED = -(-(2 * B * T // P + E - 1) // 4) * 4
FAR = 16.0
HUGE = 3e38
ROW = C + 2
VALUES, PLACE, WEIGHT = slice(0, C), slice(C, C + 1), slice(C + 1, C + 2)
Q_SLOTS = (0, 0, 1, 1, 0, 2)
K_SLOTS = (0, 1, 0, 1, 2, 0)
QK_ROWS = HD * len(Q_SLOTS)
ROWS = QK_ROWS + 3


BOTH_STEP = 12
DIFFERENCE_STEP = 13
ROUTING_STEPS = 67


def wait_apart(engine, sem, value, passed):
    engine.wait_ge(sem, value)
    engine.sem_inc(passed, 1)


def ge(engine, sem, value):
    if not (isinstance(value, int) and value <= 0):
        engine.wait_ge(sem, value)


def rot_items(g):
    items = []
    for n in range(12):
        if n == 3:
            if 0 <= g + 1 < QUADS:
                items.append(("max_rows", 0))
        elif n == 7:
            if 0 <= g - 2 < QUADS:
                items.append(("turn_back", 0))
        elif g + 2 < QUADS:
            items.append(("scores", n - (n > 3) - (n > 7)))
    return items


FIRST, LAST = -2, QUADS + 1
ROT_BASE = {}
_n = 0
for _g in range(FIRST, LAST + 1):
    ROT_BASE[_g] = _n
    _n += len(rot_items(_g))
ROT_PER = 12


def rot_base(gs, g):
    if isinstance(g, int):
        return ROT_BASE[g]
    return ROT_PER * g + (ROT_BASE[gs] - ROT_PER * gs)


NEWTON = 3
NEWTON_OPS = 4 * NEWTON
SEED_OPS = 4


def seed(dve, sem, done, y, v, half, var):
    dve.wait_ge(sem, done)
    dve.tensor_scalar(v, var, EPS, None, ALU.add).then_inc(sem, 1)
    dve.wait_ge(sem, done + 1)
    dve.tensor_scalar(half.bitcast(I32), v.bitcast(I32), 1, None, ALU.arith_shift_right).then_inc(sem, 1)
    dve.wait_ge(sem, done + 2)
    dve.tensor_scalar(y.bitcast(I32), half.bitcast(I32), -1.0, float(0x5F3759DF), ALU.mult, ALU.add).then_inc(sem, 1)


def newton(pool, passed, sem, done, y, v, t):
    for _ in range(NEWTON):
        pool.tensor_tensor(t, y, y, ALU.mult).then_inc(sem, 1)
        pool.wait_ge(sem, done + 1)
        pool.tensor_tensor(t, t, v, ALU.mult).then_inc(sem, 1)
        wait_apart(pool, sem, done + 2, passed)
        pool.tensor_scalar(t, t, -0.5, 1.5, ALU.mult, ALU.add).then_inc(sem, 1)
        pool.wait_ge(sem, done + 3)
        pool.tensor_tensor(y, y, t, ALU.mult).then_inc(sem, 1)
        done = done + 4
        pool.wait_ge(sem, done)


def rows_of(vector, n):
    return vector.rearrange("(o n) -> o n", o=1).broadcast_to([P, n])


def build(nc, a, out):
    with ExitStack() as ctx:
        def sb(name, shape, dt=F32):
            return ctx.enter_context(nc.sbuf_tensor(name, shape, dt))

        def sem(name):
            return ctx.enter_context(nc.semaphore(name))

        x_sb = sb("x_sb", [P, TILES, C])
        v_all = sb("v_all", [P, TILES, C])
        y_sb = sb("y_sb", [P, TILES, C])
        ident = sb("ident", [P, P])
        ident_bf = sb("ident_bf", [P, P], BF16)
        mask_q = sb("mask_q", [P, P], BF16)
        mask_k = sb("mask_k", [P, P], BF16)
        ysum = y_sb
        late = v_all[:, TILES - 8:TILES, :].rearrange("p t c -> p (t c)")
        lat_in = late[:, 0:3 * LAT].rearrange("p (n c) -> p n c", n=3)
        heads_in = late[0:LAT, P:4 * P].rearrange("p (n c) -> p n c", n=3)
        latT = late[0:LAT, 4 * P:7 * P].rearrange("p (n c) -> p n c", n=3)
        iota_i = v_all[:, TILES - 10:TILES - 8, :].rearrange("p t c -> p (t c)")[:, 0:ROUTED + E].bitcast(I32)
        tag_i = v_all[:, TILES - 13:TILES - 10, :].rearrange("p t c -> p (t c)")[:, 0:ROUTED + 2 * TILES].bitcast(I32)
        w_qkv = sb("w_qkv", [P, 3, C])
        st = sb("st", [P, 2, NT, 6])
        mv = sb("mv", [P, 2, NT, 2])
        rstd = sb("rstd", [P, 2, NT])
        root = sb("root", [P, 2, 3, NT])
        row_area = sb("row_area", [P, 2 * NT * ROW])
        xn = row_area[:, 0:2 * NT * C].rearrange("p (a t c) -> p a t c", a=2, c=C)
        xnT = sb("xnT", [P, 2, T])
        split_area = sb("split_area", [P, 5 * 1024])
        part = split_area[:, 0:3 * 1024].bitcast(BF16).rearrange("p (a b c t) -> p a b c t", a=2, b=2, c=3)
        rest = split_area[:, 3 * 1024:5 * 1024].rearrange("p (a b t) -> p a b t", a=2, b=2)
        we2 = split_area[:, 0:E * HR]
        quad_area = sb("quad_area", [P, 6 * 1024])
        qk = quad_area[:, 0:4 * 1024].bitcast(BF16).rearrange("p (q s r t) -> p q s r t", q=4, s=2, r=2)
        v_cur = quad_area[:, 4 * 1024:6 * 1024].rearrange("p (q t h r) -> p q t h r", q=4, t=NT, h=4)
        be1r = quad_area[0:3, 0:E * HR].bitcast(BF16)
        be2r = quad_area[0:3, 5 * 1024:5 * 1024 + E * C // 2].bitcast(BF16)
        pT_area = sb("pT_area", [P, 10 * 1024])

        def area(n, count=1):
            return pT_area[:, 1024 * n:1024 * (n + count)]

        pT = pT_area[:, :].rearrange("p (a n t) -> p a n t", a=2, n=5)
        ycur = area(0).rearrange("p (a t c) -> p a t c", a=2, c=C)
        yT = area(1).rearrange("p (a t) -> p a t", a=2)
        xn2 = area(2).rearrange("p (a t c) -> p a t c", a=2, c=C)
        gel = area(3).rearrange("p (a t) -> p a t", a=2)
        hid = area(4).rearrange("p (a t) -> p a t", a=2)
        lowest = area(5)[:, 0:TILES * E].rearrange("p (t e) -> p t e", e=E)
        onehot = [area(6 + k)[:, 0:TILES * E].rearrange("p (t e) -> p t e", e=E) for k in range(2)]
        both = area(8)[:, 0:TILES * E].rearrange("p (t e) -> p t e", e=E)
        counts = [area(9 * k)[:, 0:TILES * E].rearrange("p (t e) -> p t e", e=E) for k in range(2)]
        top = area(1)[:, 0:6 * TILES].rearrange("p (k t) -> p k t", k=6)
        small = area(1)[:, 6 * TILES:6 * TILES + 6 * E].rearrange("p (k e) -> p k e", e=E)
        small_i = area(1)[:, 512:512 + 2 * E].bitcast(I32).rearrange("p (k e) -> p k e", e=E)
        etile_f = area(1)[0:1, 640:640 + 2 * ROUTED].rearrange("p (k j) -> p k j", k=2)
        we1 = pT_area[:, 0:E * 2 * HR]
        picked = area(0, 2).rearrange("p (a k t c) -> p a k t c", a=2, t=NT, k=2)
        summed = area(2).rearrange("p (a t c) -> p a t c", a=2, t=NT)
        final = area(3).rearrange("p (a t c) -> p a t c", a=2, t=NT)
        m_q = sb("m_q", [P, 2, 16])
        m_rest = sb("m_rest", [P, 2, 16])
        m_part = sb("m_part", [P, 2, 3, 16], BF16)
        mT_sb = sb("mT_sb", [48, 2, P], BF16)
        outT_area = sb("outT_area", [P, 2 * NT * ROW])
        outT = outT_area[:, 0:2 * T].rearrange("p (a t) -> p a t", a=2)
        logits = sb("logits", [P, TILES, E])
        a_sb = xn
        xT2 = xnT
        rows_cur = [area_[:, :].rearrange("p (a t c) -> p a t c", a=2, c=ROW) for area_ in (row_area, outT_area)]
        xs = row_area[:, 0:4 * ROW].rearrange("p (a c) -> p a c", a=4)
        xsT = row_area[:, 4 * ROW:4 * ROW + 2 * C].rearrange("p (a c) -> p a c", a=2)
        ys = row_area[:, 4 * ROW + 2 * C:4 * ROW + 4 * C].rearrange("p (a c) -> p a c", a=2)
        gelE = xnT[:].rearrange("p a t -> p (a t)")[:, 0:2 * HR].rearrange("p (a h) -> p a h", a=2)
        hidE = outT_area[:, 0:2 * HR].rearrange("p (a h) -> p a h", a=2)
        hidT = logits[:].rearrange("p t e -> p (t e)").rearrange("p (a h) -> p a h", a=2)
        w_proj = sb("w_proj", [P, C])
        w_r = sb("w_r", [P, E])
        ws1 = sb("ws1", [P, 2 * HS])
        ws2 = sb("ws2", [P, 2, C])
        b_proj = sb("b_proj", [P, C])
        b_s1 = sb("b_s1", [P, 4])
        b_s2 = sb("b_s2", [P, C])
        b_r = sb("b_r", [P, E])
        be_in = outT_area[:, 0:84]
        be_rest = outT_area[:, 84:168]
        be_part = outT_area[:, 168:168 + 126].bitcast(BF16).rearrange("p (n x) -> p n x", n=3)
        ones_bf = sb("ones_bf", [3, P], BF16)
        before = sb("before", [P, P])
        ones = sb("ones", [P, P])
        st2 = sb("st2", [P, 2, NT, 6])
        mv2 = sb("mv2", [P, 2, NT, 2])
        rstd2 = sb("rstd2", [P, 2, NT])
        root2 = sb("root2", [P, 2, 3, NT])
        iota_f = sb("iota_f", [P, ROUTED + E])
        kept = split_area[:, E * HR:5 * 1024]
        weight = kept[:, 0:2 * TILES].rearrange("p (k t) -> p k t", k=2)
        slot_i = kept[:, 2 * TILES:4 * TILES].bitcast(I32).rearrange("p (t k) -> p t k", k=2)
        etile = kept[0:1, 4 * TILES:4 * TILES + ROUTED].bitcast(I32)
        place_cur = sb("place_cur", [P, 4], I32)
        weight_cur = sb("weight_cur", [P, 4])
        tag = sb("tag", [P, 2 * TILES])
        tags = tag[:, :].rearrange("p (k t) -> p k t", k=2)
        idx_cur = sb("idx_cur", [P, 2, 2 * NT], I32)
        shift = sb("shift", [P, 2, NT])
        rden = sb("rden", [P, 2, NT, 4])
        ps = ctx.enter_context(nc.psum_tensor("ps", [P, 8, 512], F32))

        qk_dram = nc.dram_tensor("qk_dram", [2, B * HEADS, QK_ROWS, T], BF16).ap()
        be1_dram = nc.dram_tensor("be1_dram", [3, E * 2 * HR], BF16).ap()
        be2_dram = nc.dram_tensor("be2_dram", [3, E * C], BF16).ap()
        xs_dram = nc.dram_tensor("xs_dram", [ROUTED * P, ROW], F32).ap()
        ys_dram = nc.dram_tensor("ys_dram", [(2 * TILES + ROUTED) * P, C], F32).ap()
        m_dram = nc.dram_tensor("m_dram", [4, 3, 2, 2 * T], BF16).ap()

        s_x = sem("x_loaded"); s_w = sem("w_loaded")
        s_const = sem("const_ready"); s_pstep = sem("pool_step")
        s_latT = sem("latT_done"); s_latT_sb = sem("latT_copied"); s_wmul = sem("w_multiplied"); s_wsb = sem("w_ready")
        s_stats = sem("ln_stats"); s_seed = sem("ln_seed"); s_newton = sem("ln_newton"); s_xn = sem("xn_ready")
        s_xT = sem("xT_done"); s_xT_sb = sem("xnT_ready")
        s_qkp = sem("qk_projected"); s_vp = sem("v_projected"); s_vsb = sem("v_ready")
        s_p1 = sem("part1_ready"); s_r = sem("rest_ready"); s_p2 = sem("part2_ready"); s_p3 = sem("part3_ready")
        s_parts = [sem("parts_stored0"), sem("parts_stored1")]
        s_qk = [sem(f"qk_loaded{n}") for n in range(4)]
        s_m = [sem(f"m_loaded{n}") for n in range(4)]
        s_mw = sem("m_stored")
        s_rot = sem("rot_filled"); s_rotf = sem("rot_freed")
        s_msplit = sem("m_split")
        s_st = sem("scoresT_filled"); s_exp = sem("exp_done"); s_pv = sem("pv_done"); s_outT = sem("outT_ready")
        s_rden = sem("rden_ready"); s_y = sem("y_ready"); s_vcur = sem("v_cur_ready")
        s_done = sem("out_stored")
        s_passed = sem("waits_passed")
        s_zset = sem("zeros_set"); s_zero = sem("rows_zeroed")
        s_w2 = sem("small_weights_loaded"); s_be = sem("be_split"); s_bew = sem("be_stored"); s_ber = sem("be_rows_loaded")
        s_we = sem("expert_weights_loaded")
        s_ycur = sem("ycur_ready"); s_yT = sem("yT_done"); s_yTsb = sem("yT_ready"); s_proj = sem("projected")
        s_a = sem("a_ready"); s_stA = sem("statsA"); s_seedA = sem("seedA"); s_newtA = sem("newtonA"); s_x1 = sem("x1_ready")
        s_res = sem("residual_steps"); s_st2 = sem("stats2")
        s_seedB = sem("seedB"); s_newtB = sem("newtonB"); s_xn2 = sem("xn2_ready")
        s_xT2 = sem("xT2_done"); s_xT2sb = sem("xT2_ready"); s_lg = sem("logits_done"); s_lgsb = sem("logits_ready")
        s_hg = sem("shared_g_done"); s_gel = sem("shared_gelu_ready"); s_ha = sem("shared_a_done"); s_hid = sem("shared_hidden_ready")
        s_y2 = sem("shared_y_done"); s_ysum = sem("shared_y_ready")
        s_rt = sem("routing_step"); s_pref = sem("prefixes_done"); s_exw = sem("exp_of_difference")
        s_rows = sem("rows_staged"); s_idx = sem("slots_staged"); s_scat = [sem(f"rows_scattered{n}") for n in range(2)]
        s_xs = [sem(f"xs_loaded{n}") for n in range(4)]
        s_xsT = sem("xsT_done"); s_xsTsb = sem("xsT_ready"); s_he = sem("expert_h_done"); s_ge = sem("expert_gelu_ready")
        s_hide = sem("expert_hidden_ready"); s_hT = sem("expert_hiddenT_done"); s_hTsb = sem("expert_hiddenT_ready")
        s_ye = sem("expert_y_done"); s_yesb = sem("expert_y_ready"); s_yst = [sem(f"ys_stored{n}") for n in range(2)]
        s_tag = sem("tags_read"); s_sum = sem("routed_sums"); s_shift = sem("shift_ready"); s_normal = sem("normalised"); s_pick = [sem(f"rows_picked{n}") for n in range(2)]
        s_comb = sem("combine_steps"); s_st3 = sem("stats3"); s_seedC = sem("seedC"); s_newtC = sem("newtonC"); s_fin = sem("final_steps")
        s_out = [sem(f"out_stored{n}") for n in range(2)]

        ROT_ALL = ROT_BASE[LAST] + len(rot_items(LAST))
        SKEW = 3

        def skewed(engine, step):
            for n in range(SKEW + 3):
                step(n, n)
            with engine.Fori(0, (B - SKEW - 3) // 2) as it:
                for k in range(2):
                    step(SKEW + 3 + k, 2 * it + (SKEW + 3 + k))
            for n in range(B, B + SKEW):
                step(n, n)

        def col(t, k, b):
            return t[:, k, b:b + 1] if isinstance(b, int) else t[:, k, bass.ds(b, 1)]

        def quad_steps(engine, step):
            for g in range(FIRST, 4):
                step(g, g)
            with engine.Fori(1, B - 1) as it:
                for q in range(4):
                    step(4 + q, 4 * it + q)
            for g in range(4 * (B - 1), LAST + 1):
                step(g, g)

        def batches(engine, first, step):
            first()
            with engine.Fori(0, B // 2 - 1) as it:
                for par in range(2):
                    step(par, 2 * it + par, True)
            for b in (B - 2, B - 1):
                step(b % 2, b, b + 1 < B)

        def tiles_by_four(engine, step):
            for n in range(8):
                step(n, n)
            with engine.Fori(2, ROUTED // 4 - 1) as it:
                for k in range(4):
                    step(8 + k, 4 * it + k)
            for n in range(ROUTED - 4, ROUTED + 2):
                step(n, n)

        def combine_steps(engine, step):
            for n in range(4):
                step(n, n)
            with engine.Fori(0, B // 2 - 3) as it:
                for k in range(2):
                    step(4 + k, 2 * it + 4 + k)
            for n in range(B - 2, B + 1):
                step(n, n)

        def tiles4(t, b):
            return t[:, 4 * b:4 * b + 4, :] if isinstance(b, int) else t[:, bass.ds(4 * b, 4), :]

        blanks, first = [], 0
        for memory in (y_sb[:].rearrange("p t c -> p (t c)"), pT_area[:, :]):
            n = min(memory.shape[-1] // ROW, ROUTED - first)
            blanks.append((memory[:, 0:n * ROW].rearrange("p (r c) -> p r c", c=ROW), first, n))
            first += n
        assert first == ROUTED

        block = ctx.enter_context(nc.Block())

        @block.sync
        def _(sp):
            for n, name in enumerate(("L0_attn_wq_lat", "L0_attn_wk_lat", "L0_attn_wv_lat")):
                sp.dma_start(lat_in[:, n, :], a[name]).then_inc(s_w, 16)
            for n, name in enumerate(("L0_attn_wq_heads", "L0_attn_wk_heads", "L0_attn_wv_heads")):
                sp.dma_start(heads_in[:, n, :], a[name]).then_inc(s_w, 16)
            small_loads = [
                (w_proj[:], a["L0_attn_w_proj"]), (w_r[:], a["L0_ffn_Wr"]), (ws1[:], a["L0_ffn_Ws1"]),
                (ws2[:], a["L0_ffn_Ws2"].rearrange("(k p) d -> p k d", p=P)),
                (b_proj[:], rows_of(a["L0_attn_b_proj"], C)), (b_s2[:], rows_of(a["L0_ffn_bs2"], C)),
                (b_r[:], rows_of(a["L0_ffn_br"], E)), (b_s1[:], a["L0_ffn_bs1"].rearrange("(k p) -> p k", p=P)),
                (be_in[:, 0:72], a["L0_ffn_be1"].rearrange("e h -> (e h)").rearrange("(p x) -> p x", p=P)),
                (be_in[:, 72:84], a["L0_ffn_be2"].rearrange("e h -> (e h)").rearrange("(p x) -> p x", p=P))]
            for n in range(4):
                sp.dma_start(x_sb[:, 16 * n:16 * n + 16, :],
                             a["L0_attn_x"][4 * n:4 * n + 4].rearrange("b (t p) c -> p (b t) c", p=P)).then_inc(s_x, 16)

            for to, what in small_loads:
                sp.dma_start(to, what, allow_slow_non_contiguous=True).then_inc(s_w2, 16)
            sp.wait_ge(s_zset, 1)
            for blank, first, n in blanks:
                sp.dma_start(xs_dram[first * P:(first + n) * P].rearrange("(r p) c -> p r c", p=P), blank).then_inc(s_zero, 16)
            sp.wait_ge(s_be, 4)
            sp.dma_start(be1_dram.rearrange("n (p x) -> p n x", p=P), be_part[:, :, 0:72]).then_inc(s_bew, 16)
            sp.dma_start(be2_dram.rearrange("n (p x) -> p n x", p=P), be_part[:, :, 72:84]).then_inc(s_bew, 16)
            sp.wait_ge(s_bew, 32)

            def store_parts(par, b, more):
                rows = [qk_dram[s, bass.ds(HEADS * b, HEADS)].rearrange("h (j d) t -> j h d t", j=6) for s in range(2)]
                for part_n, sem_ready in ((0, s_p1), (1, s_p2), (2, s_p3)):
                    sp.wait_ge(sem_ready, 2 * b + 2)
                    for s, slots in ((0, Q_SLOTS), (1, K_SLOTS)):
                        for j in range(6):
                            if slots[j] == part_n:
                                sp.dma_start(rows[s][j], part[:, par, s, part_n, :]).then_inc(s_parts[par], 16)

            batches(sp, lambda: None, store_parts)
            for par in range(2):
                sp.wait_ge(s_parts[par], 12 * 16 * B // 2)

            def load_quad(slot, h):
                for s in range(2):
                    for hp in range(2):
                        sp.dma_start(qk[64 * hp:64 * hp + QK_ROWS, slot, s],
                                     qk_dram[s, bass.ds(4 * h + 2 * hp, 2)].rearrange("r p t -> p r t")
                                     ).then_inc(s_qk[slot], 16)

            def step(gs, g):
                if gs + 3 < QUADS:
                    ge(sp, s_st, 5 * g)
                    slot = (gs + 3) % 4
                    load_quad(slot, g + 3)
                if 0 <= gs + 1 < QUADS:
                    slot = (gs + 1) % 4
                    sp.wait_ge(s_rotf, rot_base(gs, g) + rot_items(gs).index(("max_rows", 0)) + 1)
                    sp.dma_start(m_dram[slot].rearrange("n h (x q) -> (n h x) q", q=P),
                                 mT_sb[:, (gs + 1) % 2, :]).then_inc(s_mw, 16)
                    sp.wait_ge(s_mw, 16 * (g + 2))
                    for hp in range(2):
                        sp.dma_start(qk[64 * hp + QK_ROWS:64 * hp + ROWS, slot, 0].rearrange("p r t -> p (r t)"),
                                     m_dram[slot, :, hp]).then_inc(s_m[slot], 16)

            sp.wait_ge(s_const, 1)
            load_quad(0, 0)
            quad_steps(sp, step)

            sp.wait_ge(s_st, 5 * QUADS)
            sp.wait_ge(s_pv, QUADS)
            sp.dma_start(be1r, be1_dram).then_inc(s_ber, 16)
            sp.dma_start(be2r, be2_dram).then_inc(s_ber, 16)
            for e in range(E):
                sp.dma_start(we2[:, e * HR:(e + 1) * HR].rearrange("p (k d) -> p k d", k=3),
                             a["L0_ffn_We2"][e].rearrange("(k p) d -> p k d", p=P)).then_inc(s_we, 16)
            sp.wait_ge(s_rt, ROUTING_STEPS)
            for e in range(E):
                sp.dma_start(we1[:, e * 2 * HR:(e + 1) * 2 * HR], a["L0_ffn_We1"][e]).then_inc(s_we, 16)
            for par in range(2):
                sp.wait_ge(s_scat[par], 16 * 2 * NT * B // 2)

            def load_rows(ring, j):
                sp.dma_start(xs[:, ring, :], xs_dram[bass.ds(j * P, P), :]).then_inc(s_xs[ring], 16)

            for j in range(3):
                load_rows(j, j)

            def expert_tile(ns, n):
                if ns + 3 < ROUTED:
                    if ns > 0:
                        wait_apart(sp, s_xsT, n, s_passed)
                        sp.wait_ge(s_tag, 2 * n)
                    load_rows((ns + 3) % 4, n + 3)

            tiles_by_four(sp, expert_tile)
            for par in range(2):
                sp.wait_ge(s_yst[par], 16 * ROUTED // 2)

            def pick(par, n):
                for k in range(2):
                    sp.dma_start(picked[:, par, k], ys_dram[bass.ds((k * TILES + NT * n) * P, NT * P)]
                                 .rearrange("(t p) c -> p t c", p=P)).then_inc(s_pick[par], 16)

            for n in range(2):
                pick(n, n)

            def store(ns, n):
                if 0 <= ns - 1 < B:
                    par = (ns - 1) % 2
                    if ns + 1 < B:
                        wait_apart(sp, s_comb, n, s_passed)
                        pick(par, n + 1)
                    sp.wait_ge(s_fin, n)
                    sp.dma_start(out[bass.ds(n - 1, 1)].rearrange("b (t p) c -> p (b t) c", p=P), final[:, par]).then_inc(s_out[par], 16)

            combine_steps(sp, store)
            for par in range(2):
                sp.wait_ge(s_out[par], 16 * B // 2)

        @block.gpsimd
        def _(pool):
            n = 0

            def chain(ins):
                nonlocal n
                n += 1
                ins.then_inc(s_pstep, 1)
                pool.wait_ge(s_pstep, n)

            for blank, _, _ in blanks:
                pool.memset(blank, 0.0)
            pool.iota(tag_i[:, 0:ROUTED], pattern=[[P, ROUTED]], base=2 * TILES * P, channel_multiplier=1)
            chain(pool.iota(tag_i[:, ROUTED:], pattern=[[TILES * P, 2], [P, TILES]], base=0, channel_multiplier=1))
            for blank, first, n_ in blanks:
                last = pool.tensor_copy(blank[:, :, PLACE], tag_i[:, first:first + n_].rearrange("p (r o) -> p r o", o=1))
            last.then_inc(s_zset, 1)
            pool.tensor_copy(tag[:], tag_i[:, ROUTED:])
            pool.memset(ident[:], 0.0)
            pool.memset(before[:], 1.0)
            pool.memset(ones[:], 1.0)
            pool.memset(ones_bf[:], 1.0)
            pool.iota(iota_i[:, 0:ROUTED], pattern=[[1, ROUTED]], base=0, channel_multiplier=0)
            pool.iota(iota_i[:, ROUTED:], pattern=[[1, E]], base=-int(FAR), channel_multiplier=0)
            pool.memset(mask_q[:], 0.0)
            pool.memset(mask_k[:], 0.0)
            pool.memset(qk[:], 1.0)
            chain(pool.memset(v_cur[:], 0.0))
            pool.memset(v_cur[:, :, :, :, HD:HD + 1], 1.0)
            chain(pool.affine_select(out=ident[:], in_=ident[:], compare_op=ALU.not_equal, fill=1.0, base=0,
                                     pattern=[[-1, P]], channel_multiplier=1))
            pool.affine_select(out=before[:], in_=before[:], compare_op=ALU.is_gt, fill=0.0, base=0,
                               pattern=[[1, P]], channel_multiplier=-1)
            pool.tensor_copy(iota_f[:], iota_i[:])
            pool.affine_select(out=mask_q[:], in_=mask_q[:], compare_op=ALU.is_ge, fill=MASKED, base=0,
                               pattern=[[-1, P]], channel_multiplier=1)
            pool.affine_select(out=mask_k[:], in_=mask_k[:], compare_op=ALU.is_ge, fill=MASKED, base=0,
                               pattern=[[1, P]], channel_multiplier=-1)
            pool.tensor_copy(ident_bf[:], ident[:]).then_inc(s_const, 1)

            def ln_rstd(par, b):
                pool.wait_ge(s_seed, SEED_OPS * (b + 1))
                newton(pool, s_passed, s_newton, NEWTON_OPS * b, rstd[:, par, :], root[:, par, 0, :], root[:, par, 2, :])

            def third_parts(par, b, more):
                if more:
                    ln_rstd(1 - par, b + 1)
                for s in range(2):
                    pool.wait_ge(s_p2, 2 * b + s + 1)
                    pool.tensor_tensor(part[:, par, s, 2, :], rest[:, par, s, :], part[:, par, s, 1, :],
                                       ALU.subtract).then_inc(s_p3, 1)

            batches(pool, lambda: ln_rstd(0, 0), third_parts)

            def step(gs, g):
                if not 0 <= gs + 1 < QUADS:
                    return
                ge(pool, s_pv, g - 2)
                q = (gs + 1) % 4
                if isinstance(g, int):
                    first = 4 * ((g + 1) // 4)
                    src = v_all[:, first:first + 4, 32 * q:32 * q + 32]
                else:
                    src = v_all[:, bass.ds(g + 1 - q, 4), 32 * q:32 * q + 32]
                pool.tensor_copy(v_cur[:, q, :, :, 0:HD], src.rearrange("p t (h d) -> p t h d", d=HD)).then_inc(s_vcur, 1)

            pool.wait_ge(s_vsb, B)
            quad_steps(pool, step)

            def roots(ns, n):
                if 0 <= ns < B:
                    par = ns % 2
                    pool.wait_ge(s_seedA, SEED_OPS * (n + 1))
                    newton(pool, s_passed, s_newtA, NEWTON_OPS * n, rstd[:, par, :], root[:, par, 0, :], root[:, par, 2, :])
                if 0 <= ns - 1 < B:
                    par = (ns - 1) % 2
                    pool.wait_ge(s_seedB, SEED_OPS * n)
                    newton(pool, s_passed, s_newtB, NEWTON_OPS * (n - 1), rstd2[:, par, :], root2[:, par, 0, :], root2[:, par, 2, :])

            skewed(pool, roots)
            pool.wait_ge(s_zero, 32)

            def scatter(par, b):
                pool.wait_ge(s_rows, b + 1)
                wait_apart(pool, s_idx, b + 1, s_passed)
                for t in range(NT):
                    for k in range(2):
                        at = bass.IndirectOffsetOnAxis(ap=idx_cur[:, par, 2 * t + k:2 * t + k + 1], axis=0)
                        pool.indirect_dma_start(xs_dram, at, rows_cur[k][:, par, t, :], None).then_inc(s_scat[par], 16)

            with pool.Fori(0, B // 2) as it:
                for par in range(2):
                    scatter(par, 2 * it + par)

            def expert_tile(ns, n):
                if ns < ROUTED:
                    pool.wait_ge(s_xs[ns % 4], 16 * (n // 4 + 1) if isinstance(n, int) else 4 * (n - ns % 4) + 16)
                    if ns >= 4:
                        wait_apart(pool, s_yst[ns % 2], 8 * (n - ns % 2) - 16, s_passed)
                    pool.tensor_copy(place_cur[:, ns % 4:ns % 4 + 1], xs[:, ns % 4, PLACE]).then_inc(s_tag, 1)
                    pool.tensor_copy(weight_cur[:, ns % 4:ns % 4 + 1], xs[:, ns % 4, WEIGHT]).then_inc(s_tag, 1)
                if 0 <= ns - 2:
                    pool.wait_ge(s_tag, 2 * n - 2)
                    wait_apart(pool, s_yesb, n - 1, s_passed)
                    at = bass.IndirectOffsetOnAxis(ap=place_cur[:, (ns - 2) % 4:(ns - 2) % 4 + 1], axis=0)
                    pool.indirect_dma_start(ys_dram, at, ys[:, ns % 2, :], None).then_inc(s_yst[ns % 2], 16)

            tiles_by_four(pool, expert_tile)

            def sums(ns, n):
                if 0 <= ns < B:
                    par = ns % 2
                    pool.wait_ge(s_pick[par], 32 * (n // 2 + 1) if isinstance(n, int) else 16 * (n - par) + 32)
                    ge(pool, s_fin, n - 1)
                    pool.tensor_tensor(summed[:, par], picked[:, par, 0], picked[:, par, 1], ALU.add).then_inc(s_sum, 1)
                if 0 <= ns - 1 < B:
                    par = (ns - 1) % 2
                    pool.wait_ge(s_seedC, SEED_OPS * n)
                    newton(pool, s_passed, s_newtC, NEWTON_OPS * (n - 1), rstd[:, par, :], root[:, par, 0, :], root[:, par, 2, :])

            combine_steps(pool, sums)

        @block.scalar
        def _(act):
            act.wait_ge(s_latT, 1)
            act.activation(latT[:], ps[0:LAT, 0, 0:3 * P].rearrange("p (n c) -> p n c", n=3), ACT.Copy).then_inc(s_latT_sb, 1)
            act.wait_ge(s_wmul, 1)
            act.activation(w_qkv[:, 0, :], ps[:, 1, 0:C], ACT.Copy, scale=float(HD) ** -0.5)
            act.activation(w_qkv[:, 1:3, :], ps[:, 1, C:3 * C].rearrange("p (n c) -> p n c", n=2), ACT.Copy).then_inc(s_wsb, 1)

            def copy_xT(par, b):
                act.wait_ge(s_xT, b + 1)
                ge(act, s_vp, b - 1)
                act.activation(xnT[:, par, :], ps[:, par, :], ACT.Copy).then_inc(s_xT_sb, 1)

            def first_parts(par, b, more):
                if more:
                    copy_xT(1 - par, b + 1)
                if isinstance(b, int):
                    if b >= 2:
                        act.wait_ge(s_parts[par], 12 * 16 * (b // 2))
                for s in range(2):
                    act.wait_ge(s_qkp, 2 * b + s + 1)
                    act.activation(part[:, par, s, 0, :], ps[:, 2 + 2 * s + par, :], ACT.Copy).then_inc(s_p1, 1)
                for s in range(2):
                    act.wait_ge(s_r, 2 * b + s + 1)
                    act.activation(part[:, par, s, 1, :], rest[:, par, s, :], ACT.Copy).then_inc(s_p2, 1)

            copy_xT(0, 0)
            for b in (0, 1):
                first_parts(b, b, True)
            with act.Fori(1, B // 2 - 1) as it:
                for par in range(2):
                    act.wait_ge(s_parts[par], 12 * 16 * it)
                    first_parts(par, 2 * it + par, True)
            for b in (B - 2, B - 1):
                first_parts(b % 2, b, b + 1 < B)

            def step(gs, g):
                for n in range(5):
                    if n == 4 and 0 <= gs - 1 < QUADS:
                        act.wait_ge(s_pv, g)
                        if gs - 3 >= 0:
                            pos = rot_items(gs - 1).index(("turn_back", 0))
                            act.wait_ge(s_rot, rot_base(gs - 1, g - 1) + pos + 1)
                        act.activation(outT[:, (gs - 1) % 2, :], ps[:, 6 + (gs - 1) % 2, :], ACT.Copy).then_inc(s_outT, 1)
                    if 0 <= gs < QUADS:
                        act.wait_ge(s_st, 5 * g + n + 1)
                        if n == 0:
                            ge(act, s_pv, g - 1)
                        u = 2 + 2 * ((5 * gs + n) % 2)
                        act.activation(pT[:, gs % 2, n, :], ps[:, u:u + 2, :].rearrange("p a b -> p (a b)"),
                                       ACT.Exp).then_inc(s_exp, 1)

            act.wait_ge(s_zero, 32)
            act.wait_ge(s_bew, 32)
            quad_steps(act, step)

            act.wait_ge(s_w2, 160)
            act.wait_ge(s_rotf, ROT_ALL)

            def shared(ns, n):
                if 0 <= ns < B:
                    par = ns % 2
                    ge(act, s_yT, n - 1)
                    act.activation(ycur[:, par], tiles4(y_sb, n), ACT.Copy).then_inc(s_ycur, 1)
                if 0 <= ns - SKEW < B:
                    par, b = (ns - SKEW) % 2, n - SKEW
                    act.wait_ge(s_xT2, b + 1)
                    ge(act, s_ha, 2 * b - 2)
                    act.activation(xT2[:, par, :], ps[:, 0, :], ACT.Copy).then_inc(s_xT2sb, 1)
                    act.activation(tiles4(v_all, b), xn2[:, par], ACT.Copy).then_inc(s_y, 1)
                    for j in range(2):
                        act.wait_ge(s_hg, 2 * b + j + 1)
                        ge(act, s_hid, 2 * b + j - 1)
                        act.activation(gel[:, j, :], ps[:, 4 + 2 * j, :], ACT.Gelu, bias=b_s1[:, 2 + j:3 + j]).then_inc(s_gel, 1)
                if 0 <= ns < B:
                    par = ns % 2
                    act.wait_ge(s_yT, n + 1)
                    ge(act, s_proj, n - 1)
                    act.activation(yT[:, par, :], ps[:, 0, :], ACT.Copy).then_inc(s_yTsb, 1)

            skewed(act, shared)
            act.wait_ge(s_rt, DIFFERENCE_STEP)
            act.activation(top[:, 4, :], top[:, 3, :], ACT.Exp, scale=1.0 / TAU).then_inc(s_exw, 1)
            act.wait_ge(s_y, B)
            act.wait_ge(s_rt, ROUTING_STEPS)

            def stage_rows(par, b):
                for k in range(2):
                    act.activation(rows_cur[k][:, par, :, VALUES], tiles4(v_all, b), ACT.Copy)
                    for to, table in ((PLACE, tags), (WEIGHT, weight)):
                        t4 = table[:, k, 4 * b:4 * b + 4] if isinstance(b, int) else table[:, k, bass.ds(4 * b, 4)]
                        last = act.activation(rows_cur[k][:, par, :, to], t4.rearrange("p (t o) -> p t o", o=1), ACT.Copy)
                last.then_inc(s_rows, 1)

            for b in range(2):
                stage_rows(b, b)
            with act.Fori(1, B // 2) as it:
                for par in range(2):
                    act.wait_ge(s_scat[par], 16 * 2 * NT * it)
                    stage_rows(par, 2 * it + par)

            def copy_xsT(ns, n):
                act.wait_ge(s_xsT, n + 1)
                ge(act, s_he, 2 * n - 2)
                act.activation(xsT[:, ns % 2, :], ps[:, ns % 2, 0:C], ACT.Copy).then_inc(s_xsTsb, 1)

            def expert_tile(ns, n):
                if ns < ROUTED:
                    act.wait_ge(s_he, 2 * n + 1)
                    ge(act, s_hide, n - 1)
                    act.activation(gelE[:, ns % 2, :], ps[:, 2 + ns % 2, 0:HR], ACT.Gelu).then_inc(s_ge, 1)
                if ns + 1 < ROUTED:
                    copy_xsT(ns + 1, n + 1)
                if 0 <= ns - 1 < ROUTED:
                    par = (ns - 1) % 2
                    act.wait_ge(s_hT, n)
                    ge(act, s_ye, n - 2)
                    act.activation(hidT[:, par, :], ps[:, 6 + par, 0:HR], ACT.Copy).then_inc(s_hTsb, 1)

            copy_xsT(0, 0)
            tiles_by_four(act, expert_tile)

            def normalise(ns, n):
                if 0 <= ns - 1 < B:
                    par, b = (ns - 1) % 2, n - 1
                    act.wait_ge(s_shift, n)
                    ge(act, s_out[par], 8 * (b - par))
                    for t in range(NT):
                        last = act.activation(final[:, par, t, :], summed[:, par, t, :], ACT.Identity,
                                              scale=rstd[:, par, t:t + 1], bias=shift[:, par, t:t + 1])
                    last.then_inc(s_normal, 1)

            combine_steps(act, normalise)

        @block.tensor
        def _(pe):
            pe.wait_ge(s_const, 1)
            pe.wait_ge(s_w, 6 * 16)
            for n in range(3):
                last = pe.transpose(ps[0:LAT, 0, n * P:(n + 1) * P], lat_in[:, n, :], ident[:])
            last.then_inc(s_latT, 1)
            pe.wait_ge(s_latT_sb, 1)
            for n in range(3):
                last = pe.matmul(ps[:, 1, n * C:(n + 1) * C], latT[:, n, :], heads_in[:, n, :], start=True, stop=True)
            last.then_inc(s_wmul, 1)
            pe.wait_ge(s_wsb, 1)

            def turn_x(par, b):
                pe.wait_ge(s_xn, b + 1)
                ge(pe, s_xT_sb, b - 1)
                for t in range(NT):
                    last = pe.transpose(ps[:, par, t * P:(t + 1) * P], xn[:, par, t, :], ident[:])
                last.then_inc(s_xT, 1)

            def project(par, b, more):
                if more:
                    turn_x(1 - par, b + 1)
                pe.wait_ge(s_xT_sb, b + 1)
                ge(pe, s_r, 2 * b - 2)
                for s in range(2):
                    pe.matmul(ps[:, 2 + 2 * s + par, :], w_qkv[:, s, :], xnT[:, par, :], start=True, stop=True).then_inc(s_qkp, 1)
                ge(pe, s_vsb, b - 1)
                for t in range(NT):
                    last = pe.matmul(ps[:, 6 + par, t * C:(t + 1) * C], xnT[:, par, t * P:(t + 1) * P], w_qkv[:, 2, :],
                                     start=True, stop=True)
                last.then_inc(s_vp, 1)

            turn_x(0, 0)
            project(0, 0, True)
            project(1, 1, True)
            with pe.Fori(1, B // 2 - 1) as it:
                for par in range(2):
                    project(par, 2 * it + par, True)
            for b in (B - 2, B - 1):
                project(b % 2, b, b + 1 < B)
            pe.wait_ge(s_r, 2 * B)
            pe.wait_ge(s_vsb, B)

            def rows(i, part_of_q, lo, hi, slot, k):
                base = 64 * (i // 2)
                return qk[base:base + k, slot, part_of_q, i % 2, lo:hi]

            def rot(gs, g, pos, kind, n):
                index = rot_base(gs, g) + pos
                bank = (rot_base(gs, gs) + pos) % 2
                ge(pe, s_rotf, index - 1)
                if kind == "scores":
                    slot = (gs + 2) % 4
                    if n == 0:
                        pe.wait_ge(s_qk[slot], 16 * (g + 2 - slot) + 64)
                    pr, j = divmod(n, 5)
                    if j < 4:
                        i = 2 * pr + j // 2
                        places = [(i, 3, 0)] if j % 2 == 0 else [(i, 2, 0), (i, 0, 384)]
                    else:
                        places = [(2 * pr, 1, 0), (2 * pr + 1, 1, 256)]
                    for i, qt, at in places:
                        w = (qt + 1) * P
                        pe.matmul(ps[:, bank, at:at + w], rows(i, 0, qt * P, qt * P + P, slot, QK_ROWS),
                                  rows(i, 1, 0, w, slot, QK_ROWS), start=True, stop=False)
                        last = pe.matmul(ps[:, bank, at + w - P:at + w], ident_bf[:], mask_q[:], start=False, stop=True)
                elif kind == "max_rows":
                    wait_apart(pe, s_msplit, 4 * (g + 2), s_passed)
                    last = pe.transpose(ps[0:48, bank, 0:64].bitcast(BF16), m_part[:, (gs + 1) % 2].rearrange("p n x -> p (n x)"),
                                        ident_bf[:])
                else:
                    pe.wait_ge(s_outT, g - 1)
                    for qt in range(NT):
                        last = pe.transpose(ps[:, bank, qt * P:(qt + 1) * P], outT[:, gs % 2, qt * P:(qt + 1) * P], ident[:])
                last.then_inc(s_rot, 1)

            def scores_by_key(gs, g, n, half):
                u = 2 + 2 * ((5 * gs + n) % 2) + half
                slot = gs % 4
                if half == 0:
                    ge(pe, s_exp, 5 * g + n - 1)
                    if n == 0:
                        pe.wait_ge(s_m[slot], 8 * (g - slot) + 32)
                if n < 4:
                    places = [(n, 0, 0)] if half == 0 else [(n, 1, 0), (n, 3, 384)]
                else:
                    places = [(2 * half, 2, 0), (2 * half + 1, 2, 256)]
                for i, kb, at in places:
                    w = T - kb * P
                    pe.matmul(ps[:, u, at:at + w], rows(i, 1, kb * P, kb * P + P, slot, ROWS),
                              rows(i, 0, kb * P, T, slot, ROWS), start=True, stop=False)
                    last = pe.matmul(ps[:, u, at:at + P], ident_bf[:], mask_k[:], start=False, stop=True)
                if half == 1:
                    last.then_inc(s_st, 1)

            def products(gs, g, kb):
                buf, slot = (gs - 1) % 2, (gs - 1) % 4
                if kb == 0:
                    pe.wait_ge(s_exp, 5 * g)
                    pe.wait_ge(s_vcur, g)
                    ge(pe, s_outT, g - 2)
                w = T - kb * P
                for i in range(4):
                    at = i * 1024 + (0, 512, 0, 896)[kb] if kb != 2 else 4 * 1024 + i * 256
                    flat = pT[:, buf].rearrange("p n t -> p (n t)")
                    last = pe.matmul(ps[32 * i:32 * i + 32, 6 + buf, kb * P:T], v_cur[:, slot, kb, i, :], flat[:, at:at + w],
                                     start=(kb == 0), stop=(kb == 3))
                if kb == 3:
                    last.then_inc(s_pv, 1)

            def step(gs, g):
                items = rot_items(gs)
                todo = list(enumerate(items))

                def some(k):
                    for _ in range(k):
                        if todo:
                            pos, (kind, n) = todo.pop(0)
                            rot(gs, g, pos, kind, n)

                for n in range(5):
                    if 0 <= gs < QUADS:
                        scores_by_key(gs, g, n, 0)
                    some(1)
                    if 0 <= gs < QUADS:
                        scores_by_key(gs, g, n, 1)
                    some(1)
                    if n < 4 and 0 <= gs - 1 < QUADS:
                        products(gs, g, n)
                    if n in (1, 3):
                        some(1)
                some(12)

            quad_steps(pe, step)

            pe.wait_ge(s_w2, 160)
            pe.wait_ge(s_rotf, ROT_ALL)
            pe.wait_ge(s_outT, QUADS)

            def shared(ns, n):
                if 0 <= ns - SKEW < B:
                    par, b = (ns - SKEW) % 2, n - SKEW
                    pe.wait_ge(s_xn2, b + 1)
                    if ns - 1 < B:
                        pe.wait_ge(s_yTsb, n)
                    else:
                        pe.wait_ge(s_yTsb, B)
                        pe.wait_ge(s_xT2sb, b)
                    for t in range(NT):
                        last = pe.transpose(ps[:, 0, t * P:(t + 1) * P], xn2[:, par, t, :], ident[:])
                    last.then_inc(s_xT2, 1)
                    pe.wait_ge(s_xT2sb, b + 1)
                    ge(pe, s_lgsb, b)
                    for t in range(NT):
                        last = pe.matmul(ps[:, 3, t * E:(t + 1) * E], xT2[:, par, t * P:(t + 1) * P], w_r[:],
                                         start=True, stop=True)
                    last.then_inc(s_lg, 1)
                    for j in range(2):
                        ge(pe, s_gel, 2 * b + j - 1)
                        pe.matmul(ps[:, 4 + 2 * j, :], ws1[:, HS + j * P:HS + (j + 1) * P], xT2[:, par, :],
                                  start=True, stop=True).then_inc(s_hg, 1)
                        ge(pe, s_hid, 2 * b + j - 1)
                        pe.matmul(ps[:, 5 + 2 * j, :], ws1[:, j * P:(j + 1) * P], xT2[:, par, :],
                                  start=True, stop=True).then_inc(s_ha, 1)
                if 0 <= ns < B:
                    par = ns % 2
                    pe.wait_ge(s_ycur, n + 1)
                    if ns - SKEW >= 0:
                        pe.wait_ge(s_xT2sb, n - SKEW + 1)
                    else:
                        ge(pe, s_yTsb, n)
                    for t in range(NT):
                        last = pe.transpose(ps[:, 0, t * P:(t + 1) * P], ycur[:, par, t, :], ident[:])
                    last.then_inc(s_yT, 1)
                    pe.wait_ge(s_yTsb, n + 1)
                    ge(pe, s_a, n)
                    for t in range(NT):
                        last = pe.matmul(ps[:, 1, t * C:(t + 1) * C], yT[:, par, t * P:(t + 1) * P], w_proj[:],
                                         start=True, stop=True)
                    last.then_inc(s_proj, 1)
                if 0 <= ns - SKEW < B:
                    b = n - SKEW
                    pe.wait_ge(s_hid, 2 * b + 2)
                    ge(pe, s_ysum, b)
                    for t in range(NT):
                        for j in range(2):
                            last = pe.matmul(ps[:, 2, t * C:(t + 1) * C], hid[:, j, t * P:(t + 1) * P], ws2[:, j, :],
                                             start=(j == 0), stop=(j == 1))
                    last.then_inc(s_y2, 1)

            skewed(pe, shared)

            pe.wait_ge(s_rt, BOTH_STEP)
            pe.wait_ge(s_ysum, B)
            flat = both.rearrange("p t e -> p (t e)")
            half = TILES * E // 2
            for k in range(2):
                pe.matmul(ps[:, k, 0:half], before[:], flat[:, k * half:(k + 1) * half], start=True, stop=True)
                last = pe.matmul(ps[:, 2 + k, 0:half], ones[:], flat[:, k * half:(k + 1) * half], start=True, stop=True)
            last.then_inc(s_pref, 1)

            pe.wait_ge(s_rt, ROUTING_STEPS)
            pe.wait_ge(s_we, 16 * 2 * E)
            pe.wait_ge(s_ber, 32)

            def turn_rows(ns, j):
                pe.wait_ge(s_xs[ns % 4], 16 * (j // 4 + 1) if isinstance(j, int) else 4 * (j - ns % 4) + 16)
                ge(pe, s_yesb, j - 3)
                pe.transpose(ps[:, ns % 2, 0:C], xs[:, ns % 4, VALUES], ident[:]).then_inc(s_xsT, 1)

            def expert_tile(ns, n):
                if ns < ROUTED:
                    par = ns % 2
                    e = pe.value_load(etile[0:1, bass.ds(n, 1)], min_val=0, max_val=E - 1)
                    pe.wait_ge(s_xsTsb, n + 1)
                    for k, bank in ((1, 2 + par), (0, 4 + par)):
                        ge(pe, s_ge if k else s_hide, n - 1)
                        pe.matmul(ps[:, bank, 0:HR], ones_bf[:], be1r[:, bass.ds(e * (2 * HR) + k * HR, HR)], start=True, stop=False)
                        pe.matmul(ps[:, bank, 0:HR], xsT[:, par, :], we1[:, bass.ds(e * (2 * HR) + k * HR, HR)],
                                  start=False, stop=True).then_inc(s_he, 1)
                if ns + 1 < ROUTED:
                    turn_rows(ns + 1, n + 1)
                if 0 <= ns - 1 < ROUTED:
                    par = (ns - 1) % 2
                    pe.wait_ge(s_hide, n)
                    ge(pe, s_hTsb, n - 2)
                    for k in range(3):
                        last = pe.transpose(ps[:, 6 + par, k * P:(k + 1) * P], hidE[:, par, k * P:(k + 1) * P], ident[:])
                    last.then_inc(s_hT, 1)
                if 0 <= ns - 2 < ROUTED:
                    par = ns % 2
                    e = pe.value_load(etile[0:1, bass.ds(n - 2, 1)], min_val=0, max_val=E - 1)
                    pe.wait_ge(s_hTsb, n - 1)
                    if ns >= ROUTED:
                        pe.wait_ge(s_yesb, n - 3)
                    pe.matmul(ps[:, par, 0:C], ones_bf[:], be2r[:, bass.ds(e * C, C)], start=True, stop=False)
                    for k in range(3):
                        last = pe.matmul(ps[:, par, 0:C], hidT[:, par, k * P:(k + 1) * P], we2[:, bass.ds(e * HR + k * P, P)],
                                         start=False, stop=(k == 2))
                    last.then_inc(s_ye, 1)

            turn_rows(0, 0)
            tiles_by_four(pe, expert_tile)

        @block.vector
        def _(dve):
            def norm_x(par, b):
                x4 = tiles4(x_sb, b)
                for t in range(NT):
                    last = dve.bn_stats(st[:, par, t, :], x4[:, t, :])
                last.then_inc(s_stats, 1)
                wait_apart(dve, s_stats, b + 1, s_passed)
                for t in range(NT):
                    last = dve.bn_aggr(mv[:, par, t, :], st[:, par, t, :])
                last.then_inc(s_seed, 1)
                seed(dve, s_seed, SEED_OPS * b + 1, rstd[:, par, :], root[:, par, 0, :], root[:, par, 1, :], mv[:, par, :, 1])
                dve.wait_ge(s_newton, NEWTON_OPS * (b + 1))
                ge(dve, s_xT, b - 1)
                for t in range(NT):
                    last = dve.tensor_scalar(xn[:, par, t, :], x4[:, t, :], mv[:, par, t, 0:1], rstd[:, par, t:t + 1],
                                             ALU.subtract, ALU.mult)
                last.then_inc(s_xn, 1)

            def rests(par, b, more):
                if more:
                    norm_x(1 - par, b + 1)
                for s in range(2):
                    dve.wait_ge(s_p1, 2 * b + s + 1)
                    ge(dve, s_p3, 2 * b + s - 3)
                    dve.tensor_tensor(rest[:, par, s, :], ps[:, 2 + 2 * s + par, :], part[:, par, s, 0, :],
                                      ALU.subtract).then_inc(s_r, 1)
                dve.wait_ge(s_vp, b + 1)
                dve.tensor_copy(tiles4(v_all, b), ps[:, 6 + par, :].rearrange("p (t c) -> p t c", c=C)).then_inc(s_vsb, 1)

            dve.wait_ge(s_w2, 160)
            dve.tensor_copy(be_part[:, 0, :], be_in[:]).then_inc(s_be, 1)
            dve.wait_ge(s_be, 1)
            dve.tensor_tensor(be_rest[:], be_in[:], be_part[:, 0, :], ALU.subtract).then_inc(s_be, 1)
            dve.wait_ge(s_be, 2)
            dve.tensor_copy(be_part[:, 1, :], be_rest[:]).then_inc(s_be, 1)
            dve.wait_ge(s_be, 3)
            dve.tensor_tensor(be_part[:, 2, :], be_rest[:], be_part[:, 1, :], ALU.subtract).then_inc(s_be, 1)
            dve.wait_ge(s_x, 64)
            norm_x(0, 0)
            rests(0, 0, True)
            rests(1, 1, True)
            with dve.Fori(1, B // 2 - 1) as it:
                for par in range(2):
                    rests(par, 2 * it + par, True)
            for b in (B - 2, B - 1):
                rests(b % 2, b, b + 1 < B)

            def take(gs, g, pos, kind, n):
                index = rot_base(gs, g) + pos
                bank = (rot_base(gs, gs) + pos) % 2
                dve.wait_ge(s_rot, index + 1)
                if kind == "scores":
                    buf = (gs + 2) % 2
                    pr, j = divmod(n, 5)
                    if n == 0:
                        ge(dve, s_msplit, 4 * (g + 1))
                    if j < 4:
                        i = 2 * pr + j // 2
                        places = [(i, 3, 0)] if j % 2 == 0 else [(i, 2, 0), (i, 0, 384)]
                        for i, qt, at in places:
                            last = dve.tensor_reduce(m_q[:, buf, 4 * i + qt:4 * i + qt + 1],
                                                     ps[:, bank, at:at + (qt + 1) * P], AX, ALU.max)
                    else:
                        cols = m_q[:, buf, 8 * pr:8 * pr + 8].rearrange("p (i q) -> p i q", q=4)[:, :, 1]
                        last = dve.tensor_reduce(cols, ps[:, bank, :].rearrange("p (i k) -> p i k", i=2), AX, ALU.max)
                    last.then_inc(s_rotf, 1)
                    if n == 9:
                        done = 4 * (g + 2)
                        dve.wait_ge(s_rotf, index + 1)
                        dve.tensor_scalar(m_part[:, buf, 0, :], m_q[:, buf, :], -1.0, None, ALU.mult).then_inc(s_msplit, 1)
                        dve.wait_ge(s_msplit, done + 1)
                        dve.scalar_tensor_tensor(out=m_rest[:, buf, :], in0=m_q[:, buf, :], scalar=-1.0,
                                                 in1=m_part[:, buf, 0, :], op0=ALU.mult, op1=ALU.subtract).then_inc(s_msplit, 1)
                        dve.wait_ge(s_msplit, done + 2)
                        dve.tensor_copy(m_part[:, buf, 1, :], m_rest[:, buf, :]).then_inc(s_msplit, 1)
                        dve.wait_ge(s_msplit, done + 3)
                        dve.tensor_tensor(m_part[:, buf, 2, :], m_rest[:, buf, :], m_part[:, buf, 1, :],
                                          ALU.subtract).then_inc(s_msplit, 1)
                elif kind == "max_rows":
                    ge(dve, s_mw, 16 * g)
                    dve.tensor_copy(mT_sb[:, (gs + 1) % 2, :], ps[0:48, bank, 0:64].bitcast(BF16)).then_inc(s_rotf, 1)
                else:
                    o = ps[:, bank, :].rearrange("p (t i r) -> p t i r", t=NT, i=4)
                    dve.reciprocal(rden[:, gs % 2], o[:, :, :, HD]).then_inc(s_rden, 1)
                    dve.wait_ge(s_rden, g - 1)
                    q = (gs - 2) % 4
                    y4 = (y_sb[:, g - 2 - q:g + 2 - q] if isinstance(g, int) else y_sb[:, bass.ds(g - 2 - q, 4)])
                    dve.tensor_tensor(y4[:, :, 32 * q:32 * q + 32].rearrange("p t (i d) -> p t i d", d=HD),
                                      o[:, :, :, 0:HD], rden[:, gs % 2].rearrange("p t (i o) -> p t i o", o=1).broadcast_to([P, NT, 4, HD]),
                                      ALU.mult).then_inc(s_rotf, 1)

            def step(gs, g):
                for pos, (kind, n) in enumerate(rot_items(gs)):
                    take(gs, g, pos, kind, n)

            quad_steps(dve, step)

            def stats(x4, st_, mv_, s_stat, s_seed_, par, b, y, r):
                for t in range(NT):
                    last = dve.bn_stats(st_[:, par, t, :], x4[:, t, :])
                last.then_inc(s_stat, 1)
                wait_apart(dve, s_stat, b + 1, s_passed)
                for t in range(NT):
                    last = dve.bn_aggr(mv_[:, par, t, :], st_[:, par, t, :])
                last.then_inc(s_seed_, 1)
                seed(dve, s_seed_, SEED_OPS * b + 1, y[:, par, :], r[:, par, 0, :], r[:, par, 1, :], mv_[:, par, :, 1])

            def spread(row, n):
                return row[:].rearrange("p (o n) -> p o n", o=1).broadcast_to([P, NT, n])

            def shared(ns, n):
                if 0 <= ns < B:
                    par = ns % 2
                    dve.wait_ge(s_proj, n + 1)
                    dve.tensor_tensor(a_sb[:, par], ps[:, 1, :].rearrange("p (t c) -> p t c", c=C), spread(b_proj, C),
                                      ALU.add).then_inc(s_a, 1)
                    dve.wait_ge(s_a, n + 1)
                    stats(a_sb[:, par], st, mv, s_stA, s_seedA, par, n, rstd, root)
                if 0 <= ns - 1 < B:
                    par, b = (ns - 1) % 2, n - 1
                    x4 = tiles4(x_sb, b)
                    dve.wait_ge(s_newtA, NEWTON_OPS * (b + 1))
                    for t in range(NT):
                        last = dve.tensor_scalar(a_sb[:, par, t, :], a_sb[:, par, t, :], mv[:, par, t, 0:1],
                                                 rstd[:, par, t:t + 1], ALU.subtract, ALU.mult)
                    last.then_inc(s_res, 1)
                    dve.wait_ge(s_res, 2 * b + 1)
                    dve.tensor_tensor(x4, x4, a_sb[:, par], ALU.add).then_inc(s_res, 1)
                    wait_apart(dve, s_res, 2 * b + 2, s_passed)
                    stats(x4, st2, mv2, s_st2, s_seedB, par, b, rstd2, root2)
                if 0 <= ns - 2 < B:
                    par, b = (ns - 2) % 2, n - 2
                    x4 = tiles4(x_sb, b)
                    dve.wait_ge(s_newtB, NEWTON_OPS * (b + 1))
                    ge(dve, s_xT2, b - 1)
                    ge(dve, s_y, b - 1)
                    for t in range(NT):
                        last = dve.tensor_scalar(xn2[:, par, t, :], x4[:, t, :], mv2[:, par, t, 0:1],
                                                 rstd2[:, par, t:t + 1], ALU.subtract, ALU.mult)
                    last.then_inc(s_xn2, 1)
                if 0 <= ns - SKEW < B:
                    b = n - SKEW
                    dve.wait_ge(s_lg, b + 1)
                    dve.tensor_tensor(tiles4(logits, b), ps[:, 3, 0:NT * E].rearrange("p (t e) -> p t e", e=E), spread(b_r, E),
                                      ALU.add).then_inc(s_lgsb, 1)
                    for j in range(2):
                        dve.wait_ge(s_gel, 2 * b + j + 1)
                        dve.wait_ge(s_ha, 2 * b + j + 1)
                        ge(dve, s_y2, b)
                        dve.scalar_tensor_tensor(out=hid[:, j, :], in0=ps[:, 5 + 2 * j, :], scalar=b_s1[:, j:j + 1],
                                                 in1=gel[:, j, :], op0=ALU.add, op1=ALU.mult).then_inc(s_hid, 1)
                    dve.wait_ge(s_y2, b + 1)
                    dve.tensor_tensor(tiles4(ysum, b), ps[:, 2, :].rearrange("p (t c) -> p t c", c=C), spread(b_s2, C),
                                      ALU.add).then_inc(s_ysum, 1)

            skewed(dve, shared)

            def wide(t):
                return t.rearrange("p (t o) -> p t o", o=1).broadcast_to([P, TILES, E])

            def per_expert(t):
                return t.rearrange("p (o e) -> p o e", o=1).broadcast_to([P, TILES, E])

            done = 0

            def then(ins):
                nonlocal done
                done += 1
                ins.then_inc(s_rt, 1)
                dve.wait_ge(s_rt, done)

            numbers = per_expert(iota_f[:, ROUTED:])
            dve.wait_ge(s_lgsb, B)
            source = logits[:]
            for k in range(2):
                then(dve.tensor_reduce(top[:, k, :], source, AX, ALU.max))
                then(dve.tensor_tensor(lowest, source, wide(top[:, k, :]), ALU.is_equal))
                then(dve.tensor_tensor(lowest, lowest, numbers, ALU.mult))
                then(dve.tensor_reduce(top[:, 2, :], lowest, AX, ALU.min))
                then(dve.tensor_tensor(onehot[k], numbers, wide(top[:, 2, :]), ALU.is_equal))
                if k == 0:
                    then(dve.scalar_tensor_tensor(out=both, in0=onehot[0], scalar=-HUGE, in1=logits[:], op0=ALU.mult, op1=ALU.add))
                    source = both
            then(dve.tensor_tensor(both, onehot[0], onehot[1], ALU.add))
            assert done == BOTH_STEP
            then(dve.tensor_tensor(top[:, 3, :], top[:, 1, :], top[:, 0, :], ALU.subtract))
            assert done == DIFFERENCE_STEP
            dve.wait_ge(s_exw, 1)
            then(dve.tensor_scalar(top[:, 5, :], top[:, 4, :], 1.0, None, ALU.add))
            then(dve.reciprocal(weight[:, 0, :], top[:, 5, :]))
            then(dve.tensor_tensor(weight[:, 1, :], top[:, 4, :], weight[:, 0, :], ALU.mult))
            dve.wait_ge(s_pref, 1)

            def halves(bank):
                return ps[:, bank:bank + 2, 0:TILES * E // 2]

            def split2(t):
                return t.rearrange("p (k t) e -> p k (t e)", k=2)

            then(dve.tensor_copy(split2(counts[0]), halves(2)))
            at, s_ = 0, 1
            while s_ < TILES:
                then(dve.tensor_tensor(counts[1 - at][:, s_:, :], counts[at][:, s_:, :], counts[at][:, :TILES - s_, :], ALU.add))
                then(dve.tensor_copy(counts[1 - at][:, :s_, :], counts[at][:, :s_, :]))
                at, s_ = 1 - at, 2 * s_
            then(dve.tensor_scalar(small[:, 0, :], counts[at][:, TILES - 1, :], float(P - 1), None, ALU.add))
            then(dve.tensor_copy(small_i[:, 0, :], small[:, 0, :]))
            then(dve.tensor_scalar(small_i[:, 1, :], small_i[:, 0, :], 7, None, ALU.arith_shift_right))
            then(dve.tensor_copy(small[:, 1, :], small_i[:, 1, :]))
            then(dve.tensor_copy(small[:, 2, :], small[:, 1, :]))
            end, s_ = 2, 1
            while s_ < E:
                then(dve.tensor_tensor(small[:, 5 - end, s_:], small[:, end, s_:], small[:, end, :E - s_], ALU.add))
                then(dve.tensor_copy(small[:, 5 - end, :s_], small[:, end, :s_]))
                end, s_ = 5 - end, 2 * s_
            then(dve.tensor_tensor(small[:, 4, :], small[:, end, :], small[:, 1, :], ALU.subtract))
            then(dve.tensor_scalar(small[:, 5, :], small[:, 4, :], float(P), None, ALU.mult))
            then(dve.tensor_scalar(etile_f[:, 0, :], iota_f[0:1, 0:ROUTED], small[0:1, end, 0:1], None, ALU.is_ge))
            for e in range(1, E):
                then(dve.scalar_tensor_tensor(out=etile_f[:, e % 2, :], in0=iota_f[0:1, 0:ROUTED], scalar=small[0:1, end, e:e + 1],
                                              in1=etile_f[:, 1 - e % 2, :], op0=ALU.is_ge, op1=ALU.add))
            then(dve.tensor_scalar(etile_f[:, E % 2, :], etile_f[:, 1 - E % 2, :], float(E - 1), None, ALU.min))
            then(dve.tensor_copy(etile[:], etile_f[:, E % 2, :]))
            then(dve.tensor_tensor(split2(counts[at]), split2(counts[at]), halves(2), ALU.subtract))
            then(dve.tensor_tensor(split2(counts[at]), split2(counts[at]), halves(0), ALU.add))
            then(dve.tensor_tensor(counts[at], counts[at], per_expert(small[:, 5, :]), ALU.add))
            for k in range(2):
                then(dve.tensor_tensor(onehot[k], onehot[k], counts[at], ALU.mult))
                then(dve.tensor_reduce(top[:, k, :], onehot[k], AX, ALU.add))
                then(dve.tensor_copy(slot_i[:, :, k], top[:, k, :]))
            assert done == ROUTING_STEPS, done

            def stage_slots(par, b, sem_):
                b4 = slot_i[:, 4 * b:4 * b + 4, :] if isinstance(b, int) else slot_i[:, bass.ds(4 * b, 4), :]
                dve.tensor_copy(idx_cur[:, par, :], b4.rearrange("p t k -> p (t k)")).then_inc(sem_, 1)

            for b in range(2):
                stage_slots(b, b, s_idx)
            with dve.Fori(1, B // 2) as it:
                for par in range(2):
                    dve.wait_ge(s_scat[par], 16 * 2 * NT * it)
                    stage_slots(par, 2 * it + par, s_idx)

            def expert_tile(ns, n):
                if ns < ROUTED:
                    par = ns % 2
                    dve.wait_ge(s_ge, n + 1)
                    dve.wait_ge(s_he, 2 * n + 2)
                    ge(dve, s_hT, n - 1)
                    dve.tensor_tensor(hidE[:, par, :], ps[:, 4 + par, 0:HR], gelE[:, par, :], ALU.mult).then_inc(s_hide, 1)
                if 0 <= ns - 2:
                    par = ns % 2
                    dve.wait_ge(s_ye, n - 1)
                    dve.wait_ge(s_tag, 2 * n - 2)
                    if ns >= 4:
                        dve.wait_ge(s_yst[par], 8 * (n - par) - 16)
                    dve.tensor_scalar(ys[:, par, :], ps[:, par, 0:C], weight_cur[:, (ns - 2) % 4:(ns - 2) % 4 + 1], None,
                                      ALU.mult).then_inc(s_yesb, 1)

            tiles_by_four(dve, expert_tile)

            def combine(ns, n):
                if 0 <= ns < B:
                    par = ns % 2
                    dve.wait_ge(s_sum, n + 1)
                    dve.tensor_tensor(summed[:, par], summed[:, par], tiles4(ysum, n), ALU.add).then_inc(s_comb, 1)
                    dve.wait_ge(s_comb, n + 1)
                    stats(summed[:, par], st, mv, s_st3, s_seedC, par, n, rstd, root)
                if 0 <= ns - 1 < B:
                    par, b = (ns - 1) % 2, n - 1
                    dve.wait_ge(s_newtC, NEWTON_OPS * (b + 1))
                    dve.scalar_tensor_tensor(out=shift[:, par], in0=mv[:, par, :, 0], scalar=-1.0, in1=rstd[:, par], op0=ALU.mult,
                                             op1=ALU.mult).then_inc(s_shift, 1)
                    dve.wait_ge(s_normal, n)
                    dve.tensor_tensor(final[:, par], final[:, par], tiles4(x_sb, b), ALU.add).then_inc(s_fin, 1)

            combine_steps(dve, combine)


_OUTS = [((16, 512, 128), "float32")]


def kernel(**inputs):
    import numpy as _np
    import concourse.bacc as _bacc
    from concourse import mybir as _mybir
    from concourse.bass_utils import run_bass_kernel_spmd as _run

    nc = _bacc.Bacc("TRN2", target_bir_lowering=False, num_devices=1)
    arrays, aps = {}, {}
    for name, value in inputs.items():
        v = _np.ascontiguousarray(value)
        arrays[f"in_{name}"] = v
        aps[name] = nc.dram_tensor(f"in_{name}", v.shape, _mybir.dt.from_np(v.dtype), kind="ExternalInput").ap()
    shape, dtype = _OUTS[0]
    out = nc.dram_tensor("out_0_dram", shape, _mybir.dt.from_np(_np.dtype(dtype)), kind="ExternalOutput").ap()
    build(nc, aps, out)
    r = _run(nc, [arrays], core_ids=[0])
    return r.results[0]["out_0_dram"]
```

```python
from contextlib import ExitStack

import concourse.bass as bass
from concourse import mybir

ALU = mybir.AluOpType
ACT = mybir.ActivationFunctionType
AX = mybir.AxisListType.X
F32 = mybir.dt.float32
BF16 = mybir.dt.bfloat16
I32 = mybir.dt.int32

P = 128
B, T, C = 16, 512, 128
NT = T // P
TILES = B * NT
LAT, HEADS, HD = 32, 16, 8
QUADS = B * HEADS // 4
E, HS, HR = 12, 256, 384
TAU = 1.5
EPS = 1e-5
MASKED = -1e30
ROUTED = -(-(2 * B * T // P + E - 1) // 4) * 4
FAR = 16.0
HUGE = 3e38
ROW = C + 2
VALUES, PLACE, WEIGHT = slice(0, C), slice(C, C + 1), slice(C + 1, C + 2)
Q_SLOTS = (0, 0, 0, 1, 1, 2)
K_SLOTS = (2, 0, 1, 0, 1, 0)
SLOTS = len(Q_SLOTS)
QK_ROWS = HD * SLOTS
ROWS = P // 2
M_ROWS = slice(ROWS - 3, ROWS)


ROOM = B * T + P
EXTRA = ROUTED - 2 * TILES
BLANKS = EXTRA + E
PICK_STEPS, BOTH_STEP, PLACE_STEPS = 13, 12, 9
ROUTE_STEPS = PICK_STEPS + PLACE_STEPS
TABLE_STEPS = 14


def wait_apart(engine, sem, value, passed):
    engine.wait_ge(sem, value)
    engine.sem_inc(passed, 1)


def ge(engine, sem, value):
    if not (isinstance(value, int) and value <= 0):
        engine.wait_ge(sem, value)


def rot_items(g):
    items = []
    for n in range(12):
        if n == 2:
            if 0 <= g + 1 < QUADS:
                items.append(("max_rows", 0))
        elif n == 7:
            if 0 <= g - 2 < QUADS:
                items.append(("turn_back", 0))
        elif g + 2 < QUADS:
            items.append(("scores", n - (n > 2) - (n > 7)))
    return items


FIRST, LAST = -2, QUADS + 1
ROT_BASE = {}
_n = 0
for _g in range(FIRST, LAST + 1):
    ROT_BASE[_g] = _n
    _n += len(rot_items(_g))
ROT_PER = 12
ROT_BANKS = (0, 1, 6)
PV_BANK = 7


def rot_base(gs, g):
    if isinstance(g, int):
        return ROT_BASE[g]
    return ROT_PER * g + (ROT_BASE[gs] - ROT_PER * gs)


ROOT_STEPS = 13
NEWTON = 3
ROOT_OPS = 3 + 3 * NEWTON
NEWTON_OPS = 4 * NEWTON
SEED_OPS = 4


def seed(dve, sem, done, y, v, half, var):
    dve.wait_ge(sem, done)
    dve.tensor_scalar(v, var, EPS, None, ALU.add).then_inc(sem, 1)
    dve.wait_ge(sem, done + 1)
    dve.tensor_scalar(half.bitcast(I32), v.bitcast(I32), 1, None, ALU.arith_shift_right).then_inc(sem, 1)
    dve.wait_ge(sem, done + 2)
    dve.tensor_scalar(y.bitcast(I32), half.bitcast(I32), -1.0, float(0x5F3759DF), ALU.mult, ALU.add).then_inc(sem, 1)


def newton(pool, passed, sem, done, y, v, t):
    for _ in range(NEWTON):
        pool.tensor_tensor(t, y, y, ALU.mult).then_inc(sem, 1)
        pool.wait_ge(sem, done + 1)
        pool.tensor_tensor(t, t, v, ALU.mult).then_inc(sem, 1)
        wait_apart(pool, sem, done + 2, passed)
        pool.tensor_scalar(t, t, -0.5, 1.5, ALU.mult, ALU.add).then_inc(sem, 1)
        pool.wait_ge(sem, done + 3)
        pool.tensor_tensor(y, y, t, ALU.mult).then_inc(sem, 1)
        done = done + 4
        pool.wait_ge(sem, done)


def rows_of(vector, n):
    return vector.rearrange("(o n) -> o n", o=1).broadcast_to([P, n])


def build(nc, a, out):
    with ExitStack() as ctx:
        def sb(name, shape, dt=F32):
            return ctx.enter_context(nc.sbuf_tensor(name, shape, dt))

        def sem(name):
            return ctx.enter_context(nc.semaphore(name))

        x_sb = sb("x_sb", [P, TILES, C])
        v_all = sb("v_all", [P, TILES, C])
        y_sb = sb("y_sb", [P, TILES, C])
        ident = sb("ident", [P, P])
        ident_bf = sb("ident_bf", [P, P], BF16)
        mask_q = sb("mask_q", [P, P], BF16)
        ysum = kept_xT = y_sb
        late = v_all[:, TILES - 8:TILES, :].rearrange("p t c -> p (t c)")
        lat_in = late[:, 0:3 * LAT].rearrange("p (n c) -> p n c", n=3)
        heads_in = late[0:LAT, P:4 * P].rearrange("p (n c) -> p n c", n=3)
        latT = late[0:LAT, 4 * P:7 * P].rearrange("p (n c) -> p n c", n=3)
        iota_i = v_all[:, TILES - 10:TILES - 8, :].rearrange("p t c -> p (t c)")[:, 0:ROUTED + E].bitcast(I32)
        tag_i = v_all[:, TILES - 13:TILES - 10, :].rearrange("p t c -> p (t c)")[:, 0:BLANKS + 2 * TILES + E].bitcast(I32)
        w_qkv = sb("w_qkv", [P, 3, C])
        st = sb("st", [P, 2, NT, 6])
        y_tail = y_sb[:, TILES - 2:TILES].rearrange("p t c -> p (t c)")
        mv1 = y_tail[:, 0:2 * TILES].rearrange("p (t k) -> p t k", k=2)
        rstd1 = y_tail[:, 2 * TILES:3 * TILES]
        root1 = y_tail[:, 3 * TILES:3 * TILES + 6 * NT].rearrange("p (k t) -> p k t", k=3)
        mv = sb("mv", [P, 2, NT, 2])
        row_area = sb("row_area", [P, 2 * NT * ROW])
        xn = row_area[:, 0:2 * NT * C].rearrange("p (a t c) -> p a t c", a=2, c=C)
        xnT = sb("xnT", [P, 2, T])
        split_area = sb("split_area", [P, 5 * 1024])
        part = split_area[:, 0:3 * 1024].bitcast(BF16).rearrange("p (a b c t) -> p a b c t", a=2, b=2, c=3)
        rest = split_area[:, 3 * 1024:5 * 1024].rearrange("p (a b t) -> p a b t", a=2, b=2)
        we2 = split_area[:, 0:E * HR]
        quad_area = sb("quad_area", [P, 6 * 1024])
        qk = quad_area[:, 0:4 * 1024].bitcast(BF16).rearrange("p (q s r t) -> p q s r t", q=4, s=2, r=2)
        v_cur = quad_area[:, 4 * 1024:6 * 1024].rearrange("p (q t h r) -> p q t h r", q=4, t=NT, h=4)
        be1r = quad_area[0:3, 0:E * HR].bitcast(BF16)
        be2r = quad_area[0:3, 5 * 1024:5 * 1024 + E * C // 2].bitcast(BF16)
        pT_area = sb("pT_area", [P, 10 * 1024])

        def area(n, count=1):
            return pT_area[:, 1024 * n:1024 * (n + count)]

        pT = pT_area[:, :].rearrange("p (a n t) -> p a n t", a=2, n=5)
        v_flat = v_all[:].rearrange("p t c -> p (t c)")
        ycur = v_flat[:, 0:1024].rearrange("p (a t c) -> p a t c", a=2, c=C)
        yT = v_flat[:, 1024:2048].rearrange("p (a t) -> p a t", a=2)
        xn2 = v_flat[:, 2048:3072].rearrange("p (a t c) -> p a t c", a=2, c=C)
        gel = v_flat[:, 3072:4096].rearrange("p (a t) -> p a t", a=2)
        hid = v_flat[:, 4096:6144].rearrange("p (a j t) -> p a j t", a=2, j=2)
        R = 2 * NT
        used = 6144

        def table(n):
            nonlocal used
            used += n
            assert used <= TILES * C
            return v_flat[:, used - n:used]

        def by_expert(t):
            return t.rearrange("p (t e) -> p t e", e=E)

        logit, lowest, masked, place = (by_expert(table(R * E)) for _ in range(4))
        onehot = table(2 * R * E).rearrange("p (k t e) -> p k t e", k=2, e=E)
        chosen = table(2 * R * E).rearrange("p (k t e) -> p k t e", k=2, e=E)
        both = table(R * E // 2).bitcast(BF16)
        counted = table(E // 2).bitcast(BF16)
        newly = table(E)
        top = table(4 * R).rearrange("p (k t) -> p k t", k=4)
        slot_f = table(2 * R).rearrange("p (k t) -> p k t", k=2)
        pair_w = table(2 * R).rearrange("p (k t) -> p k t", k=2)
        small = table(8)
        ends = table(ROUTED)
        tile_row = ycur[0:1].rearrange("p a t c -> p (a t c)")[:, 0:2 * ROUTED].rearrange("p (k j) -> p k j", k=2)
        we1 = pT_area[:, 0:E * 2 * HR]
        m_q = sb("m_q", [P, 2, 16])
        m_rest = sb("m_rest", [P, 2, 16])
        m_part = sb("m_part", [P, 2, 3, 16], BF16)
        mT_sb = sb("mT_sb", [48, 2, P], BF16)
        outT_area = sb("outT_area", [P, 2 * NT * ROW])
        outT = outT_area[:, 0:2 * T].rearrange("p (a t) -> p a t", a=2)
        hidT_area = sb("hidT_area", [P, 2 * HR])
        xT2 = xnT
        rows_cur = [area_[:, :].rearrange("p (a t c) -> p a t c", a=2, c=ROW) for area_ in (row_area, outT_area)]
        xs = row_area[:, 0:4 * ROW].rearrange("p (a c) -> p a c", a=4)
        xsT = row_area[:, 4 * ROW:4 * ROW + 2 * C].rearrange("p (a c) -> p a c", a=2)
        ys = row_area[:, 4 * ROW + 2 * C:4 * ROW + 4 * C].rearrange("p (a c) -> p a c", a=2)
        gelE = xnT[:].rearrange("p a t -> p (a t)")[:, 0:2 * HR].rearrange("p (a h) -> p a h", a=2)
        hidE = outT_area[:, 0:2 * HR].rearrange("p (a h) -> p a h", a=2)
        hidT = hidT_area[:, :].rearrange("p (a h) -> p a h", a=2)
        w_proj = sb("w_proj", [P, C])
        w_r = sb("w_r", [P, E])
        ws1 = sb("ws1", [P, 2 * HS])
        ws2 = sb("ws2", [P, 2, C])
        b_s1 = sb("b_s1", [P, 4])
        b_r = sb("b_r", [P, E])
        be_in = outT_area[:, 0:86]
        be_rest = outT_area[:, 86:172]
        be_part = outT_area[:, 172:172 + 129].bitcast(BF16).rearrange("p (n x) -> p n x", n=3)
        ones_bf = sb("ones_bf", [3, P], BF16)
        bias_rows = sb("bias_rows", [3, 2, C], BF16)
        before = sb("before", [P, P])
        before_bf = sb("before_bf", [P, P], BF16)
        all_bf = sb("all_bf", [P, P], BF16)
        ones = sb("ones", [P, P])
        st2 = sb("st2", [P, 2, 2 * NT, 6])
        mv2 = sb("mv2", [P, 2, 2 * NT, 2])
        rstd2 = sb("rstd2", [P, 2, 2 * NT])
        root2 = sb("root2", [P, 3, 2 * NT])
        shift2 = sb("shift2", [P, 2, NT])
        moved = sb("moved", [P, TILES])
        iota_f = sb("iota_f", [P, ROUTED + E])
        kept = split_area[:, E * HR:5 * 1024]
        etile = kept[0:1, 0:ROUTED].bitcast(I32)
        atile = kept[0:1, ROUTED:2 * ROUTED].bitcast(I32)
        rooms = sb("rooms", [P, E])
        pad_rows = kept[:, 2 * ROUTED + E:2 * ROUTED + 2 * E]
        pad_row = kept[0:1, 2 * ROUTED + 2 * E:2 * ROUTED + 3 * E].bitcast(I32)
        place_cur = sb("place_cur", [P, 4], I32)
        weight_cur = sb("weight_cur", [P, 4])
        tag = sb("tag", [P, 2 * TILES])
        tags = tag[:, :].rearrange("p (k t) -> p k t", k=2)
        idx_cur = sb("idx_cur", [P, 2, 2, NT], I32)
        picked = area(0, 4).rearrange("p (a k t c) -> p a k t c", a=2, k=2, c=C)
        summed = area(4, 3).rearrange("p (a t c) -> p a t c", a=3, c=C)
        final = area(7, 2).rearrange("p (a t c) -> p a t c", a=2, c=C)
        root3 = area(9)[:, 0:9 * R].rearrange("p (a k t) -> p a k t", a=3, k=3)
        mv3 = area(9)[:, 9 * R:15 * R].rearrange("p (a t k) -> p a t k", a=3, k=2)
        rstd3 = area(9)[:, 15 * R:18 * R].rearrange("p (a t) -> p a t", a=3)
        shift = area(9)[:, 18 * R:21 * R].rearrange("p (a t) -> p a t", a=3)
        rden = sb("rden", [P, 2, NT, 4])
        ps = ctx.enter_context(nc.psum_tensor("ps", [P, 8, 512], F32))

        qk_dram = nc.dram_tensor("qk_dram", [2, SLOTS, B * C, T], BF16).ap()
        be1_dram = nc.dram_tensor("be1_dram", [3, E * 2 * HR], BF16).ap()
        be2_dram = nc.dram_tensor("be2_dram", [3, E * C], BF16).ap()
        b2_dram = nc.dram_tensor("b2_dram", [3, 2, C], BF16).ap()
        xn2_dram = nc.dram_tensor("xn2_dram", [B * T, C], F32).ap()
        xs_dram = nc.dram_tensor("xs_dram", [E * ROOM + BLANKS * P, ROW], F32).ap()
        ys_dram = nc.dram_tensor("ys_dram", [(2 * TILES + BLANKS) * P, C], F32).ap()
        m_dram = nc.dram_tensor("m_dram", [4, 3, 2, 2 * T], BF16).ap()

        X_LOADS = ((0, 2), (2, 4), (4, 8), (8, 16))
        s_x = [sem(f"x_loaded{n}") for n in range(len(X_LOADS))]; s_w = sem("w_loaded")
        s_const = sem("const_ready"); s_pstep = sem("pool_step")
        s_latT = sem("latT_done"); s_latT_sb = sem("latT_copied"); s_wmul = sem("w_multiplied"); s_wsb = sem("w_ready")
        s_stats = sem("ln_stats"); s_aggr = sem("ln_moments"); s_root1 = sem("ln_root_steps"); s_xn = sem("xn_ready")
        s_xT = sem("xT_done"); s_xT_sb = sem("xnT_ready")
        s_qkp = sem("qk_projected"); s_vp = sem("v_projected"); s_vsb = sem("v_ready")
        s_p1 = sem("part1_ready"); s_r = sem("rest_ready"); s_p2 = sem("part2_ready"); s_p3 = sem("part3_ready")
        s_parts = [[sem(f"parts{n}_stored{par}") for n in range(3)] for par in range(2)]
        s_ident = sem("ident_ready")
        s_qk = [sem(f"qk_loaded{n}") for n in range(4)]
        s_m = [sem(f"m_loaded{n}") for n in range(4)]
        s_mw = sem("m_stored")
        s_rot = sem("rot_filled"); s_rotf = sem("rot_freed")
        s_msplit = sem("m_split")
        s_st = sem("scoresT_filled"); s_exp = sem("exp_done"); s_masked = sem("probs_masked"); s_pv = sem("pv_done"); s_outT = sem("outT_ready")
        s_rden = sem("rden_ready"); s_vcur = sem("v_cur_ready")
        s_passed = sem("waits_passed")
        s_zset = sem("zeros_set"); s_zero = sem("rows_zeroed")
        s_w2 = sem("small_weights_loaded"); s_be = sem("be_split"); s_bew = sem("be_stored"); s_ber = sem("be_rows_loaded")
        s_we = sem("expert_weights_loaded")
        s_ycur = sem("ycur_ready"); s_yT = sem("yT_done"); s_yTsb = sem("yT_ready"); s_proj = sem("projected")
        s_st2 = sem("joint_stats"); s_root = sem("joint_root_steps"); s_z = sem("residual_ready")
        s_shift2 = sem("shift2_ready"); s_xn2 = sem("xn2_ready"); s_store = [sem(f"xn2_stored{n}") for n in range(2)]
        s_rowl = [sem(f"rows_loaded{n}") for n in range(2)]
        s_xT2 = sem("xT2_done"); s_xT2sb = sem("xT2_ready"); s_lg = sem("logits_done"); s_lgsb = sem("logits_ready")
        s_hg = sem("shared_g_done"); s_gel = sem("shared_gelu_ready"); s_ha = sem("shared_a_done"); s_hid = sem("shared_hidden_ready")
        s_y2 = sem("shared_y_done"); s_ysum = sem("shared_y_ready")
        s_rt = sem("routing_step"); s_pref = sem("prefixes_done"); s_exw = sem("exp_of_difference")
        s_tagged = sem("rows_tagged"); s_idx = sem("slots_staged"); s_scat = [sem(f"rows_scattered{n}") for n in range(2)]
        s_cset = sem("counts_cleared"); s_table = sem("table_step"); s_tsum = sem("table_sums"); s_pad = sem("rows_padded")
        s_xs = [sem(f"xs_loaded{n}") for n in range(4)]
        s_xsT = sem("xsT_done"); s_xsTsb = sem("xsT_ready"); s_he = sem("expert_h_done"); s_ge = sem("expert_gelu_ready")
        s_hide = sem("expert_hidden_ready"); s_hT = sem("expert_hiddenT_done"); s_hTsb = sem("expert_hiddenT_ready")
        s_ye = sem("expert_y_done"); s_yesb = sem("expert_y_ready"); s_yst = [sem(f"ys_stored{n}") for n in range(2)]
        s_tag = sem("tags_read"); s_sum = sem("routed_sums"); s_shift = sem("shift_ready"); s_normal = sem("normalised"); s_pick = [sem(f"rows_picked{n}") for n in range(2)]
        s_comb = sem("combine_steps"); s_st3 = sem("stats3"); s_seedC = sem("seedC"); s_newtC = sem("newtonC"); s_fin = sem("final_steps")
        s_out = [sem(f"out_stored{n}") for n in range(2)]

        ROT_ALL = ROT_BASE[LAST] + len(rot_items(LAST))
        STEPS = B + 8
        TABLE_AT = B + 5

        def skewed(engine, step):
            for n in range(10):
                step(n, n)
            with engine.Fori(5, B // 2 - 1) as it:
                for k in range(2):
                    step(10 + k, 2 * it + k)
            for n in range(B - 2, STEPS):
                step(n, n)

        def routed_before(ns, n):
            return ROUTE_STEPS // 2 * (n - ns % 2) + ROUTE_STEPS

        def project_steps(engine, step):
            for n in range(8):
                step(n, n)
            with engine.Fori(4, B // 2 - 1) as it:
                for k in range(2):
                    step(8 + k, 2 * it + k)
            for n in range(B - 2, B + 4):
                step(n, n)

        def quad_steps(engine, step):
            for g in range(FIRST, 4):
                step(g, g)
            with engine.Fori(1, B - 1) as it:
                for q in range(4):
                    step(4 + q, 4 * it + q)
            for g in range(4 * (B - 1), LAST + 1):
                step(g, g)

        def expert_steps(engine, step):
            for n in range(8):
                step(n, n)
            with engine.Fori(1, (ROUTED - 4) // 8) as it:
                for k in range(8):
                    step(8 + k, 8 * it + k)
            for n in range(ROUTED - 4, ROUTED + 2):
                step(n, n)

        PAIRS = B // 2

        def pair_of(t, n):
            return t[:, R * n:R * n + R]

        def tiles4(t, b):
            return t[:, 4 * b:4 * b + 4, :] if isinstance(b, int) else t[:, bass.ds(4 * b, 4), :]

        blank = y_sb[:].rearrange("p t c -> p (t c)")[:, 0:BLANKS * ROW].rearrange("p (r c) -> p r c", c=ROW)

        def one(t, at):
            return t[:, at:at + 1] if isinstance(at, int) else t[:, bass.ds(at, 1)]

        def pad(engine, experts):
            engine.wait_ge(s_table, TABLE_STEPS)
            engine.wait_ge(s_zero, 16)
            for e in experts:
                row = engine.value_load(pad_row[0:1, e:e + 1], min_val=0, max_val=E * ROOM - P)
                at = E * ROOM + (EXTRA + e) * P
                engine.dma_start(xs_dram[bass.ds(row, P)], xs_dram[at:at + P]).then_inc(s_pad, 16)

        block = ctx.enter_context(nc.Block())

        @block.sync
        def _(sp):
            for n, name in enumerate(("L0_attn_wq_lat", "L0_attn_wk_lat", "L0_attn_wv_lat")):
                sp.dma_start(lat_in[:, n, :], a[name]).then_inc(s_w, 16)
            for n, name in enumerate(("L0_attn_wq_heads", "L0_attn_wk_heads", "L0_attn_wv_heads")):
                sp.dma_start(heads_in[:, n, :], a[name]).then_inc(s_w, 16)
            small_loads = [
                (w_proj[:], a["L0_attn_w_proj"]), (w_r[:], a["L0_ffn_Wr"]), (ws1[:], a["L0_ffn_Ws1"]),
                (ws2[:], a["L0_ffn_Ws2"].rearrange("(k p) d -> p k d", p=P)),
                (be_in[:, 84:85], a["L0_attn_b_proj"].rearrange("(p x) -> p x", p=P)),
                (be_in[:, 85:86], a["L0_ffn_bs2"].rearrange("(p x) -> p x", p=P)),
                (b_r[:], rows_of(a["L0_ffn_br"], E)), (b_s1[:], a["L0_ffn_bs1"].rearrange("(k p) -> p k", p=P)),
                (be_in[:, 0:72], a["L0_ffn_be1"].rearrange("e h -> (e h)").rearrange("(p x) -> p x", p=P)),
                (be_in[:, 72:84], a["L0_ffn_be2"].rearrange("e h -> (e h)").rearrange("(p x) -> p x", p=P))]
            for to, what in small_loads:
                sp.dma_start(to, what, allow_slow_non_contiguous=True).then_inc(s_w2, 16)
            sp.wait_ge(s_zset, 1)
            sp.dma_start(xs_dram[E * ROOM:].rearrange("(r p) c -> p r c", p=P), blank).then_inc(s_zero, 16)

            def store_part(par, b, n):
                for s, slots in ((0, Q_SLOTS), (1, K_SLOTS)):
                    at = [j for j in range(SLOTS) if slots[j] == n]
                    by = at[1] - at[0] if len(at) > 1 else 1
                    source = part[:, par, s, n, :].rearrange("p (o t) -> p o t", o=1).broadcast_to([P, len(at), T])
                    sp.dma_start(qk_dram[s, at[0]:at[-1] + 1:by, bass.ds(C * b, C), :].rearrange("j p t -> p j t"),
                                 source).then_inc(s_parts[par][n], 16)

            def load_rows_of(slot, h, loads):
                for load in loads:
                    i, side = divmod(load, 2)
                    base = ROWS * (i // 2)
                    sp.dma_start(qk[base:base + QK_ROWS, slot, side, i % 2],
                                 qk_dram[side, :, bass.ds(4 * HD * h + HD * i, HD), :]).then_inc(s_qk[slot], 16)

            def store_parts(ns, n):
                if ns == 7:
                    sp.wait_ge(s_const, 1)
                    for k in range(3):
                        sp.wait_ge(s_parts[0][k], 2 * 16)
                    load_rows_of(0, 0, range(8))
                if ns in (B - 1, B + 1):
                    h = (ns - B + 3) // 2
                    load_rows_of(h, h, range(8))
                if 0 <= ns - 4 < B:
                    sp.wait_ge(s_p3, 2 * n - 6)
                    store_part(ns % 2, n - 4, 2)
                if 0 <= ns - 2 < B:
                    sp.wait_ge(s_p1, 2 * n - 2)
                    store_part(ns % 2, n - 2, 0)
                if 0 <= ns - 3 < B:
                    sp.wait_ge(s_p2, 2 * n - 4)
                    store_part((ns - 3) % 2, n - 3, 1)

            project_steps(sp, store_parts)
            sp.wait_ge(s_be, 4)
            sp.dma_start(be1_dram.rearrange("n (p x) -> p n x", p=P), be_part[:, :, 0:72]).then_inc(s_bew, 16)
            sp.dma_start(be2_dram.rearrange("n (p x) -> p n x", p=P), be_part[:, :, 72:84]).then_inc(s_bew, 16)
            for n in range(2):
                sp.dma_start(b2_dram[:, n].rearrange("n (p x) -> p n x", p=P), be_part[:, :, 84 + n:85 + n],
                             allow_slow_non_contiguous=True).then_inc(s_bew, 16)

            def step(gs, g):
                maxima = 0 <= gs + 1 < QUADS
                slot = (gs + 1) % 4
                if gs == 1:
                    sp.wait_ge(s_bew, 64)
                    sp.dma_start(bias_rows[:], b2_dram).then_inc(s_w2, 16)
                if gs == 0:
                    for par in range(2):
                        for n in range(3):
                            sp.wait_ge(s_parts[par][n], 2 * 16 * B // 2)
                if 0 <= gs and gs + 3 < QUADS:
                    ge(sp, s_st, 5 * g)
                    load_rows_of((gs + 3) % 4, g + 3, range(5))
                if maxima:
                    sp.wait_ge(s_rotf, rot_base(gs, g) + rot_items(gs).index(("max_rows", 0)) + 1)
                    sp.dma_start(m_dram[slot].rearrange("n h (x q) -> (n h x) q", q=P),
                                 mT_sb[:, (gs + 1) % 2, :]).then_inc(s_mw, 16)
                if 0 <= gs and gs + 3 < QUADS:
                    load_rows_of((gs + 3) % 4, g + 3, range(5, 7))
                if maxima:
                    sp.wait_ge(s_mw, 16 * (g + 2))
                    for hp in range(2):
                        sp.dma_start(qk[ROWS * hp + M_ROWS.start:ROWS * hp + M_ROWS.stop, slot, 0].rearrange("p r t -> p (r t)"),
                                     m_dram[slot, :, hp]).then_inc(s_m[slot], 16)
                if 0 <= gs and gs + 3 < QUADS:
                    load_rows_of((gs + 3) % 4, g + 3, range(7, 8))

            quad_steps(sp, step)

            sp.wait_ge(s_st, 5 * QUADS)
            sp.wait_ge(s_pv, QUADS)
            sp.dma_start(be1r, be1_dram).then_inc(s_ber, 16)
            sp.dma_start(be2r, be2_dram).then_inc(s_ber, 16)
            for e in range(E):
                sp.dma_start(we2[:, e * HR:(e + 1) * HR].rearrange("p (k d) -> p k d", k=3),
                             a["L0_ffn_We2"][e].rearrange("(k p) d -> p k d", p=P)).then_inc(s_we, 16)
            for e in range(E):
                sp.dma_start(we1[:, e * 2 * HR:(e + 1) * 2 * HR], a["L0_ffn_We1"][e]).then_inc(s_we, 16)

            def tokens(b):
                return xn2_dram[bass.ds(T * b, T)].rearrange("(t p) c -> p t c", p=P)

            def move_rows(ns, n):
                if 0 <= ns - 2 < B:
                    par = (ns - 2) % 2
                    sp.wait_ge(s_xn2, n - 1)
                    sp.dma_start(tokens(n - 2), xn2[:, par]).then_inc(s_store[par], 16)
                if 0 <= ns - 6 < B:
                    par, b = (ns - 6) % 2, n - 6
                    wait_apart(sp, s_store[par], 8 * (b - par) + 16, s_passed)
                    if ns - 8 >= 0:
                        wait_apart(sp, s_scat[par], 8 * R * (b - par), s_passed)
                    for k in range(2):
                        sp.dma_start(rows_cur[k][:, par, :, VALUES], tokens(b)).then_inc(s_rowl[par], 16)

            skewed(sp, move_rows)
            pad(sp, range(E))
            sp.wait_ge(s_pad, 16 * E)
            for par in range(2):
                sp.wait_ge(s_scat[par], 8 * R * B)

            def load_rows(ring, j):
                row = sp.value_load(atile[0:1, bass.ds(j, 1)], min_val=0, max_val=E * ROOM + (EXTRA - 1) * P)
                sp.dma_start(xs[:, ring, :], xs_dram[bass.ds(row, P), :]).then_inc(s_xs[ring], 16)

            for j in range(3):
                load_rows(j, j)

            def expert_tile(ns, n):
                if ns + 3 < ROUTED:
                    if ns > 0:
                        wait_apart(sp, s_xsT, n, s_passed)
                        wait_apart(sp, s_tag, 2 * n, s_passed)
                    load_rows((ns + 3) % 4, n + 3)

            expert_steps(sp, expert_tile)
            for par in range(2):
                sp.wait_ge(s_yst[par], 16 * ROUTED // 2)

            def pick(n):
                for k in range(2):
                    at = (k * TILES + R * n) * P
                    sp.dma_start(picked[:, n % 2, k], ys_dram[at:at + R * P].rearrange("(t p) c -> p t c", p=P)).then_inc(s_pick[n % 2], 16)

            for n in range(2):
                pick(n)
            for n in range(PAIRS + 2):
                if n + 2 < PAIRS:
                    sp.wait_ge(s_comb, n + 1)
                    pick(n + 2)
                if n >= 2:
                    sp.wait_ge(s_fin, n - 1)
                    sp.dma_start(out[2 * n - 4:2 * n - 2].rearrange("b (t p) c -> p (b t) c", p=P), final[:, n % 2]).then_inc(s_out[n % 2], 16)
            for par in range(2):
                sp.wait_ge(s_out[par], 16 * PAIRS // 2)

        @block.gpsimd
        def _(pool):
            n = 0

            def chain(ins):
                nonlocal n
                n += 1
                ins.then_inc(s_pstep, 1)
                pool.wait_ge(s_pstep, n)

            chain(pool.memset(ident[:], 0.0))
            pool.affine_select(out=ident[:], in_=ident[:], compare_op=ALU.not_equal, fill=1.0, base=0,
                               pattern=[[-1, P]], channel_multiplier=1).then_inc(s_ident, 1)
            pool.memset(blank, 0.0)
            pool.iota(tag_i[:, 0:BLANKS], pattern=[[P, BLANKS]], base=2 * TILES * P, channel_multiplier=1)
            pool.iota(tag_i[:, BLANKS:BLANKS + 2 * TILES], pattern=[[TILES * P, 2], [P, TILES]], base=0, channel_multiplier=1)
            chain(pool.iota(tag_i[:, BLANKS + 2 * TILES:], pattern=[[ROOM, E]], base=0, channel_multiplier=0))
            pool.tensor_copy(blank[:, :, PLACE], tag_i[:, 0:BLANKS].rearrange("p (r o) -> p r o", o=1)).then_inc(s_zset, 1)
            pool.tensor_copy(tag[:], tag_i[:, BLANKS:BLANKS + 2 * TILES])
            pool.tensor_copy(rooms[:], tag_i[:, BLANKS + 2 * TILES:])
            pool.memset(all_bf[:], 1.0)
            pool.memset(before[:], 1.0)
            pool.memset(ones[:], 1.0)
            pool.memset(ones_bf[:], 1.0)
            pool.iota(iota_i[:, 0:ROUTED], pattern=[[1, ROUTED]], base=0, channel_multiplier=0)
            pool.iota(iota_i[:, ROUTED:], pattern=[[1, E]], base=-int(FAR), channel_multiplier=0)
            pool.memset(mask_q[:], 0.0)
            for side in range(2):
                pool.memset(qk[:, :, side], float(side))
            chain(pool.memset(v_cur[:], 0.0))
            pool.memset(v_cur[:, :, :, :, HD:HD + 1], 1.0)
            pool.wait_ge(s_ident, 1)
            chain(pool.affine_select(out=before[:], in_=before[:], compare_op=ALU.is_gt, fill=0.0, base=0,
                                     pattern=[[1, P]], channel_multiplier=-1))
            pool.tensor_copy(iota_f[:], iota_i[:])
            pool.affine_select(out=mask_q[:], in_=mask_q[:], compare_op=ALU.is_ge, fill=MASKED, base=0,
                               pattern=[[-1, P]], channel_multiplier=1)
            pool.tensor_copy(before_bf[:], before[:])
            pool.tensor_copy(ident_bf[:], ident[:]).then_inc(s_const, 1)

            def third_parts(ns, n):
                if 0 <= ns - 4 < B:
                    par, b = ns % 2, n - 4
                    if ns - 6 >= 0:
                        pool.wait_ge(s_parts[par][2], 16 * (b - par))
                    for s in range(2):
                        pool.wait_ge(s_p2, 2 * n + s - 7)
                        pool.tensor_tensor(part[:, par, s, 2, :], rest[:, par, s, :], part[:, par, s, 1, :],
                                           ALU.subtract).then_inc(s_p3, 1)

            project_steps(pool, third_parts)

            def mask(blocks, count):
                return pool.affine_select(out=blocks, in_=blocks, compare_op=ALU.is_ge, fill=0.0, base=0,
                                          pattern=[[0, count], [1, P]], channel_multiplier=-1)

            def step(gs, g):
                if 0 <= gs < QUADS:
                    for n in range(5):
                        wait_apart(pool, s_exp, 5 * g + n + 1, s_passed)
                        if n < 4:
                            mask(pT[:, gs % 2, n].rearrange("p (k t) -> p k t", k=2)[:, :, 0:P], 2)
                            last = mask(pT[:, gs % 2, n].rearrange("p (k t) -> p k t", t=P)[:, 7:8], 1)
                        else:
                            last = mask(pT[:, gs % 2, n].rearrange("p (i t) -> p i t", i=4)[:, :, 0:P], 4)
                        last.then_inc(s_masked, 1)
                if not 0 <= gs + 1 < QUADS:
                    return
                ge(pool, s_pv, g - 2)
                q = (gs + 1) % 4
                if isinstance(g, int):
                    first = 4 * ((g + 1) // 4)
                    src = v_all[:, first:first + 4, 32 * q:32 * q + 32]
                else:
                    src = v_all[:, bass.ds(g + 1 - q, 4), 32 * q:32 * q + 32]
                pool.tensor_copy(v_cur[:, q, :, :, 0:HD], src.rearrange("p t (h d) -> p t h d", d=HD)).then_inc(s_vcur, 1)

            pool.wait_ge(s_vsb, B)
            quad_steps(pool, step)

            def scatter(ns, n):
                if 0 <= ns - 7 < B:
                    par, b = (ns - 7) % 2, n - 7
                    pool.wait_ge(s_rowl[par], 16 * (b - par) + 32)
                    pool.wait_ge(s_tagged, n - 6)
                    wait_apart(pool, s_idx, n - 6, s_passed)
                    for t in range(NT):
                        for k in range(2):
                            at = bass.IndirectOffsetOnAxis(ap=idx_cur[:, par, k, t:t + 1], axis=0)
                            pool.indirect_dma_start(xs_dram, at, rows_cur[k][:, par, t, :], None).then_inc(s_scat[par], 16)

            skewed(pool, scatter)

            def expert_tile(ns, n):
                if ns < ROUTED:
                    pool.wait_ge(s_xs[ns % 4], 16 * (n // 4 + 1) if isinstance(n, int) else 4 * (n - ns % 4) + 16)
                    if ns >= 4:
                        wait_apart(pool, s_yst[ns % 2], 8 * (n - ns % 2) - 16, s_passed)
                    pool.tensor_copy(place_cur[:, ns % 4:ns % 4 + 1], xs[:, ns % 4, PLACE]).then_inc(s_tag, 1)
                    pool.tensor_copy(weight_cur[:, ns % 4:ns % 4 + 1], xs[:, ns % 4, WEIGHT]).then_inc(s_tag, 1)
                if 0 <= ns - 2:
                    pool.wait_ge(s_tag, 2 * n - 2)
                    wait_apart(pool, s_yesb, n - 1, s_passed)
                    at = bass.IndirectOffsetOnAxis(ap=place_cur[:, (ns - 2) % 4:(ns - 2) % 4 + 1], axis=0)
                    pool.indirect_dma_start(ys_dram, at, ys[:, ns % 2, :], None).then_inc(s_yst[ns % 2], 16)

            expert_steps(pool, expert_tile)

            for n in range(PAIRS + 1):
                if n < PAIRS:
                    par = n % 2
                    pool.wait_ge(s_pick[par], 32 * (n // 2 + 1))
                    pool.tensor_tensor(picked[:, par, 0], picked[:, par, 0], picked[:, par, 1], ALU.add).then_inc(s_sum, 1)
                if n >= 1:
                    ring = (n - 1) % 3
                    pool.wait_ge(s_seedC, SEED_OPS * n)
                    newton(pool, s_passed, s_newtC, NEWTON_OPS * (n - 1), rstd3[:, ring, :], root3[:, ring, 0, :], root3[:, ring, 2, :])

        @block.scalar
        def _(act):
            def load_x(n):
                first, last = X_LOADS[n]
                act.dma_start(x_sb[:, NT * first:NT * last, :],
                              a["L0_attn_x"][first:last].rearrange("b (t p) c -> p (b t) c", p=P)).then_inc(s_x[n], 16)

            for n in (0, 1):
                load_x(n)
            act.wait_ge(s_latT, 1)
            act.activation(latT[:], ps[0:LAT, 0, 0:3 * P].rearrange("p (n c) -> p n c", n=3), ACT.Copy).then_inc(s_latT_sb, 1)
            for n in (2, 3):
                load_x(n)
            act.wait_ge(s_wmul, 1)
            act.activation(w_qkv[:, 0, :], ps[:, 1, 0:C], ACT.Copy, scale=float(HD) ** -0.5)
            act.activation(w_qkv[:, 1:3, :], ps[:, 1, C:3 * C].rearrange("p (n c) -> p n c", n=2), ACT.Copy).then_inc(s_wsb, 1)

            def first_parts(ns, n):
                if 0 <= ns - 1 < B:
                    act.wait_ge(s_xT, n)
                    ge(act, s_vp, n - 2)
                    act.activation(xnT[:, (ns - 1) % 2, :], ps[:, (ns - 1) % 2, :], ACT.Copy).then_inc(s_xT_sb, 1)
                if 0 <= ns - 2 < B:
                    par, b = ns % 2, n - 2
                    if ns - 4 >= 0:
                        act.wait_ge(s_parts[par][0], 16 * (b - par))
                    for s in range(2):
                        act.wait_ge(s_qkp, 2 * n + s - 3)
                        act.activation(part[:, par, s, 0, :], ps[:, 2 + 2 * s + par, :], ACT.Copy).then_inc(s_p1, 1)
                if 0 <= ns - 3 < B:
                    par, b = (ns - 3) % 2, n - 3
                    if ns - 5 >= 0:
                        act.wait_ge(s_parts[par][1], 16 * (b - par))
                        act.wait_ge(s_p3, 2 * n - 8)
                    for s in range(2):
                        act.wait_ge(s_r, 2 * n + s - 5)
                        act.activation(part[:, par, s, 1, :], rest[:, par, s, :], ACT.Copy).then_inc(s_p2, 1)
                if 0 <= ns - 2 < B:
                    if ns == 8:
                        act.wait_ge(s_const, 1)
                    act.wait_ge(s_vp, n - 1)
                    act.activation(tiles4(v_all, n - 2), ps[:, 6 + ns % 2, :].rearrange("p (t c) -> p t c", c=C),
                                   ACT.Copy).then_inc(s_vsb, 1)

            project_steps(act, first_parts)

            def step(gs, g):
                for n in range(5):
                    if n == 4 and 0 <= gs - 1 < QUADS:
                        act.wait_ge(s_pv, g)
                        if gs - 3 >= 0:
                            pos = rot_items(gs - 1).index(("turn_back", 0))
                            act.wait_ge(s_rot, rot_base(gs - 1, g - 1) + pos + 1)
                        act.activation(outT[:, (gs - 1) % 2, :], ps[:, PV_BANK, :], ACT.Copy).then_inc(s_outT, 1)
                    if 0 <= gs < QUADS:
                        act.wait_ge(s_st, 5 * g + n + 1)
                        if n == 0:
                            ge(act, s_pv, g - 1)
                        u = 2 + 2 * ((5 * gs + n) % 2)
                        act.activation(pT[:, gs % 2, n, :], ps[:, u:u + 2, :].rearrange("p a b -> p (a b)"),
                                       ACT.Exp).then_inc(s_exp, 1)

            act.wait_ge(s_bew, 64)
            quad_steps(act, step)

            act.wait_ge(s_w2, 176)
            act.wait_ge(s_rotf, ROT_ALL)
            act.wait_ge(s_vcur, QUADS)

            def stage_y(ns, n):
                ge(act, s_yT, n - 1)
                act.activation(ycur[:, ns % 2], tiles4(y_sb, n), ACT.Copy).then_inc(s_ycur, 1)

            def shared(ns, n):
                if ns % 2 == 0 and 0 <= ns - 6 < B:
                    act.wait_ge(s_rt, ROUTE_STEPS // 2 * (n - 6) + PICK_STEPS)
                    act.activation(top[:, 3, :], top[:, 2, :], ACT.Exp, scale=1.0 / TAU).then_inc(s_exw, 2)
                if 0 <= ns - 7 < B:
                    par, b = (ns - 7) % 2, n - 7
                    act.wait_ge(s_rt, routed_before(ns - 7, b))
                    if ns - 9 >= 0:
                        act.wait_ge(s_scat[par], 8 * R * (b - par))
                    for k in range(2):
                        tags4 = tags[:, k, 4 * b:4 * b + 4] if isinstance(b, int) else tags[:, k, bass.ds(4 * b, 4)]
                        for at, t4 in ((PLACE, tags4), (WEIGHT, pair_w[:, k, 4 * par:4 * par + 4])):
                            last = act.activation(rows_cur[k][:, par, :, at], t4.rearrange("p (t o) -> p t o", o=1), ACT.Copy)
                    last.then_inc(s_tagged, 1)
                if 0 <= ns < B:
                    par = ns % 2
                    act.wait_ge(s_yT, n + 1)
                    ge(act, s_proj, n - 1)
                    act.activation(yT[:, par, :], ps[:, 0, :], ACT.Copy).then_inc(s_yTsb, 1)
                if 0 <= ns - 3 < B:
                    par = (ns - 3) % 2
                    act.wait_ge(s_xT2, n - 2)
                    ge(act, s_lg, n - 4)
                    act.activation(xT2[:, par, :], ps[:, 3, :], ACT.Copy)
                    act.activation(tiles4(kept_xT, n - 3), ps[:, 3, :].rearrange("p (t c) -> p t c", c=C), ACT.Copy).then_inc(s_xT2sb, 1)
                if 0 <= ns - 8 < B:
                    act.wait_ge(s_y2, n - 7)
                    act.activation(tiles4(ysum, n - 8), ps[:, 6, :].rearrange("p (t c) -> p t c", c=C), ACT.Copy).then_inc(s_ysum, 1)
                for j in range(2):
                    if j == 1 and ns + 1 < B:
                        stage_y(ns + 1, n + 1)
                    if 0 <= ns - 7 < B:
                        act.wait_ge(s_hg, 2 * n + j - 13)
                        ge(act, s_hid, 2 * n + j - 15)
                        act.activation(gel[:, j, :], ps[:, 4, :], ACT.Gelu, bias=b_s1[:, 2 + j:3 + j]).then_inc(s_gel, 1)
                if 0 <= ns - 2 < B:
                    par, b = (ns - 2) % 2, n - 2
                    act.wait_ge(s_shift2, n - 1)
                    ge(act, s_xT2, n - 3)
                    if ns - 4 >= 0:
                        act.wait_ge(s_store[par], 8 * (b - par))
                    x4 = tiles4(x_sb, b)
                    for t in range(NT):
                        last = act.activation(xn2[:, par, t, :], x4[:, t, :], ACT.Identity,
                                              scale=rstd2[:, ns % 2, NT + t:NT + t + 1], bias=shift2[:, ns % 2, t:t + 1])
                    last.then_inc(s_xn2, 1)

            stage_y(0, 0)
            skewed(act, shared)

            def copy_xsT(ns, n):
                act.wait_ge(s_xsT, n + 1)
                ge(act, s_he, 2 * n - 2)
                act.activation(xsT[:, ns % 2, :], ps[:, ns % 2, 0:C], ACT.Copy).then_inc(s_xsTsb, 1)

            def expert_tile(ns, n):
                if ns < ROUTED:
                    act.wait_ge(s_he, 2 * n + 1)
                    ge(act, s_hide, n - 1)
                    act.activation(gelE[:, ns % 2, :], ps[:, 2 + ns % 2, 0:HR], ACT.Gelu).then_inc(s_ge, 1)
                if ns + 1 < ROUTED:
                    copy_xsT(ns + 1, n + 1)
                if 0 <= ns - 1 < ROUTED:
                    par = (ns - 1) % 2
                    act.wait_ge(s_hT, n)
                    ge(act, s_ye, n - 2)
                    act.activation(hidT[:, par, :], ps[:, 6 + par, 0:HR], ACT.Copy).then_inc(s_hTsb, 1)

            copy_xsT(0, 0)
            expert_steps(act, expert_tile)

            for n in range(PAIRS):
                par = n % 2
                act.wait_ge(s_shift, 2 * n + 2)
                if n >= 2:
                    act.wait_ge(s_out[par], 16 * (n // 2))
                for t in range(R):
                    last = act.activation(final[:, par, t, :], summed[:, n % 3, t, :], ACT.Identity,
                                          scale=rstd3[:, n % 3, t:t + 1], bias=shift[:, n % 3, t:t + 1])
                last.then_inc(s_normal, 1)

        @block.tensor
        def _(pe):
            pe.wait_ge(s_ident, 1)
            pe.wait_ge(s_w, 6 * 16)
            for n in range(3):
                last = pe.transpose(ps[0:LAT, 0, n * P:(n + 1) * P], lat_in[:, n, :], ident[:])
            last.then_inc(s_latT, 1)
            pe.wait_ge(s_latT_sb, 1)
            for n in range(3):
                last = pe.matmul(ps[:, 1, n * C:(n + 1) * C], latT[:, n, :], heads_in[:, n, :], start=True, stop=True)
            last.then_inc(s_wmul, 1)
            pe.wait_ge(s_wsb, 1)

            def project(ns, n):
                if 0 <= ns - 1 < B:
                    par = (ns - 1) % 2
                    pe.wait_ge(s_xn, n)
                    ge(pe, s_xT_sb, n - 2)
                    for t in range(NT):
                        last = pe.transpose(ps[:, par, t * P:(t + 1) * P], xn[:, par, t, :], ident[:])
                    last.then_inc(s_xT, 1)
                if 0 <= ns - 2 < B:
                    par = ns % 2
                    pe.wait_ge(s_xT_sb, n - 1)
                    ge(pe, s_r, 2 * n - 6)
                    for s in range(2):
                        pe.matmul(ps[:, 2 + 2 * s + par, :], w_qkv[:, s, :], xnT[:, par, :], start=True, stop=True).then_inc(s_qkp, 1)
                    ge(pe, s_vsb, n - 3)
                    for t in range(NT):
                        last = pe.matmul(ps[:, 6 + par, t * C:(t + 1) * C], xnT[:, par, t * P:(t + 1) * P], w_qkv[:, 2, :],
                                         start=True, stop=True)
                    last.then_inc(s_vp, 1)

            project_steps(pe, project)
            pe.wait_ge(s_const, 1)
            pe.wait_ge(s_r, 2 * B)
            pe.wait_ge(s_vsb, B)

            def rows(i, part_of_q, lo, hi, slot, k):
                base = 64 * (i // 2)
                return qk[base:base + k, slot, part_of_q, i % 2, lo:hi]

            def rot(gs, g, pos, kind, n):
                index = rot_base(gs, g) + pos
                bank = ROT_BANKS[(rot_base(gs, gs) + pos) % len(ROT_BANKS)]
                ge(pe, s_rotf, index - len(ROT_BANKS) + 1)
                if kind == "scores":
                    slot = (gs + 2) % 4
                    if n == 0:
                        pe.wait_ge(s_qk[slot], 32 * (g + 2 - slot) + 128)
                    pr, j = divmod(n, 5)
                    if j < 4:
                        i = 2 * pr + j // 2
                        places = [(i, 3, 0)] if j % 2 == 0 else [(i, 2, 0), (i, 0, 384)]
                    else:
                        places = [(2 * pr, 1, 0), (2 * pr + 1, 1, 256)]
                    for i, qt, at in places:
                        w = (qt + 1) * P
                        pe.matmul(ps[:, bank, at:at + w], rows(i, 0, qt * P, qt * P + P, slot, ROWS - 3),
                                  rows(i, 1, 0, w, slot, ROWS - 3), start=True, stop=False)
                        last = pe.matmul(ps[:, bank, at + w - P:at + w], ident_bf[:], mask_q[:], start=False, stop=True)
                elif kind == "max_rows":
                    wait_apart(pe, s_msplit, 4 * (g + 2), s_passed)
                    last = pe.transpose(ps[0:48, bank, 0:64].bitcast(BF16), m_part[:, (gs + 1) % 2].rearrange("p n x -> p (n x)"),
                                        ident_bf[:])
                else:
                    pe.wait_ge(s_outT, g - 1)
                    for qt in range(NT):
                        last = pe.transpose(ps[:, bank, qt * P:(qt + 1) * P], outT[:, gs % 2, qt * P:(qt + 1) * P], ident[:])
                last.then_inc(s_rot, 1)

            def scores_by_key(gs, g, n, half):
                u = 2 + 2 * ((5 * gs + n) % 2) + half
                slot = gs % 4
                if half == 0:
                    ge(pe, s_exp, 5 * g + n - 1)
                    if n == 0:
                        pe.wait_ge(s_m[slot], 8 * (g - slot) + 32)
                if n < 4:
                    places = [(n, 0, 0)] if half == 0 else [(n, 1, 0), (n, 3, 384)]
                else:
                    places = [(2 * half, 2, 0), (2 * half + 1, 2, 256)]
                for i, kb, at in places:
                    w = T - kb * P
                    last = pe.matmul(ps[:, u, at:at + w], rows(i, 1, kb * P, kb * P + P, slot, ROWS),
                                     rows(i, 0, kb * P, T, slot, ROWS), start=True, stop=True)
                if half == 1:
                    last.then_inc(s_st, 1)

            def products(gs, g, kb):
                buf, slot = (gs - 1) % 2, (gs - 1) % 4
                if kb == 0:
                    pe.wait_ge(s_masked, 5 * g - 1)
                    pe.wait_ge(s_vcur, g)
                    ge(pe, s_outT, g - 1)
                if kb == 2:
                    pe.wait_ge(s_masked, 5 * g)
                w = T - kb * P
                for i in range(4):
                    at = i * 1024 + (0, 512, 0, 896)[kb] if kb != 2 else 4 * 1024 + i * 256
                    flat = pT[:, buf].rearrange("p n t -> p (n t)")
                    last = pe.matmul(ps[32 * i:32 * i + 32, PV_BANK, kb * P:T], v_cur[:, slot, kb, i, :], flat[:, at:at + w],
                                     start=(kb == 0), stop=(kb == 3))
                if kb == 3:
                    last.then_inc(s_pv, 1)

            def step(gs, g):
                items = rot_items(gs)
                todo = list(enumerate(items))

                def some(k):
                    for _ in range(k):
                        if todo:
                            pos, (kind, n) = todo.pop(0)
                            rot(gs, g, pos, kind, n)

                for n in range(5):
                    if 0 <= gs < QUADS:
                        scores_by_key(gs, g, n, 0)
                    some(1)
                    if 0 <= gs < QUADS:
                        scores_by_key(gs, g, n, 1)
                    some(1)
                    if n < 4 and 0 <= gs - 1 < QUADS:
                        products(gs, g, n)
                    if n in (1, 3):
                        some(1)
                some(12)

            quad_steps(pe, step)

            pe.wait_ge(s_w2, 176)
            pe.wait_ge(s_rotf, ROT_ALL)
            pe.wait_ge(s_outT, QUADS)

            def bias(bank, n):
                row = bias_rows[:, n].rearrange("k (o c) -> k o c", o=1).broadcast_to([3, NT, C])
                pe.matmul(ps[:, bank, :], ones_bf[:], row, start=True, stop=False)

            def shared(ns, n):
                if 0 <= ns < B:
                    pe.wait_ge(s_ycur, n + 1)
                    ge(pe, s_yTsb, n)
                    for t in range(NT):
                        last = pe.transpose(ps[:, 0, t * P:(t + 1) * P], ycur[:, ns % 2, t, :], ident[:])
                    last.then_inc(s_yT, 1)
                if 0 <= ns - 3 < B:
                    par = (ns - 3) % 2
                    pe.wait_ge(s_xn2, n - 2)
                    ge(pe, s_xT2sb, n - 3)
                    for t in range(NT):
                        last = pe.transpose(ps[:, 3, t * P:(t + 1) * P], xn2[:, par, t, :], ident[:])
                    last.then_inc(s_xT2, 1)
                if 0 <= ns - 8 < B:
                    par = ns % 2
                    pe.wait_ge(s_hid, 2 * n - 14)
                    ge(pe, s_ysum, n - 8)
                    bias(6, 1)
                    for t in range(NT):
                        for j in range(2):
                            last = pe.matmul(ps[:, 6, t * C:(t + 1) * C], hid[:, par, j, t * P:(t + 1) * P], ws2[:, j, :],
                                             start=False, stop=(t == NT - 1 and j == 1))
                    last.then_inc(s_y2, 1)
                if 0 <= ns - 3 < B:
                    par = (ns - 3) % 2
                    pe.wait_ge(s_xT2sb, n - 2)
                    ge(pe, s_lgsb, n - 3)
                    if ns % 2 == 0 and ns - 6 >= 0:
                        pe.wait_ge(s_rt, ROUTE_STEPS // 2 * (n - 6) + PICK_STEPS + 1)
                    for t in range(NT):
                        last = pe.matmul(ps[:, 7, t * E:(t + 1) * E], xT2[:, par, t * P:(t + 1) * P], w_r[:],
                                         start=True, stop=True)
                    last.then_inc(s_lg, 1)
                for j in range(2):
                    if 0 <= ns - 7 < B:
                        xT = tiles4(kept_xT, n - 7).rearrange("p t c -> p (t c)")
                        ge(pe, s_gel, 2 * n + j - 14)
                        pe.matmul(ps[:, 4, :], ws1[:, HS + j * P:HS + (j + 1) * P], xT, start=True, stop=True).then_inc(s_hg, 1)
                        ge(pe, s_hid, 2 * n + j - 14)
                        pe.matmul(ps[:, 5, :], ws1[:, j * P:(j + 1) * P], xT, start=True, stop=True).then_inc(s_ha, 1)
                    if j == 0 and 0 <= ns < B:
                        par = ns % 2
                        pe.wait_ge(s_yTsb, n + 1)
                        ge(pe, s_z, n - 1)
                        bias(1 + par, 0)
                        for t in range(NT):
                            last = pe.matmul(ps[:, 1 + par, t * C:(t + 1) * C], yT[:, par, t * P:(t + 1) * P], w_proj[:],
                                             start=False, stop=(t == NT - 1))
                        last.then_inc(s_proj, 1)
                if ns % 2 == 1 and 0 <= ns - 5 < B:
                    pe.wait_ge(s_lgsb, n - 2 if ns - 3 < B else B)
                    pe.wait_ge(s_rt, ROUTE_STEPS // 2 * (n - 5) + BOTH_STEP)
                    to = ps[:, 7, NT * E:NT * E + R * E]
                    pe.matmul(to, before_bf[:], both, start=True, stop=False)
                    for d in range(1, R):
                        pe.matmul(to[:, d * E:], all_bf[:], both[:, 0:(R - d) * E], start=False, stop=False)
                    earlier = counted.rearrange("p (o e) -> p o e", o=1).broadcast_to([P, R, E])
                    pe.matmul(to, all_bf[:], earlier, start=False, stop=True).then_inc(s_pref, 2)
                if ns == TABLE_AT:
                    tile_table()

            def tile_table():
                pe.wait_ge(s_rt, ROUTE_STEPS * B // 2)
                pe.matmul(ps[0:E, 7, 0:1], counted, all_bf[:, 0:1], start=True, stop=True)
                pe.matmul(ps[:, 7, 16:16 + E], all_bf[:], counted, start=True, stop=True).then_inc(s_tsum, 1)
                pe.wait_ge(s_table, 4)
                pe.matmul(ps[0:E, 3, 0:1], before[0:E, 0:E], small[0:E, 3:4], start=True, stop=False)
                pe.matmul(ps[0:E, 3, 0:1], ident[0:E, 0:E], small[0:E, 3:4], start=False, stop=True).then_inc(s_tsum, 1)
                pe.wait_ge(s_table, 9)
                pe.matmul(ps[0:1, 1, 0:ROUTED], ones[0:E, 0:1], ends[0:E], start=True, stop=True)
                pe.matmul(ps[0:1, 1, ROUTED:2 * ROUTED], small[0:E, 4:5], ends[0:E], start=True, stop=True).then_inc(s_tsum, 1)

            skewed(pe, shared)

            pe.wait_ge(s_ysum, B)
            pe.wait_ge(s_table, TABLE_STEPS)
            pe.wait_ge(s_we, 16 * 2 * E)
            pe.wait_ge(s_ber, 32)

            def turn_rows(ns, j):
                pe.wait_ge(s_xs[ns % 4], 16 * (j // 4 + 1) if isinstance(j, int) else 4 * (j - ns % 4) + 16)
                ge(pe, s_yesb, j - 3)
                pe.transpose(ps[:, ns % 2, 0:C], xs[:, ns % 4, VALUES], ident[:]).then_inc(s_xsT, 1)

            experts = {}

            def expert(ns, n, at):
                if ns + at not in experts:
                    experts[ns + at] = pe.value_load(etile[0:1, bass.ds(n + at, 1)], min_val=0, max_val=E - 1)
                return experts[ns + at]

            def expert_tile(ns, n):
                if ns == 8:
                    experts.clear()
                if ns < ROUTED:
                    par = ns % 2
                    e = expert(ns, n, 0)
                    pe.wait_ge(s_xsTsb, n + 1)
                    for k, bank in ((1, 2 + par), (0, 4 + par)):
                        ge(pe, s_ge if k else s_hide, n - 1)
                        pe.matmul(ps[:, bank, 0:HR], ones_bf[:], be1r[:, bass.ds(e * (2 * HR) + k * HR, HR)], start=True, stop=False)
                        pe.matmul(ps[:, bank, 0:HR], xsT[:, par, :], we1[:, bass.ds(e * (2 * HR) + k * HR, HR)],
                                  start=False, stop=True).then_inc(s_he, 1)
                    if ns + 1 < ROUTED and ns != 15:
                        expert(ns, n, 1)
                if ns + 1 < ROUTED:
                    turn_rows(ns + 1, n + 1)
                if 0 <= ns - 1 < ROUTED:
                    par = (ns - 1) % 2
                    pe.wait_ge(s_hide, n)
                    ge(pe, s_hTsb, n - 2)
                    for k in range(3):
                        last = pe.transpose(ps[:, 6 + par, k * P:(k + 1) * P], hidE[:, par, k * P:(k + 1) * P], ident[:])
                    last.then_inc(s_hT, 1)
                if 0 <= ns - 2 < ROUTED:
                    par = ns % 2
                    e = expert(ns, n, -2)
                    pe.wait_ge(s_hTsb, n - 1)
                    if ns >= ROUTED:
                        pe.wait_ge(s_yesb, n - 3)
                    pe.matmul(ps[:, par, 0:C], ones_bf[:], be2r[:, bass.ds(e * C, C)], start=True, stop=False)
                    for k in range(3):
                        last = pe.matmul(ps[:, par, 0:C], hidT[:, par, k * P:(k + 1) * P], we2[:, bass.ds(e * HR + k * P, P)],
                                         start=False, stop=(k == 2))
                    last.then_inc(s_ye, 1)

            turn_rows(0, 0)
            expert_steps(pe, expert_tile)

        @block.vector
        def _(dve):
            def statistics(par, b):
                x4 = tiles4(x_sb, b)
                for t in range(NT):
                    last = dve.bn_stats(st[:, par, t, :], x4[:, t, :])
                last.then_inc(s_stats, 1)

            def moments(par, b):
                wait_apart(dve, s_stats, b + 1, s_passed)
                for t in range(NT):
                    last = dve.bn_aggr(mv[:, par, t, :], st[:, par, t, :])
                last.then_inc(s_aggr, 1)

            def keep_moments(par, b):
                dve.wait_ge(s_aggr, 2 * b + 1)
                dve.tensor_copy(tiles4(mv1, b), mv[:, par]).then_inc(s_aggr, 1)

            def roots_of_pair(b):
                tiles = slice(NT * b, NT * (b + 2)) if isinstance(b, int) else bass.ds(NT * b, 2 * NT)
                y = rstd1[:, tiles]
                v, half, t = (root1[:, k, :] for k in range(3))
                done = ROOT_OPS // 2 * b
                dve.wait_ge(s_aggr, 2 * b + 4)
                dve.tensor_scalar(v, mv1[:, tiles, 1], EPS, None, ALU.add).then_inc(s_root1, 1)
                dve.wait_ge(s_root1, done + 1)
                dve.tensor_scalar(half.bitcast(I32), v.bitcast(I32), 1, None, ALU.arith_shift_right).then_inc(s_root1, 1)
                dve.wait_ge(s_root1, done + 2)
                dve.tensor_scalar(y.bitcast(I32), half.bitcast(I32), -1.0, float(0x5F3759DF), ALU.mult, ALU.add).then_inc(s_root1, 1)
                for k in range(NEWTON):
                    dve.wait_ge(s_root1, done + 3 * k + 3)
                    dve.tensor_tensor(t, y, y, ALU.mult).then_inc(s_root1, 1)
                    dve.wait_ge(s_root1, done + 3 * k + 4)
                    dve.scalar_tensor_tensor(out=t, in0=t, scalar=-0.5, in1=v, op0=ALU.mult, op1=ALU.mult).then_inc(s_root1, 1)
                    dve.wait_ge(s_root1, done + 3 * k + 5)
                    dve.scalar_tensor_tensor(out=y, in0=t, scalar=1.5, in1=y, op0=ALU.add, op1=ALU.mult).then_inc(s_root1, 1)

            def rests(ns, n):
                if ns < B:
                    par = ns % 2
                    wait_apart(dve, s_root1, ROOT_OPS // 2 * (n - par) + ROOT_OPS, s_passed)
                    ge(dve, s_xT, n - 1)
                    x4 = tiles4(x_sb, n)
                    for t in range(NT):
                        last = dve.tensor_scalar(xn[:, par, t, :], x4[:, t, :], one(mv1, NT * n + t)[:, :, 0],
                                                 one(rstd1, NT * n + t), ALU.subtract, ALU.mult)
                    last.then_inc(s_xn, 1)
                if ns + 2 < B:
                    if isinstance(n, int):
                        for k, (first, _) in enumerate(X_LOADS):
                            if first == n + 2 or (n == 7 and first > n + 2):
                                dve.wait_ge(s_x[k], 16)
                    statistics(ns % 2, n + 2)
                for k in range(2):
                    if 0 <= ns - 3 < B:
                        par = (ns - 3) % 2
                        dve.wait_ge(s_p1, 2 * n + k - 5)
                        ge(dve, s_p3, 2 * n + k - 9)
                        dve.tensor_tensor(rest[:, par, k, :], ps[:, 2 + 2 * k + par, :], part[:, par, k, 0, :],
                                          ALU.subtract).then_inc(s_r, 1)
                    if ns + 2 < B:
                        (moments, keep_moments)[k](ns % 2, n + 2)
                if ns % 2 == 1 and ns + 2 < B:
                    roots_of_pair(n + 1)

            dve.wait_ge(s_x[0], 16)
            for b in range(2):
                statistics(b, b)
                moments(b, b)
                keep_moments(b, b)
            roots_of_pair(0)
            project_steps(dve, rests)
            dve.wait_ge(s_w2, 160)
            dve.tensor_copy(be_part[:, 0, :], be_in[:]).then_inc(s_be, 1)
            dve.wait_ge(s_be, 1)
            dve.tensor_tensor(be_rest[:], be_in[:], be_part[:, 0, :], ALU.subtract).then_inc(s_be, 1)
            dve.wait_ge(s_be, 2)
            dve.tensor_copy(be_part[:, 1, :], be_rest[:]).then_inc(s_be, 1)
            dve.wait_ge(s_be, 3)
            dve.tensor_tensor(be_part[:, 2, :], be_rest[:], be_part[:, 1, :], ALU.subtract).then_inc(s_be, 1)

            def take(gs, g, pos, kind, n):
                index = rot_base(gs, g) + pos
                bank = ROT_BANKS[(rot_base(gs, gs) + pos) % len(ROT_BANKS)]
                dve.wait_ge(s_rot, index + 1)
                if kind == "scores":
                    buf = (gs + 2) % 2
                    pr, j = divmod(n, 5)
                    if n == 0:
                        ge(dve, s_msplit, 4 * (g + 1))
                    if j < 4:
                        i = 2 * pr + j // 2
                        places = [(i, 3, 0)] if j % 2 == 0 else [(i, 2, 0), (i, 0, 384)]
                        for i, qt, at in places:
                            last = dve.tensor_reduce(m_q[:, buf, 4 * i + qt:4 * i + qt + 1],
                                                     ps[:, bank, at:at + (qt + 1) * P], AX, ALU.max)
                    else:
                        cols = m_q[:, buf, 8 * pr:8 * pr + 8].rearrange("p (i q) -> p i q", q=4)[:, :, 1]
                        last = dve.tensor_reduce(cols, ps[:, bank, :].rearrange("p (i k) -> p i k", i=2), AX, ALU.max)
                    last.then_inc(s_rotf, 1)
                    if n == 9:
                        done = 4 * (g + 2)
                        dve.wait_ge(s_rotf, index + 1)
                        dve.tensor_scalar(m_part[:, buf, 0, :], m_q[:, buf, :], -1.0, None, ALU.mult).then_inc(s_msplit, 1)
                        dve.wait_ge(s_msplit, done + 1)
                        dve.scalar_tensor_tensor(out=m_rest[:, buf, :], in0=m_q[:, buf, :], scalar=-1.0,
                                                 in1=m_part[:, buf, 0, :], op0=ALU.mult, op1=ALU.subtract).then_inc(s_msplit, 1)
                        dve.wait_ge(s_msplit, done + 2)
                        dve.tensor_copy(m_part[:, buf, 1, :], m_rest[:, buf, :]).then_inc(s_msplit, 1)
                        dve.wait_ge(s_msplit, done + 3)
                        dve.tensor_tensor(m_part[:, buf, 2, :], m_rest[:, buf, :], m_part[:, buf, 1, :],
                                          ALU.subtract).then_inc(s_msplit, 1)
                elif kind == "max_rows":
                    ge(dve, s_mw, 16 * g)
                    dve.tensor_copy(mT_sb[:, (gs + 1) % 2, :], ps[0:48, bank, 0:64].bitcast(BF16)).then_inc(s_rotf, 1)
                else:
                    o = ps[:, bank, :].rearrange("p (t i r) -> p t i r", t=NT, i=4)
                    dve.reciprocal(rden[:, gs % 2], o[:, :, :, HD]).then_inc(s_rden, 1)
                    dve.wait_ge(s_rden, g - 1)
                    q = (gs - 2) % 4
                    y4 = (y_sb[:, g - 2 - q:g + 2 - q] if isinstance(g, int) else y_sb[:, bass.ds(g - 2 - q, 4)])
                    dve.tensor_tensor(y4[:, :, 32 * q:32 * q + 32].rearrange("p t (i d) -> p t i d", d=HD),
                                      o[:, :, :, 0:HD], rden[:, gs % 2].rearrange("p t (i o) -> p t i o", o=1).broadcast_to([P, NT, 4, HD]),
                                      ALU.mult).then_inc(s_rotf, 1)

            def step(gs, g):
                for pos, (kind, n) in enumerate(rot_items(gs)):
                    take(gs, g, pos, kind, n)

            quad_steps(dve, step)

            numbers = iota_f[:, ROUTED:].rearrange("p (o e) -> p o e", o=1).broadcast_to([P, R, E])

            def wide(t):
                return t.rearrange("p (t o) -> p t o", o=1).broadcast_to([P, R, E])

            def pick_step(ns, n, i):
                done = ROUTE_STEPS // 2 * (n - 5) + i
                ge(dve, s_rt, done)
                k, source = (0, logit) if i < 5 else (1, masked)
                if i == 0:
                    dve.wait_ge(s_lgsb, n - 3)
                if i in (0, 6):
                    ins = dve.tensor_reduce(top[:, k, :], source, AX, ALU.max)
                elif i in (1, 7):
                    ins = dve.tensor_tensor(lowest, source, wide(top[:, k, :]), ALU.is_equal)
                elif i in (2, 8):
                    ins = dve.tensor_tensor(lowest, lowest, numbers, ALU.mult)
                elif i in (3, 9):
                    ins = dve.tensor_reduce(top[:, 2, :], lowest, AX, ALU.min)
                elif i in (4, 10):
                    ins = dve.tensor_tensor(onehot[:, k], numbers, wide(top[:, 2, :]), ALU.is_equal)
                elif i == 5:
                    ins = dve.scalar_tensor_tensor(out=masked, in0=onehot[:, 0], scalar=-HUGE, in1=logit, op0=ALU.mult, op1=ALU.add)
                elif i == 11:
                    ins = dve.tensor_tensor(by_expert(both), onehot[:, 0], onehot[:, 1], ALU.add)
                else:
                    ins = dve.tensor_tensor(top[:, 2, :], top[:, 1, :], top[:, 0, :], ALU.subtract)
                ins.then_inc(s_rt, 1)

            def place_step(ns, n, i):
                done = ROUTE_STEPS // 2 * (n - 6) + PICK_STEPS + i
                dve.wait_ge(s_rt, done)
                if i == 0:
                    dve.wait_ge(s_pref, n - 4)
                    base = rooms[:].rearrange("p (o e) -> p o e", o=1).broadcast_to([P, R, E])
                    ins = dve.tensor_tensor(place, by_expert(ps[:, 7, NT * E:NT * E + R * E]), base, ALU.add)
                elif i in (1, 2):
                    ins = dve.tensor_tensor(chosen[:, i - 1], onehot[:, i - 1], place, ALU.mult)
                elif i == 3:
                    if ns - 7 >= 0:
                        dve.wait_ge(s_idx, n - 6)
                    ins = dve.tensor_reduce(slot_f, chosen, AX, ALU.add)
                elif i == 4:
                    ins = dve.tensor_reduce(newly, both.rearrange("p (t e) -> p e t", e=E), AX, ALU.add)
                elif i == 5:
                    ins = dve.tensor_tensor(counted, counted, newly, ALU.add)
                elif i == 6:
                    dve.wait_ge(s_exw, n - 4)
                    ins = dve.tensor_scalar(top[:, 2, :], top[:, 3, :], 1.0, None, ALU.add)
                elif i == 7:
                    if ns - 7 >= 0:
                        dve.wait_ge(s_tagged, n - 6)
                    ins = dve.reciprocal(pair_w[:, 0, :], top[:, 2, :])
                else:
                    ins = dve.tensor_tensor(pair_w[:, 1, :], top[:, 3, :], pair_w[:, 0, :], ALU.mult)
                ins.then_inc(s_rt, 1)

            def root_step(n, par, cols, i):
                y, (v, half, t) = rstd2[:, par, cols], (root2[:, k, cols] for k in range(3))
                dve.wait_ge(s_root, ROOT_STEPS * (n - 1) + 1 + i)
                if i == 0:
                    ins = dve.tensor_scalar(v, mv2[:, par, cols, 1], EPS, None, ALU.add)
                elif i == 1:
                    ins = dve.tensor_scalar(half.bitcast(I32), v.bitcast(I32), 1, None, ALU.arith_shift_right)
                elif i == 2:
                    ge(dve, s_xn2, n - 3)
                    ins = dve.tensor_scalar(y.bitcast(I32), half.bitcast(I32), -1.0, float(0x5F3759DF), ALU.mult, ALU.add)
                elif i % 3 == 0:
                    ins = dve.tensor_tensor(t, y, y, ALU.mult)
                elif i % 3 == 1:
                    ins = dve.scalar_tensor_tensor(out=t, in0=t, scalar=-0.5, in1=v, op0=ALU.mult, op1=ALU.mult)
                else:
                    ins = dve.scalar_tensor_tensor(out=y, in0=t, scalar=1.5, in1=y, op0=ALU.add, op1=ALU.mult)
                ins.then_inc(s_root, 1)

            def hidden(ns, n, j):
                par = (ns - 7) % 2
                dve.wait_ge(s_gel, 2 * n + j - 13)
                dve.wait_ge(s_ha, 2 * n + j - 13)
                ge(dve, s_y2, n - 8)
                dve.scalar_tensor_tensor(out=hid[:, par, j, :], in0=ps[:, 5, :], scalar=b_s1[:, j:j + 1],
                                         in1=gel[:, j, :], op0=ALU.add, op1=ALU.mult).then_inc(s_hid, 1)

            table_done = 0

            def tile_table():
                def then(ins):
                    nonlocal table_done
                    table_done += 1
                    ins.then_inc(s_table, 1)
                    dve.wait_ge(s_table, table_done)

                count, small_i, tiles_, room_left, end = (small[0:E, k:k + 1] for k in (1, 2, 3, 4, 5))
                dve.wait_ge(s_tsum, 1)
                then(dve.tensor_scalar(count, ps[0:E, 7, 0:1], float(P - 1), None, ALU.add))
                then(dve.tensor_copy(small_i.bitcast(I32), count))
                then(dve.tensor_scalar(small_i.bitcast(I32), small_i.bitcast(I32), 7, None, ALU.arith_shift_right))
                then(dve.tensor_copy(tiles_, small_i.bitcast(I32)))
                then(dve.tensor_scalar(room_left, tiles_, -float(P), float(ROOM), ALU.mult, ALU.add))
                then(dve.tensor_tensor(pad_rows, ps[:, 7, 16:16 + E], rooms[:], ALU.add))
                then(dve.tensor_copy(pad_row, pad_rows[0:1]))
                dve.wait_ge(s_tsum, 2)
                then(dve.tensor_copy(end, ps[0:E, 3, 0:1]))
                then(dve.tensor_scalar(ends[0:E], iota_f[0:E, 0:ROUTED], end, None, ALU.is_ge))
                dve.wait_ge(s_tsum, 3)
                then(dve.tensor_scalar(tile_row[:, 0], ps[0:1, 1, 0:ROUTED], float(E - 1), None, ALU.min))
                then(dve.tensor_copy(etile, tile_row[:, 0]))
                then(dve.tensor_scalar(tile_row[:, 0], iota_f[0:1, 0:ROUTED], float(P), None, ALU.mult))
                then(dve.tensor_tensor(tile_row[:, 1], tile_row[:, 0], ps[0:1, 1, ROUTED:2 * ROUTED], ALU.add))
                then(dve.tensor_copy(atile, tile_row[:, 1]))
                assert table_done == TABLE_STEPS

            def shared(ns, n):
                par = ns % 2
                first, second, third = (0 <= ns - k < B for k in (1, 2, 3))
                if 0 <= ns - 7 < B:
                    p7, b = (ns - 7) % 2, n - 7
                    if ns - 9 >= 0:
                        dve.wait_ge(s_scat[p7], 8 * R * (b - p7))
                    dve.wait_ge(s_rt, routed_before(ns - 7, b))
                    dve.tensor_copy(idx_cur[:, p7], slot_f[:, :, 4 * p7:4 * p7 + 4]).then_inc(s_idx, 1)
                cols = slice(0 if first else NT, 2 * NT if second else NT)
                if first or second:
                    if first:
                        dve.wait_ge(s_proj, n)
                        for t in range(NT):
                            last = dve.bn_stats(st2[:, par, t, :], ps[:, 1 + (ns - 1) % 2, t * C:(t + 1) * C])
                    if second:
                        wait_apart(dve, s_z, n - 1, s_passed)
                        x4 = tiles4(x_sb, n - 2)
                        for t in range(NT):
                            last = dve.bn_stats(st2[:, par, NT + t, :], x4[:, t, :])
                    last.then_inc(s_st2, 1)
                    wait_apart(dve, s_st2, n, s_passed)
                    for t in range(cols.start, cols.stop):
                        last = dve.bn_aggr(mv2[:, par, t, :], st2[:, par, t, :])
                    last.then_inc(s_root, 1)
                for i in range(13):
                    if (first or second) and i < ROOT_STEPS - 1:
                        root_step(n, par, cols, i)
                    if ns % 2 == 1 and 0 <= ns - 5 < B:
                        pick_step(ns, n, i)
                    if ns % 2 == 0 and 0 <= ns - 6 < B and i < PLACE_STEPS:
                        place_step(ns, n, i)
                if first or second:
                    dve.wait_ge(s_root, ROOT_STEPS * n)
                if second:
                    dve.scalar_tensor_tensor(out=shift2[:, par], in0=mv2[:, par, NT:, 0], scalar=-1.0, in1=rstd2[:, par, NT:],
                                             op0=ALU.mult, op1=ALU.mult).then_inc(s_shift2, 1)
                if third:
                    dve.wait_ge(s_lg, n - 2)
                    row = b_r[:].rearrange("p (o n) -> p o n", o=1).broadcast_to([P, NT, E])
                    half = (ns - 3) % 2
                    dve.tensor_tensor(logit[:, NT * half:NT * half + NT, :], by_expert(ps[:, 7, 0:NT * E]), row,
                                      ALU.add).then_inc(s_lgsb, 1)
                if 0 <= ns - 7 < B:
                    hidden(ns, n, 0)
                if first:
                    at = moved[:, 4 * n - 4:4 * n] if isinstance(n, int) else moved[:, bass.ds(4 * n - 4, 4)]
                    dve.scalar_tensor_tensor(out=at, in0=mv2[:, par, 0:NT, 0], scalar=-1.0, in1=rstd2[:, par, 0:NT],
                                             op0=ALU.mult, op1=ALU.mult)
                    x4 = tiles4(x_sb, n - 1)
                    for t in range(NT):
                        last = dve.scalar_tensor_tensor(out=x4[:, t, :], in0=ps[:, 1 + (ns - 1) % 2, t * C:(t + 1) * C],
                                                        scalar=rstd2[:, par, t:t + 1], in1=x4[:, t, :], op0=ALU.mult, op1=ALU.add)
                    last.then_inc(s_z, 1)
                if 0 <= ns - 7 < B:
                    hidden(ns, n, 1)
                if ns == TABLE_AT:
                    tile_table()

            dve.wait_ge(s_vcur, QUADS)
            dve.memset(counted, 0.0).then_inc(s_cset, 1)
            dve.wait_ge(s_cset, 1)
            skewed(dve, shared)

            def expert_tile(ns, n):
                if ns < ROUTED:
                    par = ns % 2
                    dve.wait_ge(s_ge, n + 1)
                    dve.wait_ge(s_he, 2 * n + 2)
                    ge(dve, s_hT, n - 1)
                    dve.tensor_tensor(hidE[:, par, :], ps[:, 4 + par, 0:HR], gelE[:, par, :], ALU.mult).then_inc(s_hide, 1)
                if 0 <= ns - 2:
                    par = ns % 2
                    dve.wait_ge(s_ye, n - 1)
                    dve.wait_ge(s_tag, 2 * n - 2)
                    if ns >= 4:
                        dve.wait_ge(s_yst[par], 8 * (n - par) - 16)
                    dve.tensor_scalar(ys[:, par, :], ps[:, par, 0:C], weight_cur[:, (ns - 2) % 4:(ns - 2) % 4 + 1], None,
                                      ALU.mult).then_inc(s_yesb, 1)

            expert_steps(dve, expert_tile)

            for n in range(PAIRS + 2):
                if n < PAIRS:
                    par, ring = n % 2, n % 3
                    dve.wait_ge(s_sum, n + 1)
                    ge(dve, s_normal, n - 2)
                    dve.tensor_tensor(summed[:, ring], picked[:, par, 0], pair_of(ysum, n), ALU.add).then_inc(s_comb, 1)
                    dve.wait_ge(s_comb, n + 1)
                    for t in range(R):
                        last = dve.bn_stats(st2[:, par, t, :], summed[:, ring, t, :])
                    last.then_inc(s_st3, 1)
                    dve.wait_ge(s_st3, n + 1)
                    for t in range(R):
                        last = dve.bn_aggr(mv3[:, ring, t, :], st2[:, par, t, :])
                    last.then_inc(s_seedC, 1)
                    seed(dve, s_seedC, SEED_OPS * n + 1, rstd3[:, ring], root3[:, ring, 0], root3[:, ring, 1], mv3[:, ring, :, 1])
                if n >= 2:
                    dve.wait_ge(s_normal, n - 1)
                    dve.tensor_tensor(final[:, n % 2], final[:, n % 2], pair_of(x_sb, n - 2), ALU.add).then_inc(s_fin, 1)
                if 1 <= n <= PAIRS:
                    ring = (n - 1) % 3
                    dve.wait_ge(s_newtC, NEWTON_OPS * n)
                    dve.scalar_tensor_tensor(out=shift[:, ring], in0=mv3[:, ring, :, 0], scalar=-1.0, in1=rstd3[:, ring], op0=ALU.mult,
                                             op1=ALU.mult).then_inc(s_shift, 1)
                    dve.wait_ge(s_shift, 2 * n - 1)
                    dve.tensor_tensor(shift[:, ring], shift[:, ring], pair_of(moved, n - 1), ALU.add).then_inc(s_shift, 1)


_OUTS = [((16, 512, 128), "float32")]


def kernel(**inputs):
    import numpy as _np
    import concourse.bacc as _bacc
    from concourse import mybir as _mybir
    from concourse.bass_utils import run_bass_kernel_spmd as _run

    nc = _bacc.Bacc("TRN2", target_bir_lowering=False, num_devices=1)
    arrays, aps = {}, {}
    for name, value in inputs.items():
        v = _np.ascontiguousarray(value)
        arrays[f"in_{name}"] = v
        aps[name] = nc.dram_tensor(f"in_{name}", v.shape, _mybir.dt.from_np(v.dtype), kind="ExternalInput").ap()
    shape, dtype = _OUTS[0]
    out = nc.dram_tensor("out_0_dram", shape, _mybir.dt.from_np(_np.dtype(dtype)), kind="ExternalOutput").ap()
    build(nc, aps, out)
    r = _run(nc, [arrays], core_ids=[0])
    return r.results[0]["out_0_dram"]
```
